# Optimizing a Trainium2 kernel written in Bass

```python
import numpy as np
import jax
import jax.numpy as jnp

def _softmax(x, axis=-1):
    return jax.nn.softmax(x, axis=axis)

def _gelu(x):
    return jax.nn.gelu(x, approximate=True)

def _silu(x):
    return jax.nn.silu(x)

def _sigmoid(x):
    return jax.nn.sigmoid(x)

def _layernorm(x, axis=-1, eps=1e-05):
    m = jnp.mean(x, axis=axis, keepdims=True)
    v = jnp.var(x, axis=axis, keepdims=True)
    return (x - m) / jnp.sqrt(v + eps)

def _scatter_add(tgt, idx, src, axis=0):
    return tgt.at[idx].add(src)

def _segment_sum(src, seg, n):
    return jax.ops.segment_sum(src, seg, n)
kernel_name = 'mk_audio_tower_d1_tok_aud1d768_r4_21a514'

def setup_inputs(seed: int=0):
    np.random.seed(seed)
    _w = jnp.asarray

    def _rec_inputs():
        import jax
        import jax.numpy as jnp
        _rk = jax.random.key(seed)
        x = -0.000869125 + 1.00042 * jax.random.normal(jax.random.fold_in(_rk, 1), (64, 4000), jnp.float32)
        return x
    x = _rec_inputs()

    def _L0_tok_setup():
        import jax, jax.numpy as jnp
        import numpy as np
        CONVS = [(128, 10, 5)] + [(128, 3, 2)] * 4 + [(128, 2, 2)] * 2

        def _fp32_layernorm(x, g, b, eps=1e-05):
            xf = x.astype(jnp.float32)
            mu = xf.mean(-1, keepdims=True)
            var = xf.var(-1, keepdims=True)
            y = (xf - mu) * jax.lax.rsqrt(var + eps) * g.astype(jnp.float32) + b.astype(jnp.float32)
            return y.astype(x.dtype)

        def _conv1d(x, w, stride):
            return jax.lax.conv_general_dilated(x, w, (stride,), 'VALID', dimension_numbers=('NCH', 'OIH', 'NCH'))
        key = jax.random.key(seed)
        keys = jax.random.split(key, 16)
        inp = {'x': jax.random.normal(keys[0], (8, 40000), jnp.float32)}
        in_d = 1
        for i, (dim, k, s) in enumerate(CONVS):
            fan_in = in_d * k
            inp[f'conv_w{i}'] = jax.random.normal(keys[1 + i], (dim, in_d, k), jnp.float32) * np.float32(np.sqrt(2.0 / fan_in))
            inp[f'ln_g{i}'] = jnp.ones((dim,), jnp.float32)
            inp[f'ln_b{i}'] = jnp.zeros((dim,), jnp.float32)
            in_d = dim
        inp['fln_g'] = jnp.ones((128,), jnp.float32)
        inp['fln_b'] = jnp.zeros((128,), jnp.float32)
        inp['proj_w'] = jax.random.normal(keys[9], (128, 192), jnp.float32) * np.float32(0.02)
        inp['proj_b'] = jnp.zeros((192,), jnp.float32)
        return inp
    _L0_tok_all = _L0_tok_setup()
    _L0_tok_in = {k: v for k, v in _L0_tok_all.items() if k in ('conv_w0', 'ln_g0', 'ln_b0', 'conv_w1', 'ln_g1', 'ln_b1', 'conv_w2', 'ln_g2', 'ln_b2', 'conv_w3', 'ln_g3', 'ln_b3', 'conv_w4', 'ln_g4', 'ln_b4', 'conv_w5', 'ln_g5', 'ln_b5', 'conv_w6', 'ln_g6', 'ln_b6', 'fln_g', 'fln_b', 'proj_w', 'proj_b')}
    del _L0_tok_all

    def _L0_attn_setup():
        import jax, jax.numpy as jnp
        import numpy as np
        NUM_HEADS = 12
        NUM_LANDMARKS = 64
        PINV_ITERS = 6

        def moore_penrose_iter_pinv(x, iters=PINV_ITERS):
            abs_x = jnp.abs(x)
            col = abs_x.sum(axis=-1)
            row = abs_x.sum(axis=-2)
            z = jnp.swapaxes(x, -1, -2) / (jnp.max(col) * jnp.max(row))
            I = jnp.eye(x.shape[-1], dtype=x.dtype)
            for _ in range(iters):
                xz = x @ z
                z = 0.25 * z @ (13.0 * I - xz @ (15.0 * I - xz @ (7.0 * I - xz)))
            return z

        def _reference_tuple_inner(x, w_qkv, w_proj, b_proj):
            B, N, C = x.shape
            H = NUM_HEADS
            m = NUM_LANDMARKS
            d = C // H
            scale = d ** (-0.5)
            original_N = N
            rem = N % m
            if rem > 0:
                x = jnp.pad(x, ((0, 0), (m - rem, 0), (0, 0)))
                N = x.shape[1]
            qkv = x @ w_qkv.T
            q, k, v = jnp.split(qkv, 3, axis=-1)
            to_heads = lambda t: t.reshape(B, N, H, d).transpose(0, 2, 1, 3)
            q, k, v = (to_heads(q), to_heads(k), to_heads(v))
            q = q * scale
            l = N // m
            q_landmarks = q.reshape(B, H, m, l, d).mean(axis=3)
            k_landmarks = k.reshape(B, H, m, l, d).mean(axis=3)
            sim1 = jnp.einsum('bhnd,bhmd->bhnm', q, k_landmarks)
            sim2 = jnp.einsum('bhid,bhjd->bhij', q_landmarks, k_landmarks)
            sim3 = jnp.einsum('bhmd,bhnd->bhmn', q_landmarks, k)
            attn1 = jax.nn.softmax(sim1, axis=-1)
            attn2 = jax.nn.softmax(sim2, axis=-1)
            attn3 = jax.nn.softmax(sim3, axis=-1)
            attn2_inv = moore_penrose_iter_pinv(attn2, PINV_ITERS)
            attn = attn1 @ attn2_inv @ attn3
            out = attn1 @ (attn2_inv @ (attn3 @ v))
            out = out.transpose(0, 2, 1, 3).reshape(B, N, C)
            out = out[:, -original_N:]
            out = out @ w_proj.T + b_proj
            return (out, attn)
        key = jax.random.key(seed)
        k1, k2, k3, k4 = jax.random.split(key, 4)
        B, N, C = (2, 512, 192)
        x = jax.random.normal(k1, (B, N, C), dtype=jnp.float32)
        w_qkv = jax.random.normal(k2, (3 * C, C), dtype=jnp.float32) * 0.02
        w_proj = jax.random.normal(k3, (C, C), dtype=jnp.float32) * 0.02
        b_proj = jax.random.normal(k4, (C,), dtype=jnp.float32) * 0.02
        return {'x': x, 'w_qkv': w_qkv, 'w_proj': w_proj, 'b_proj': b_proj}
    _L0_attn_all = _L0_attn_setup()
    _L0_attn_in = {k: v for k, v in _L0_attn_all.items() if k in ('w_qkv', 'w_proj', 'b_proj')}
    del _L0_attn_all

    def _L0_ffn_setup():
        import jax, jax.numpy as jnp
        import numpy as np
        B, S, D = (4, 256, 192)
        E = 8
        H = 192
        HS = 768
        TOPK_ROUTED = 2
        key = jax.random.key(seed)
        ks = jax.random.split(key, 10)
        w = lambda k, shape: jax.random.normal(k, shape, dtype=jnp.float32) * 0.02
        return {'x': jax.random.normal(ks[0], (B, S, D), dtype=jnp.float32), 'router_w': w(ks[1], (D, E)), 'w_gate': w(ks[2], (E, D, H)), 'w_up': w(ks[3], (E, D, H)), 'w_down': w(ks[4], (E, H, D)), 'ws_gate': w(ks[5], (D, HS)), 'ws_up': w(ks[6], (D, HS)), 'ws_down': w(ks[7], (HS, D)), 'sg_w': w(ks[8], (D, 1)), 'sg_b': jnp.zeros((1,), jnp.float32)}
    _L0_ffn_all = _L0_ffn_setup()
    _L0_ffn_in = {k: v for k, v in _L0_ffn_all.items() if k in ('router_w', 'w_gate', 'w_up', 'w_down', 'ws_gate', 'ws_up', 'ws_down', 'sg_w', 'sg_b')}
    del _L0_ffn_all
    return {'x': x, 'L0_tok_conv_w0': _L0_tok_in['conv_w0'], 'L0_tok_ln_g0': _L0_tok_in['ln_g0'], 'L0_tok_ln_b0': _L0_tok_in['ln_b0'], 'L0_tok_conv_w1': _L0_tok_in['conv_w1'], 'L0_tok_ln_g1': _L0_tok_in['ln_g1'], 'L0_tok_ln_b1': _L0_tok_in['ln_b1'], 'L0_tok_conv_w2': _L0_tok_in['conv_w2'], 'L0_tok_ln_g2': _L0_tok_in['ln_g2'], 'L0_tok_ln_b2': _L0_tok_in['ln_b2'], 'L0_tok_conv_w3': _L0_tok_in['conv_w3'], 'L0_tok_ln_g3': _L0_tok_in['ln_g3'], 'L0_tok_ln_b3': _L0_tok_in['ln_b3'], 'L0_tok_conv_w4': _L0_tok_in['conv_w4'], 'L0_tok_ln_g4': _L0_tok_in['ln_g4'], 'L0_tok_ln_b4': _L0_tok_in['ln_b4'], 'L0_tok_conv_w5': _L0_tok_in['conv_w5'], 'L0_tok_ln_g5': _L0_tok_in['ln_g5'], 'L0_tok_ln_b5': _L0_tok_in['ln_b5'], 'L0_tok_conv_w6': _L0_tok_in['conv_w6'], 'L0_tok_ln_g6': _L0_tok_in['ln_g6'], 'L0_tok_ln_b6': _L0_tok_in['ln_b6'], 'L0_tok_fln_g': _L0_tok_in['fln_g'], 'L0_tok_fln_b': _L0_tok_in['fln_b'], 'L0_tok_proj_w': _L0_tok_in['proj_w'], 'L0_tok_proj_b': _L0_tok_in['proj_b'], 'L0_attn_w_qkv': _L0_attn_in['w_qkv'], 'L0_attn_w_proj': _L0_attn_in['w_proj'], 'L0_attn_b_proj': _L0_attn_in['b_proj'], 'L0_ffn_router_w': _L0_ffn_in['router_w'], 'L0_ffn_w_gate': _L0_ffn_in['w_gate'], 'L0_ffn_w_up': _L0_ffn_in['w_up'], 'L0_ffn_w_down': _L0_ffn_in['w_down'], 'L0_ffn_ws_gate': _L0_ffn_in['ws_gate'], 'L0_ffn_ws_up': _L0_ffn_in['ws_up'], 'L0_ffn_ws_down': _L0_ffn_in['ws_down'], 'L0_ffn_sg_w': _L0_ffn_in['sg_w'], 'L0_ffn_sg_b': _L0_ffn_in['sg_b']}

def reference(x, L0_tok_conv_w0, L0_tok_ln_g0, L0_tok_ln_b0, L0_tok_conv_w1, L0_tok_ln_g1, L0_tok_ln_b1, L0_tok_conv_w2, L0_tok_ln_g2, L0_tok_ln_b2, L0_tok_conv_w3, L0_tok_ln_g3, L0_tok_ln_b3, L0_tok_conv_w4, L0_tok_ln_g4, L0_tok_ln_b4, L0_tok_conv_w5, L0_tok_ln_g5, L0_tok_ln_b5, L0_tok_conv_w6, L0_tok_ln_g6, L0_tok_ln_b6, L0_tok_fln_g, L0_tok_fln_b, L0_tok_proj_w, L0_tok_proj_b, L0_attn_w_qkv, L0_attn_w_proj, L0_attn_b_proj, L0_ffn_router_w, L0_ffn_w_gate, L0_ffn_w_up, L0_ffn_w_down, L0_ffn_ws_gate, L0_ffn_ws_up, L0_ffn_ws_down, L0_ffn_sg_w, L0_ffn_sg_b):
    import jax
    import jax.numpy as jnp

    def _L0_tok_ref(x, conv_w0, ln_g0, ln_b0, conv_w1, ln_g1, ln_b1, conv_w2, ln_g2, ln_b2, conv_w3, ln_g3, ln_b3, conv_w4, ln_g4, ln_b4, conv_w5, ln_g5, ln_b5, conv_w6, ln_g6, ln_b6, fln_g, fln_b, proj_w, proj_b):
        import jax, jax.numpy as jnp
        import numpy as np
        CONVS = [(128, 10, 5)] + [(128, 3, 2)] * 4 + [(128, 2, 2)] * 2

        def _fp32_layernorm(x, g, b, eps=1e-05):
            xf = x.astype(jnp.float32)
            mu = xf.mean(-1, keepdims=True)
            var = xf.var(-1, keepdims=True)
            y = (xf - mu) * jax.lax.rsqrt(var + eps) * g.astype(jnp.float32) + b.astype(jnp.float32)
            return y.astype(x.dtype)

        def _conv1d(x, w, stride):
            return jax.lax.conv_general_dilated(x, w, (stride,), 'VALID', dimension_numbers=('NCH', 'OIH', 'NCH'))
        conv_ws = [conv_w0, conv_w1, conv_w2, conv_w3, conv_w4, conv_w5, conv_w6]
        ln_gs = [ln_g0, ln_g1, ln_g2, ln_g3, ln_g4, ln_g5, ln_g6]
        ln_bs = [ln_b0, ln_b1, ln_b2, ln_b3, ln_b4, ln_b5, ln_b6]
        strides = [s for _, _, s in CONVS]
        h = x[:, None, :]
        for w, g, b, s in zip(conv_ws, ln_gs, ln_bs, strides):
            h = _conv1d(h, w, s)
            h = jnp.swapaxes(h, -2, -1)
            h = _fp32_layernorm(h, g, b)
            h = jnp.swapaxes(h, -2, -1)
            h = jax.nn.gelu(h, approximate=False)
        h = jnp.swapaxes(h, 1, 2)
        norm_h = _fp32_layernorm(h, fln_g, fln_b)
        out = norm_h @ proj_w + proj_b
        return out

    def _L0_attn_ref(x, w_qkv, w_proj, b_proj):
        import jax, jax.numpy as jnp
        import numpy as np
        NUM_HEADS = 12
        NUM_LANDMARKS = 64
        PINV_ITERS = 6

        def moore_penrose_iter_pinv(x, iters=PINV_ITERS):
            abs_x = jnp.abs(x)
            col = abs_x.sum(axis=-1)
            row = abs_x.sum(axis=-2)
            z = jnp.swapaxes(x, -1, -2) / (jnp.max(col) * jnp.max(row))
            I = jnp.eye(x.shape[-1], dtype=x.dtype)
            for _ in range(iters):
                xz = x @ z
                z = 0.25 * z @ (13.0 * I - xz @ (15.0 * I - xz @ (7.0 * I - xz)))
            return z

        def _reference_tuple_inner(x, w_qkv, w_proj, b_proj):
            B, N, C = x.shape
            H = NUM_HEADS
            m = NUM_LANDMARKS
            d = C // H
            scale = d ** (-0.5)
            original_N = N
            rem = N % m
            if rem > 0:
                x = jnp.pad(x, ((0, 0), (m - rem, 0), (0, 0)))
                N = x.shape[1]
            qkv = x @ w_qkv.T
            q, k, v = jnp.split(qkv, 3, axis=-1)
            to_heads = lambda t: t.reshape(B, N, H, d).transpose(0, 2, 1, 3)
            q, k, v = (to_heads(q), to_heads(k), to_heads(v))
            q = q * scale
            l = N // m
            q_landmarks = q.reshape(B, H, m, l, d).mean(axis=3)
            k_landmarks = k.reshape(B, H, m, l, d).mean(axis=3)
            sim1 = jnp.einsum('bhnd,bhmd->bhnm', q, k_landmarks)
            sim2 = jnp.einsum('bhid,bhjd->bhij', q_landmarks, k_landmarks)
            sim3 = jnp.einsum('bhmd,bhnd->bhmn', q_landmarks, k)
            attn1 = jax.nn.softmax(sim1, axis=-1)
            attn2 = jax.nn.softmax(sim2, axis=-1)
            attn3 = jax.nn.softmax(sim3, axis=-1)
            attn2_inv = moore_penrose_iter_pinv(attn2, PINV_ITERS)
            attn = attn1 @ attn2_inv @ attn3
            out = attn1 @ (attn2_inv @ (attn3 @ v))
            out = out.transpose(0, 2, 1, 3).reshape(B, N, C)
            out = out[:, -original_N:]
            out = out @ w_proj.T + b_proj
            return (out, attn)
        return _reference_tuple_inner(x, w_qkv, w_proj, b_proj)[0]

    def _L0_ffn_ref(x, router_w, w_gate, w_up, w_down, ws_gate, ws_up, ws_down, sg_w, sg_b):
        import jax, jax.numpy as jnp
        import numpy as np
        B, S, D = (4, 256, 192)
        E = 8
        H = 192
        HS = 768
        TOPK_ROUTED = 2
        probs = jax.nn.softmax(x @ router_w, axis=-1)
        gates, idx = jax.lax.top_k(probs, TOPK_ROUTED)
        gates = gates / jnp.sum(gates, axis=-1, keepdims=True)
        n_exp = router_w.shape[1]
        dense_g = jnp.sum(jax.nn.one_hot(idx, n_exp, dtype=x.dtype) * gates[..., None], axis=-2)
        g = jax.nn.silu(jnp.einsum('bsd,edh->bseh', x, w_gate))
        u = jnp.einsum('bsd,edh->bseh', x, w_up)
        expert_out = jnp.einsum('bseh,ehd->bsed', g * u, w_down)
        routed = jnp.einsum('bse,bsed->bsd', dense_g, expert_out)
        shared = jax.nn.silu(x @ ws_gate) * (x @ ws_up) @ ws_down
        alpha = jax.nn.sigmoid(x @ sg_w + sg_b)
        return alpha * shared + (1.0 - alpha) * routed
    h = _L0_tok_ref(x, L0_tok_conv_w0, L0_tok_ln_g0, L0_tok_ln_b0, L0_tok_conv_w1, L0_tok_ln_g1, L0_tok_ln_b1, L0_tok_conv_w2, L0_tok_ln_g2, L0_tok_ln_b2, L0_tok_conv_w3, L0_tok_ln_g3, L0_tok_ln_b3, L0_tok_conv_w4, L0_tok_ln_g4, L0_tok_ln_b4, L0_tok_conv_w5, L0_tok_ln_g5, L0_tok_ln_b5, L0_tok_conv_w6, L0_tok_ln_g6, L0_tok_ln_b6, L0_tok_fln_g, L0_tok_fln_b, L0_tok_proj_w, L0_tok_proj_b)
    h = h + _L0_attn_ref(_layernorm(h, axis=-1), L0_attn_w_qkv, L0_attn_w_proj, L0_attn_b_proj)
    h = h + _L0_ffn_ref(_layernorm(h, axis=-1), L0_ffn_router_w, L0_ffn_w_gate, L0_ffn_w_up, L0_ffn_w_down, L0_ffn_ws_gate, L0_ffn_ws_up, L0_ffn_ws_down, L0_ffn_sg_w, L0_ffn_sg_b)
    return h

_drawn_inputs = setup_inputs


def setup_inputs(seed=0):
    import zlib

    import numpy as np

    out = dict(_drawn_inputs(seed))
    spreads = {'L0_tok_ln_g0': (1.0, 0.2),
     'L0_tok_ln_b0': (0.0, 0.1),
     'L0_tok_ln_g1': (1.0, 0.2),
     'L0_tok_ln_b1': (0.0, 0.1),
     'L0_tok_ln_g2': (1.0, 0.2),
     'L0_tok_ln_b2': (0.0, 0.1),
     'L0_tok_ln_g3': (1.0, 0.2),
     'L0_tok_ln_b3': (0.0, 0.1),
     'L0_tok_ln_g4': (1.0, 0.2),
     'L0_tok_ln_b4': (0.0, 0.1),
     'L0_tok_ln_g5': (1.0, 0.2),
     'L0_tok_ln_b5': (0.0, 0.1),
     'L0_tok_ln_g6': (1.0, 0.2),
     'L0_tok_ln_b6': (0.0, 0.1),
     'L0_tok_fln_g': (1.0, 0.2),
     'L0_tok_fln_b': (0.0, 0.1),
     'L0_tok_proj_b': (0.0, 0.1)}
    factors = {'L0_ffn_router_w': 5.51,
     'L0_ffn_w_gate': 4.051,
     'L0_ffn_w_up': 4.009,
     'L0_ffn_w_down': 3.973,
     'L0_ffn_sg_w': 8.0}
    for name, (base, spread) in spreads.items():
        noise = np.random.default_rng([zlib.crc32(name.encode()), seed]).standard_normal(out[name].shape)
        drawn = base * np.exp(spread * noise) if base else spread * noise
        out[name] = jnp.asarray(drawn.astype(out[name].dtype))
    for name, factor in factors.items():
        out[name] = (out[name] * factor).astype(out[name].dtype)
    return out
```

```python
from contextlib import ExitStack
from math import sqrt

import numpy as np
import concourse.bass as bass
from concourse import mybir

ALU = mybir.AluOpType
ACT = mybir.ActivationFunctionType
F32 = mybir.dt.float32
BF16 = mybir.dt.bfloat16
I32 = mybir.dt.int32
U32 = mybir.dt.uint32
AX = mybir.AxisListType

P = 128
BATCH, SAMPLES = 64, 4000
CH = 128
K0, STRIDE0 = 10, 5
CENTRE_EPS = 1e-5
RSQRT_GUESS = float(0x5F3759DF)

GROUP = 8
ROUND = 2 * GROUP
ROUNDS = BATCH // ROUND

POS0, ROW0 = 800, 802
SLICES = 8
SL = POS0 // SLICES
XROW = SAMPLES + STRIDE0
PARTS = 3


class Layer:

    def __init__(self, n, taps, pos, row, per_chunk, chunks, slot_chunks):
        self.n, self.taps, self.pos, self.row = n, taps, pos, row
        self.per_chunk = per_chunk
        self.chunks = chunks
        self.cols = per_chunk * pos
        self.w = self.cols // 4
        self.first_tap = slot_chunks


L1 = Layer(1, 3, 400, 402, 1, 8, 0)
L2 = Layer(2, 3, 200, 202, 2, 4, 3)
L3 = Layer(3, 3, 100, 102, 4, 2, 6)
L4 = Layer(4, 3, 50, 50, 8, 8, 9)
L5 = Layer(5, 2, 24, 24, 16, 4, 12)
L6 = Layer(6, 2, 12, 12, 32, 2, 14)
LAYERS = {x.n: x for x in (L1, L2, L3, L4, L5, L6)}
TAPS = 16

TOK = BATCH * L6.pos
TT = TOK // P
SEQ = L6.pos
D, HEADS, DH = 192, 12, 16
KD = D // 96
LANDMARKS = 64
PADS = LANDMARKS - SEQ
PINV_ITERS = 6
EXPERTS, HID, SHID = 8, 192, 768


class Steps:

    def __init__(self, eng, sem):
        self.eng, self.sem, self.base, self.n = eng, sem, 0, 0

    def done(self, ins):
        ins.then_inc(self.sem, 1)
        self.n += 1

    def settle(self):
        self.eng.wait_ge(self.sem, self.base + self.n)

    def at(self, base):
        self.base, self.n = base, 0


def newton_rsqrt(nc, steps, v, y, t, u):
    steps.done(nc.vector.tensor_scalar(y.bitcast(I32), v.bitcast(I32), -0.5, RSQRT_GUESS, ALU.mult, ALU.add))
    for _ in range(3):
        steps.settle()
        steps.done(nc.vector.tensor_tensor(t, v, y, ALU.mult))
        steps.settle()
        steps.done(nc.vector.scalar_tensor_tensor(out=u, in0=t, scalar=-0.5, in1=y, op0=ALU.mult, op1=ALU.mult))
        steps.settle()
        steps.done(nc.vector.scalar_tensor_tensor(out=y, in0=u, scalar=1.5, in1=y, op0=ALU.add, op1=ALU.mult))
    steps.settle()



def round_plan(last):
    order = []
    conv = lambda l, s, p: order.append(("conv", l, s, p))
    var = lambda l, s, p: order.append(("var", l, s, p))
    norm = lambda l, s: order.append(("norm", l, s, 0))
    rows = lambda l, s: order.append(("rows", l, s, 0))

    def scale(l, s, a, b):
        for c in range(a, b):
            order.append(("scale", l, s, c))
            if c % 2:
                order.append(("gelu", l, s, c // 2))

    for p in range(4):
        conv(1, 0, p)
        if p:
            var(1, 0, p - 1)
    conv(1, 1, 0); var(1, 0, 3); norm(1, 0)
    conv(1, 1, 1); var(1, 1, 0); rows(1, 0)
    scale(1, 0, 0, 3)
    conv(1, 1, 2); var(1, 1, 1)
    scale(1, 0, 3, 6)
    conv(1, 1, 3); var(1, 1, 2)
    scale(1, 0, 6, 8)
    conv(2, 0, 0); var(1, 1, 3); norm(1, 1)
    conv(2, 0, 1); var(2, 0, 0); rows(1, 1)
    scale(1, 1, 0, 4)
    var(2, 0, 1); norm(2, 0)
    scale(1, 1, 4, 8)
    conv(2, 1, 0); rows(2, 0)
    scale(2, 0, 0, 2)
    conv(2, 1, 1); var(2, 1, 0)
    scale(2, 0, 2, 4)
    var(2, 1, 1); norm(2, 1)
    conv(3, 0, 0); rows(2, 1)
    scale(2, 1, 0, 4)
    var(3, 0, 0); norm(3, 0)
    conv(3, 1, 0); rows(3, 0)
    var(3, 1, 0); norm(3, 1)
    first = lambda s, a, b: [order.append(("first", 0, s, p)) for p in range(a, b)]
    if not last:
        first(0, 0, 2)
    scale(3, 0, 0, 2)
    if not last:
        first(0, 2, 8)
    rows(3, 1)
    scale(3, 1, 0, 2)
    if not last:
        first(1, 0, 8)
    return counted(order)


def tail_plan():
    order = []
    for l, pairs in ((4, 4), (5, 2), (6, 1)):
        for p in range(pairs):
            order.append(("conv", l, 0, p))
            if p:
                order.append(("var", l, 0, p - 1))
        order += [("var", l, 0, pairs - 1), ("norm", l, 0, 0), ("rows", l, 0, 0)]
        for c in range(2 * pairs):
            order.append(("scale", l, 0, c))
            if c % 2:
                order.append(("gelu", l, 0, c // 2))
    return counted(order)


def counted(order):
    n = dict.fromkeys(("pair", "conv", "var", "norm", "rows", "scale", "gelu", "first"), 0)
    out = []
    for what, l, s, p in order:
        out.append((what, l, s, p, dict(n)))
        n[what] += 1
        n["pair"] += what in ("conv", "first")
    return out, n


class Origin:

    def __init__(self, rounds, per, extra_pairs=0):
        self.pair = ROUND + per["pair"] * rounds - extra_pairs
        self.conv, self.sets = per["conv"] * rounds, per["norm"] * rounds
        self.scale, self.gelu = per["scale"] * rounds, per["gelu"] * rounds


def number_of(plan, what, layer, slot, p, kind):
    return next(n[kind] for a, b, c, d, n in plan if (a, b, c, d) == (what, layer, slot, p))


def gelus_before(plan, layer, slot):
    return {p: n["gelu"] for what, l, s, p, n in plan if (what, l, s) == ("gelu", layer, slot)}


def conv_tower(nc, io, res, top):
    body, per = round_plan(False)
    last, per_last = round_plan(True)
    tail, _ = tail_plan()
    PRE = ROUND
    sem = lambda n: top.enter_context(nc.semaphore(n))
    x_in = sem("x_in")
    w_in = sem("w_in")
    s_const = sem("s_const")
    s_w0 = sem("s_w0")
    w0_in = sem("w0_in")
    weights_ready = sem("weights_ready")
    parts_ready = sem("parts_ready")
    parts_out = sem("parts_out")
    win_in = sem("win_in")
    y_ready = sem("y_ready")
    y_copied = sem("y_copied")
    y_taken = sem("y_taken")
    var_read = sem("var_read")
    var_done = sem("var_done")
    rstd_ready = sem("rstd_ready")
    rstd_turned = sem("rstd_turned")
    rows_ready = sem("rows_ready")
    bc_ready = sem("bc_ready")
    scaled = sem("scaled")
    gelu_done = sem("gelu_done")
    steps_sem = sem("steps_sem")

    ident, h6, lnp = res["ident"], res["h6"], res["lnp"]
    with ExitStack() as ctx:
        sb = lambda n, s, d=F32: ctx.enter_context(nc.sbuf_tensor(n, s, d))
        ps = ctx.enter_context(nc.psum_tensor("ps", [P, 8, 512], F32))
        ypair = [ps[:, 0:2, :], ps[:, 2:4, :]]
        spread = [ps[:, 4, :], ps[:, 5, :]]
        var_ps = ps[:, 6, :]
        rows_ps = ps[:, 7, :].bitcast(BF16)

        h0 = sb("h0", [P, 2, GROUP, ROW0])
        h1 = sb("h1", [P, 2, GROUP, L1.row])
        h2 = sb("h2", [P, 2, GROUP, L2.row])
        h3 = sb("h3", [P, ROUNDS, 2, GROUP, L3.row])
        h4 = sb("h4", [P, BATCH, L4.row])
        h5 = sb("h5", [P, BATCH, L5.row])
        sq = sb("sq", [P, 2, 2, 400])
        win = sb("win", [PARTS * PARTS * K0, ROUND * POS0], BF16)
        w = sb("w", [P, TAPS, CH])
        wmean = sb("wmean", [P, TAPS])
        w0 = sb("w0", [P, K0])
        w0_parts = sb("w0_parts", [K0, PARTS, CH], BF16)
        w0_rest = sb("w0_rest", [K0, CH])
        w0_stack = sb("w0_stack", [PARTS * PARTS * K0, CH], BF16)
        w0_pairs = sb("w0_pairs", [P, K0, K0])
        gram = sb("gram", [P, K0, K0])
        averager = sb("averager", [P, P])
        pick = sb("pick", [96, 8, P], BF16)
        ident16 = sb("ident16", [P, P], BF16)
        xs = sb("xs", [P, STRIDE0 * (SL + 1)])
        u = sb("u", [P, K0, SL])
        scaled_win = sb("scaled_win", [P, K0, SL])
        parts = sb("parts", [P, PARTS, K0, SL], BF16)
        v0, r0, t0, t1 = (sb(n, [P, SL]) for n in ("v0", "r0", "t0", "t1"))
        vs, rs, ts, us, rest = (sb(n, [100, 2, 32]) for n in ("vs", "rs", "ts", "us", "rest"))
        rparts = sb("rparts", [100, 2, 4, 96], BF16)
        rows = sb("rows", [96, 2, 400], BF16)

        windows_dram = nc.dram_tensor("windows_dram", [ROUNDS, PARTS * K0, ROUND * POS0], BF16, kind="Internal").ap()
        xwin = xs[:, :].rearrange("p (t k) -> p k t", k=STRIDE0)
        tap = lambda k: xwin[:, k % STRIDE0, k // STRIDE0:k // STRIDE0 + SL]

        def chunk(l, slot, c, r):
            L = LAYERS[l]
            a, n = c * L.per_chunk, L.per_chunk
            if l <= 2:
                return (h1, h2)[l - 1][:, slot, a:a + n, 0:L.pos]
            if l == 3:
                return h3[:, bass.ds(r, 1), slot, a:a + n, 0:L.pos].rearrange("p o b t -> p (o b) t")
            if l == 4:
                return h4[:, a:a + n, 0:L.pos]
            if l == 5:
                return h5[:, a:a + n, 0:L.pos]
            return h6[:, :].rearrange("p (b t) -> p b t", t=L.pos)[:, a:a + n, :]

        def source(l, slot, c, t):
            L = LAYERS[l]
            a, n = c * L.per_chunk, L.per_chunk
            cut = slice(t, t + 2 * L.pos - 1, 2)
            if l <= 3:
                return (h0, h1, h2)[l - 1][:, slot, a:a + n, cut]
            if l == 4:
                return h3[:, :, :, :, :].rearrange("p r s b t -> p (r s b) t")[:, a:a + n, cut]
            return (h4, h5)[l - 5][:, a:a + n, cut]

        at_tail = Origin(ROUNDS, per, per["pair"] - per_last["pair"])

        def slot_of(l, s):
            return s if l <= 3 else l % 2

        def for_rounds(eng, run):
            run(body, 0, Origin(0, per))
            with eng.Fori(1, ROUNDS - 1) as r:
                run(body, r, Origin(r, per))
            run(last, ROUNDS - 1, Origin(ROUNDS - 1, per))

        def joined(l, s, p, r):
            L = LAYERS[l]
            a, n = 2 * p * L.per_chunk, 2 * L.per_chunk
            if l <= 2:
                return (h1, h2)[l - 1][:, s, a:a + n, 0:L.pos]
            if l == 3:
                return h3[:, bass.ds(r, 1), s, a:a + n, 0:L.pos].rearrange("p o b t -> p (o b) t")
            if l == 4:
                return h4[:, a:a + n, 0:L.pos]
            if l == 5:
                return h5[:, a:a + n, 0:L.pos]
            return h6[:, :].rearrange("p (b t) -> p b t", t=L.pos)[:, a:a + n, :]

        with nc.Block() as block:

            @block.sync
            def _(sp):
                def samples(r):
                    b0 = ROUND * r
                    src = io["x"][bass.ds(b0, ROUND), :]
                    lanes = bass.AP(src.tensor, src.offset, [[XROW, ROUND], [STRIDE0 * SL, SLICES], [1, STRIDE0 * (SL + 1)]])
                    sp.dma_start(xs[:, :], lanes).then_inc(x_in, 16)

                def windows(r, more):
                    sp.wait_ge(parts_ready, r + 1)
                    if more:
                        samples(r + 1)
                    scratch = windows_dram[bass.ds(r, 1), :, :].rearrange("o k c -> (o k) c")
                    sp.dma_start(scratch.rearrange("k (l t) -> l k t", t=SL),
                                 parts[:, :, :, :].rearrange("p a k t -> p (a k) t")).then_inc(parts_out, 16)
                    sp.wait_ge(parts_out, 16 * (r + 1))
                    return scratch

                def back(scratch):
                    for a in range(PARTS):
                        sp.dma_start(win[a * PARTS * K0:(a + 1) * PARTS * K0, :], scratch).then_inc(win_in, 16)

                samples(0)
                sp.dma_start(w0[:, :], io["w0"]).then_inc(w_in, 16)
                sp.dma_start(lnp[:, :], io["lnp"]).then_inc(w_in, 16)
                sp.dma_start(w[:, :, :], io["w"]).then_inc(w_in, 16)
                sp.wait_ge(s_w0, 5)
                for a in range(PARTS):
                    for b in range(PARTS):
                        row = (a * PARTS + b) * K0
                        sp.dma_start(w0_stack[row:row + K0, :], w0_parts[:, a, :]).then_inc(w0_in, 16)
                back(windows(0, True))

                def middle(r):
                    scratch = windows(r, True)
                    sp.wait_ge(y_ready, PRE + per["pair"] * (r - 1))
                    back(scratch)

                with sp.Fori(1, ROUNDS - 1) as r:
                    middle(r)
                scratch = windows(ROUNDS - 1, False)
                sp.wait_ge(y_ready, PRE + per["pair"] * (ROUNDS - 2))
                back(scratch)

            @block.gpsimd
            def _(pool):
                pool.memset(averager[:, :], 1.0 / CH).then_inc(s_const, 1)
                pool.memset(ident[:, :], 0.0).then_inc(s_const, 1)
                pool.memset(ident16[:, :], 0.0).then_inc(s_const, 1)
                pool.memset(pick[:, :, :], 0.0).then_inc(s_const, 1)
                pool.memset(rparts[:, :, :, :], 0.0).then_inc(s_const, 1)
                pool.memset(h0[:, :, :, POS0:ROW0], 0.0).then_inc(s_const, 1)
                pool.memset(h1[:, :, :, L1.pos:L1.row], 0.0).then_inc(s_const, 1)
                pool.memset(h2[:, :, :, L2.pos:L2.row], 0.0).then_inc(s_const, 1)
                pool.memset(h3[:, :, :, :, L3.pos:L3.row], 0.0).then_inc(s_const, 1)
                pool.wait_ge(s_const, 4)
                for m in (ident, ident16):
                    pool.affine_select(out=m[:, :], in_=m[:, :], compare_op=ALU.not_equal, fill=1.0, base=0,
                                       pattern=[[-1, P]], channel_multiplier=1).then_inc(s_const, 1)
                for a in range(PARTS):
                    if a:
                        pool.wait_ge(s_const, 11 + a)
                    pool.affine_select(out=pick[:, :, :], in_=pick[:, :, :], compare_op=ALU.not_equal, fill=1.0,
                                       base=-32 * a, pattern=[[-1, 8], [0, P]], channel_multiplier=1).then_inc(s_const, 1)

            CONSTS = 14

            @block.tensor
            def _(pe):
                pe.wait_ge(s_const, CONSTS)
                pe.wait_ge(w_in, 48)
                pe.matmul(spread[0][:, 0:K0], averager[:, :], w0[:, :], start=True, stop=True).then_inc(s_w0, 1)
                pe.wait_ge(s_w0, 3)
                pe.matmul(spread[1][:, 0:K0 * K0], averager[:, :], w0_pairs[:, :, :], start=True, stop=True).then_inc(s_w0, 1)
                pe.transpose(ps[0:K0, 6, 0:CH], w0[:, :], ident[:, :]).then_inc(weights_ready, 1)

                def first(b, bank):
                    for h in range(2):
                        mm = pe.matmul(ypair[bank][:, h, 0:400], w0_stack[:, :],
                                       win[:, b * POS0 + h * 400:b * POS0 + h * 400 + 400], start=True, stop=True)
                    mm.then_inc(y_ready, 1)

                pe.wait_ge(w0_in, 16 * PARTS * PARTS)
                pe.wait_ge(win_in, 48)
                for b in range(PRE):
                    if b >= 2:
                        pe.wait_ge(y_taken, b - 1)
                    first(b, b % 2)
                pe.wait_ge(weights_ready, 2)

                PREVIOUS = {False: ["first", "first"], True: ["conv", "conv"]}

                def run(plan, r, o):
                    pairs = [x[0] for x in plan if x[0] in ("conv", "first")]
                    for what, l, s, p, n in plan:
                        L, pair, bank = LAYERS.get(l), n["pair"], n["pair"] % 2
                        if what in ("conv", "first"):
                            user = (PREVIOUS[plan is tail] + pairs)[pair]
                            before = (PREVIOUS[plan is tail] + pairs)[pair + 1]
                            if user == "first":
                                pe.wait_ge(y_taken, o.pair + pair - 1)
                            else:
                                pe.wait_ge(y_copied, o.conv + n["conv"] - (before == "conv"))
                        if what == "first":
                            if n["first"] == 0:
                                pe.wait_ge(win_in, 48 * (r + 2))
                            first(s * GROUP + p, bank)
                        elif what == "conv":
                            if l == 1:
                                pe.wait_ge(y_taken, o.pair - PRE + GROUP * s + 2 * p + 2)
                            elif l == 4:
                                pe.wait_ge(gelu_done, o.gelu)
                            else:
                                done = gelus_before(plan, l - 1, s)
                                pe.wait_ge(gelu_done, o.gelu + done[min(2 * p + 1, max(done))] + 1)
                            for c in range(2):
                                out = ypair[bank][:, c, 0:L.cols].rearrange("p (b t) -> p b t", t=L.pos)
                                for t in range(L.taps):
                                    mm = pe.matmul(out, w[:, L.first_tap + t, :], source(l, s, 2 * p + c, t),
                                                   start=(t == 0), stop=(t == L.taps - 1))
                            mm.then_inc(y_ready, 1)
                        elif what == "var":
                            pe.wait_ge(y_taken, o.pair + number_of(plan, "conv", l, s, p, "pair") + 1)
                            before = o.sets + n["norm"]
                            if p == 0 and not (isinstance(before, int) and before < 1):
                                pe.wait_ge(var_read, before)
                            for c in range(2):
                                for q in range(4):
                                    at = q * L.chunks + 2 * p + c
                                    mm = pe.matmul(var_ps[0:L.w, at:at + 1],
                                                   sq[:, n["var"] % 2, c, q * L.w:(q + 1) * L.w], averager[:, 0:1],
                                                   start=True, stop=True)
                            mm.then_inc(var_done, 1)
                        elif what == "rows":
                            pe.wait_ge(rstd_ready, o.sets + n["rows"] + 1)
                            for q in range(4):
                                mm = pe.transpose(rows_ps[0:96, q * L.w:(q + 1) * L.w],
                                                  rparts[0:L.w, slot_of(l, s), q, :], ident16[0:L.w, 0:L.w])
                            mm.then_inc(rstd_turned, 1)
                        elif what == "scale":
                            if p == 0:
                                pe.wait_ge(rows_ready, o.sets + n["rows"])
                            used = o.scale + n["scale"] - 1
                            if not (isinstance(used, int) and used < 1):
                                pe.wait_ge(scaled, used)
                            pe.matmul(spread[n["scale"] % 2][:, 0:L.cols], pick[:, p, :],
                                      rows[:, slot_of(l, s), 0:L.cols], start=True, stop=True).then_inc(bc_ready, 1)

                for_rounds(pe, run)
                run(tail, ROUNDS, at_tail)

            @block.scalar
            def _(act):
                act.wait_ge(w_in, 48)

                def first(s, p, b, pair):
                    act.wait_ge(y_ready, pair + 1)
                    act.activation(h0[:, s, p, 0:POS0].rearrange("p (h t) -> p h t", h=2), ypair[b][:, :, 0:400],
                                   ACT.Gelu, scale=lnp[:, 0:1], bias=lnp[:, 1:2]).then_inc(y_taken, 1)

                for p in range(PRE):
                    first(p // GROUP, p % GROUP, p % 2, p)

                def run(plan, r, o):
                    for what, l, s, p, n in plan:
                        L, bank = LAYERS.get(l), n["pair"] % 2
                        if what == "first":
                            first(s, p, bank, o.pair + n["pair"])
                        elif what == "conv":
                            act.wait_ge(y_copied, o.conv + n["conv"] + 1)
                            used = o.conv + n["conv"] - 1
                            if not (isinstance(used, int) and used < 1):
                                act.wait_ge(var_done, used)
                            if l == 3:
                                act.nop(nofuse=True)
                            act.activation(sq[:, n["conv"] % 2, :, 0:L.cols].rearrange("p c (b t) -> p c b t", t=L.pos),
                                           joined(l, s, p, r).rearrange("p (c b) t -> p c b t", c=2), ACT.Square).then_inc(y_taken, 1)
                        elif what == "gelu":
                            act.wait_ge(scaled, o.scale + n["scale"])
                            if l == 3:
                                act.nop(nofuse=True)
                            both = joined(l, s, p, r)
                            act.activation(both, both, ACT.Gelu, scale=lnp[:, 2 * l:2 * l + 1],
                                           bias=lnp[:, 2 * l + 1:2 * l + 2]).then_inc(gelu_done, 1)

                for_rounds(act, run)
                run(tail, ROUNDS, at_tail)

            @block.vector
            def _(dve):
                steps = Steps(dve, steps_sem)
                dve.wait_ge(s_w0, 1)
                nc.vector.tensor_tensor(w0[:, :], w0[:, :], spread[0][:, 0:K0], ALU.subtract).then_inc(s_w0, 1)
                dve.wait_ge(s_w0, 2)
                nc.vector.tensor_tensor(w0_pairs[:, :, :], w0[:, :].unsqueeze(2).broadcast_to([P, K0, K0]),
                                        w0[:, :].unsqueeze(1).broadcast_to([P, K0, K0]), ALU.mult).then_inc(s_w0, 1)
                dve.wait_ge(s_w0, 4)
                steps.done(nc.vector.tensor_scalar(gram[:, :, :], spread[1][:, 0:K0 * K0].rearrange("p (a b) -> p a b", a=K0), 2.0, None, ALU.mult))
                dve.wait_ge(weights_ready, 1)
                turned = ps[0:K0, 6, 0:CH]
                steps.done(nc.vector.tensor_copy(w0_parts[:, 0, :], turned))
                steps.settle()
                steps.done(nc.vector.tensor_tensor(w0_rest[:, :], turned, w0_parts[:, 0, :], ALU.subtract))
                steps.settle()
                steps.done(nc.vector.tensor_copy(w0_parts[:, 1, :], w0_rest[:, :]))
                steps.settle()
                nc.vector.tensor_tensor(w0_parts[:, 2, :], w0_rest[:, :], w0_parts[:, 1, :], ALU.subtract).then_inc(s_w0, 1)

                def prepare(r, part):
                    if part == 0:
                        dve.wait_ge(x_in, 16 * (r + 1))
                    if part < K0:
                        steps.settle()
                        for k in range(K0 - part):
                            l = k + part
                            if part == 0:
                                steps.done(nc.vector.tensor_scalar(u[:, k, :], tap(l), gram[:, k, l:l + 1], 0.5, ALU.mult, ALU.mult))
                            else:
                                steps.done(nc.vector.scalar_tensor_tensor(out=u[:, k, :], in0=tap(l), scalar=gram[:, k, l:l + 1],
                                                                          in1=u[:, k, :], op0=ALU.mult, op1=ALU.add))
                    elif part == K0:
                        steps.settle()
                        for h in range(2):
                            steps.done(nc.vector.tensor_tensor(u[:, 5 * h:5 * h + 5, :], u[:, 5 * h:5 * h + 5, :],
                                                               xwin[:, :, h:h + SL], ALU.mult))
                        steps.settle()
                        steps.done(nc.vector.tensor_reduce(v0[:, :], u[:, :, :].rearrange("p k t -> p t k"), AX.X, ALU.add))
                        steps.settle()
                        steps.done(nc.vector.tensor_scalar(v0[:, :], v0[:, :], 0.0, CENTRE_EPS, ALU.max, ALU.add))
                        steps.settle()
                    elif part == K0 + 1:
                        newton_rsqrt(nc, steps, v0[:, :], r0[:, :], t0[:, :], t1[:, :])
                    elif part == K0 + 2:
                        for h in range(2):
                            steps.done(nc.vector.tensor_tensor(scaled_win[:, 5 * h:5 * h + 5, :], xwin[:, :, h:h + SL],
                                                               r0[:, :].unsqueeze(1).broadcast_to([P, 5, SL]), ALU.mult))
                        steps.settle()
                        if not (isinstance(r, int) and r == 0):
                            dve.wait_ge(parts_out, 16 * r)
                        steps.done(nc.vector.tensor_copy(parts[:, 0, :, :], scaled_win[:, :, :]))
                        steps.settle()
                    else:
                        steps.done(nc.vector.tensor_tensor(scaled_win[:, :, :], scaled_win[:, :, :], parts[:, 0, :, :], ALU.subtract))
                        steps.settle()
                        steps.done(nc.vector.tensor_copy(parts[:, 1, :, :], scaled_win[:, :, :]))
                        steps.settle()
                        nc.vector.tensor_tensor(parts[:, 2, :, :], scaled_win[:, :, :], parts[:, 1, :, :],
                                                ALU.subtract).then_inc(parts_ready, 1)

                PREP = K0 + 4
                steps.settle()
                for part in range(PREP):
                    prepare(0, part)
                dve.wait_ge(w_in, 48)
                steps.done(nc.vector.tensor_reduce(wmean[:, :], w[:, :, :], AX.X, ALU.add))
                steps.settle()
                steps.done(nc.vector.tensor_scalar(wmean[:, :], wmean[:, :], 1.0 / CH, None, ALU.mult))
                steps.settle()
                nc.vector.tensor_tensor(w[:, :, :], w[:, :, :], wmean[:, :].unsqueeze(2).broadcast_to([P, TAPS, CH]),
                                        ALU.subtract).then_inc(weights_ready, 1)
                dve.wait_ge(s_const, CONSTS)

                def run(plan, r, o):
                    prep = list(range(PREP)) if plan is body else []
                    for what, l, s, p, n in plan:
                        L, bank = LAYERS.get(l), n["pair"] % 2
                        if what == "conv":
                            dve.wait_ge(y_ready, o.pair + n["pair"] + 1)
                            nc.vector.tensor_copy(
                                joined(l, s, p, r).rearrange("p (c b) t -> p c b t", c=2),
                                ypair[bank][:, :, 0:L.cols].rearrange("p c (b t) -> p c b t", t=L.pos)).then_inc(y_copied, 1)
                            for _ in range(2):
                                if prep:
                                    prepare(r + 1, prep.pop(0))
                        elif what == "norm":
                            k, sl, wide = 4 * L.chunks, slot_of(l, s), L.w
                            v, y, t, q, left = (x[0:wide, sl, 0:k] for x in (vs, rs, ts, us, rest))
                            part = lambda a: rparts[0:wide, sl, :, 32 * a:32 * a + L.chunks]
                            four = lambda x: x.rearrange("p (q c) -> p q c", q=4)
                            dve.wait_ge(var_done, o.conv + n["var"])
                            nc.vector.tensor_scalar(v, var_ps[0:wide, 0:k], CENTRE_EPS, None, ALU.add).then_inc(var_read, 1)
                            dve.wait_ge(var_read, o.sets + n["norm"] + 1)
                            newton_rsqrt(nc, steps, v, y, t, q)
                            steps.done(nc.vector.tensor_copy(part(0), four(y)))
                            steps.settle()
                            steps.done(nc.vector.tensor_tensor(four(left), four(y), part(0), ALU.subtract))
                            steps.settle()
                            steps.done(nc.vector.tensor_copy(part(1), four(left)))
                            steps.settle()
                            nc.vector.tensor_tensor(part(2), four(left), part(1), ALU.subtract).then_inc(rstd_ready, 1)
                        elif what == "rows":
                            dve.wait_ge(rstd_turned, o.sets + n["rows"] + 1)
                            nc.vector.tensor_copy(rows[:, slot_of(l, s), 0:L.cols],
                                                  rows_ps[0:96, 0:L.cols]).then_inc(rows_ready, 1)
                        elif what == "scale":
                            dve.wait_ge(bc_ready, o.scale + n["scale"] + 1)
                            if p % 2 == 0:
                                dve.wait_ge(y_copied, o.conv + number_of(plan, "conv", l, s, p // 2, "conv") + 1)
                            h = chunk(l, s, p, r)
                            nc.vector.tensor_tensor(h, h, spread[n["scale"] % 2][:, 0:L.cols].rearrange(
                                "p (b t) -> p b t", t=L.pos), ALU.mult).then_inc(scaled, 1)
                    assert not prep

                start = steps.n
                run(body, 0, Origin(0, per))
                each = steps.n - start
                with dve.Fori(1, ROUNDS - 1) as r:
                    steps.at(start + each * r)
                    run(body, r, Origin(r, per))
                    assert steps.n == each
                steps.at(start + each * (ROUNDS - 1))
                run(last, ROUNDS - 1, Origin(ROUNDS - 1, per))
                run(tail, ROUNDS, at_tail)



class Rows(Steps):

    def mark(self):
        return self.base + self.n

    def until(self, mark):
        self.eng.wait_ge(self.sem, mark)


def normalise(nc, steps, src, dst, stats, mv, y, t, u):
    for i in range(TT):
        steps.done(nc.vector.bn_stats(stats[:, i, :], src[i]))
    steps.settle()
    for i in range(TT):
        steps.done(nc.vector.bn_aggr(mv[:, i, :], stats[:, i, :]))
    steps.settle()
    steps.done(nc.vector.tensor_scalar(mv[:, :, 1], mv[:, :, 1], CENTRE_EPS, None, ALU.add))
    steps.settle()
    steps.done(nc.vector.tensor_copy(stats[:, :, 0], mv[:, :, 1]))
    steps.settle()
    newton_rsqrt(nc, steps, stats[:, :, 0], y, t, u)
    for i in range(TT):
        steps.done(nc.vector.tensor_scalar(dst[i], src[i], mv[:, i, 0:1], y[:, i:i + 1], ALU.subtract, ALU.mult))
    steps.settle()


def turn(pe, ps, src, ident, done):
    for k in range(KD):
        for t in range(TT):
            mm = pe.transpose(ps[0:96, k, t * P:(t + 1) * P], src[:, t, 96 * k:96 * k + 96], ident[:, :])
    mm.then_inc(done, 1)


def attention(nc, io, res, top):
    sem = lambda n: top.enter_context(nc.semaphore(n))
    a_in = sem("a_in")
    turned = sem("turned")
    a_steps = sem("a_steps")
    to_pe = sem("to_pe")
    projected = sem("projected")
    qkv_ready = sem("qkv_ready")
    qkv_copied = sem("qkv_copied")
    qkv_out = sem("qkv_out")
    lanes_in = sem("lanes_in")
    scores_ready = sem("scores_ready")
    exp_done = sem("exp_done")
    peaks = sem("peaks")
    eye_ready = sem("eye_ready")
    row_done = sem("row_done")
    mirrored = sem("mirrored")
    out_lanes = sem("out_lanes")
    o_out = sem("o_out")
    o_in = sem("o_in")
    R = SEQ + 1
    HL = HEADS // 2
    ROOT = sqrt(PADS)
    ident, h6, lnp, hidden = (res[k] for k in ("ident", "h6", "lnp", "hidden"))
    with ExitStack() as ctx:
        sb = lambda n, s, d=F32: ctx.enter_context(nc.sbuf_tensor(n, s, d))
        pt = ctx.enter_context(nc.psum_tensor("pt", [P, 4, 1024], F32))
        proj_w = sb("proj_w", [CH, D])
        qkv_w = sb("qkv_w", [96, KD, 3 * D])
        out_w = sb("out_w", [96, KD, D])
        proj_b, out_b = sb("proj_b", [P, D]), sb("out_b", [P, D])
        norm6 = sb("norm6", [P, TT, CH])
        norm6t = sb("norm6t", [CH, TOK])
        stats, mv = sb("a_stats", [P, TT, 6]), sb("a_mv", [P, TT, 2])
        y6, t6, u6 = sb("a_y6", [P, TT]), sb("a_t6", [P, TT]), sb("a_u6", [P, TT])
        xhat = sb("a_xhat", [P, TT, D])
        xhat_t = sb("a_xhat_t", [96, KD, TOK])
        qkv = sb("qkv", [P, TT, 3 * D])
        lanes = sb("lanes", [P, SEQ, 3, HL * DH])
        rowt = sb("rowt", [P, 2, HL * R * DH])
        scores = sb("scores", [P, HL, SEQ, SEQ])
        peak, epad, den, rden = (sb(n, [P, HL, SEQ]) for n in ("peak", "epad", "den", "rden"))
        smat = sb("smat", [P, HL, R, R])
        e1, e2, c4 = (sb(n, [P, HL, R, R]) for n in ("e1", "e2", "c4"))
        eye = sb("eye", [P, R, R])
        norms, all_norms, scale = sb("norms", [P, 2]), sb("all_norms", [P, 2]), sb("scale", [P, 2])
        padsum = sb("padsum", [P, HL])
        wv = sb("wv", [P, HL, R, DH])
        attn = sb("attn", [P, SEQ, HL * DH])
        attn_tok = sb("attn_tok", [P, TT, D])
        qkv_dram = nc.dram_tensor("qkv_dram", [TOK, 3 * D], F32, kind="Internal").ap()
        attn_dram = nc.dram_tensor("attn_dram", [TOK, D], F32, kind="Internal").ap()
        q_l, k_l, v_l = (lanes[:, :, a, :] for a in range(3))
        LOADS = 5
        ROWS_EACH = 2 * (R - 1)

        with nc.Block() as block:

            @block.sync
            def _(sp):
                sp.dma_start(proj_w[:, :], io["proj_w"]).then_inc(a_in, 16)
                sp.dma_start(proj_b[:, :], io["proj_b"].partition_broadcast(P)).then_inc(a_in, 16)
                sp.dma_start(qkv_w[:, :, :], io["qkv_w"].rearrange("(k p) n -> p k n", k=KD)).then_inc(a_in, 16)
                sp.dma_start(out_w[:, :, :], io["out_w"].rearrange("(k p) n -> p k n", k=KD)).then_inc(a_in, 16)
                sp.dma_start(out_b[:, :], io["out_b"].partition_broadcast(P)).then_inc(a_in, 16)
                for t in range(TT):
                    sp.wait_ge(qkv_copied, t + 1)
                    sp.dma_start(qkv_dram[t * P:(t + 1) * P, :], qkv[:, t, :]).then_inc(qkv_out, 16)
                sp.wait_ge(qkv_out, 16 * TT)
                for half in range(2):
                    src = qkv_dram.rearrange("(b i) (a g c) -> b i a g c", i=SEQ, a=3, g=2)[:, :, :, half, :]
                    sp.dma_start(lanes[half * BATCH:(half + 1) * BATCH, :, :, :], src).then_inc(lanes_in, 16)
                sp.wait_ge(out_lanes, 1)
                for half in range(2):
                    dst = attn_dram.rearrange("(b i) (g c) -> b i g c", i=SEQ, g=2)[:, :, half, :]
                    sp.dma_start(dst, attn[half * BATCH:(half + 1) * BATCH, :, :]).then_inc(o_out, 16)
                sp.wait_ge(o_out, 32)
                sp.dma_start(attn_tok[:, :, :], attn_dram.rearrange("(t p) c -> p t c", p=P)).then_inc(o_in, 16)

            @block.tensor
            def _(pe):
                for t in range(TT):
                    mm = pe.transpose(pt[:, 0, t * P:(t + 1) * P], h6[:, t * P:(t + 1) * P], ident[:, :])
                mm.then_inc(turned, 1)
                pe.wait_ge(to_pe, 1)
                for t in range(TT):
                    mm = pe.transpose(pt[:, 1, t * P:(t + 1) * P], norm6[:, t, :], ident[:, :])
                mm.then_inc(turned, 1)
                pe.wait_ge(to_pe, 2)
                pe.wait_ge(a_in, 16 * LOADS)
                for t in range(TT):
                    mm = pe.matmul(pt[:, 2 + t // 4, (t % 4 // 2) * 512 + (t % 2) * D:(t % 4 // 2) * 512 + (t % 2) * D + D],
                                   norm6t[:, t * P:(t + 1) * P], proj_w[:, :], start=True, stop=True)
                mm.then_inc(projected, 1)
                pe.wait_ge(to_pe, 3)
                turn(pe, pt, xhat, ident, turned)
                pe.wait_ge(to_pe, 4)
                for t in range(TT):
                    if t >= 2:
                        pe.wait_ge(qkv_copied, t - 1)
                    for n in range(2):
                        for k in range(KD):
                            mm = pe.matmul(pt[:, 2 + t % 2, n * 512:n * 512 + 288], xhat_t[:, k, t * P:(t + 1) * P],
                                           qkv_w[:, k, n * 288:(n + 1) * 288], start=(k == 0), stop=(k == KD - 1))
                    mm.then_inc(qkv_ready, 1)
                pe.wait_ge(o_in, 16)
                turn(pe, pt, attn_tok, ident, turned)
                pe.wait_ge(to_pe, 5)
                for t in range(TT):
                    for k in range(KD):
                        mm = pe.matmul(pt[:, 2 + t // 4, (t % 4 // 2) * 512 + (t % 2) * D:(t % 4 // 2) * 512 + (t % 2) * D + D],
                                       xhat_t[:, k, t * P:(t + 1) * P], out_w[:, k, :], start=(k == 0), stop=(k == KD - 1))
                mm.then_inc(projected, 1)

            @block.gpsimd
            def _(pool):
                pool.memset(eye[:, :, :], 0.0).then_inc(eye_ready, 1)
                pool.wait_ge(eye_ready, 1)
                pool.affine_select(out=eye[:, :, :], in_=eye[:, :, :], compare_op=ALU.not_equal, fill=1.0, base=0,
                                   pattern=[[1, R], [-1, R]], channel_multiplier=0).then_inc(eye_ready, 1)
                pool.memset(smat[:, :, 0, :], ROOT / LANDMARKS).then_inc(eye_ready, 1)
                pool.wait_ge(eye_ready, 3)
                pool.memset(smat[:, :, 0, 0], PADS / LANDMARKS).then_inc(eye_ready, 1)
                pool.wait_ge(peaks, 2)
                pool.partition_all_reduce(all_norms[:, :], norms[:, :], P, bass.bass_isa.ReduceOp.max).then_inc(peaks, 1)

            @block.scalar
            def _(act):
                for t in range(TT):
                    act.wait_ge(qkv_ready, t + 1)
                    act.copy(qkv[:, t, :].rearrange("p (n c) -> p n c", n=2),
                             pt[:, 2 + t % 2, :].rearrange("p (n c) -> p n c", n=2)[:, :, 0:288]).then_inc(qkv_copied, 1)
                act.wait_ge(scores_ready, 1)
                act.activation(scores[:, :, :, :], scores[:, :, :, :], ACT.Exp, scale=DH ** -0.5).then_inc(exp_done, 1)
                act.activation(epad[:, :, :], peak[:, :, :], ACT.Exp, scale=-(DH ** -0.5)).then_inc(exp_done, 1)

                def mirror(m, before):
                    for i in range(R - 1):
                        act.wait_ge(row_done, before + i + 1)
                        act.copy(m[:, :, i + 1:R, i], m[:, :, i, i + 1:R]).then_inc(mirrored, 1)

                mirror(e2, 0)
                with act.Fori(0, PINV_ITERS) as n:
                    mirror(e2, (R - 1) + ROWS_EACH * n)
                    mirror(e1, 2 * (R - 1) + ROWS_EACH * n)

            @block.vector
            def _(dve):
                steps = Rows(dve, a_steps)
                tile = lambda x: [x[:, t, :] for t in range(TT)]
                small = (stats, mv, y6[:, :], t6[:, :], u6[:, :])
                dve.wait_ge(turned, 1)
                normalise(nc, steps, [pt[:, 0, t * P:(t + 1) * P] for t in range(TT)], tile(norm6), *small)
                nc.vector.tensor_copy(t6[:, :], y6[:, :]).then_inc(to_pe, 1)
                dve.wait_ge(turned, 2)
                nc.vector.tensor_scalar(norm6t[:, :], pt[:, 1, 0:TOK], lnp[:, 14:15], lnp[:, 15:16],
                                        ALU.mult, ALU.add).then_inc(to_pe, 1)
                dve.wait_ge(projected, 1)
                dve.wait_ge(a_in, 16 * LOADS)

                def projected_tiles():
                    for c in range(TT // 2):
                        bank = pt[:, 2 + c // 2, (c % 2) * 512:(c % 2) * 512 + 2 * D]
                        yield hidden[:, 2 * c:2 * c + 2, :], bank.rearrange("p (t n) -> p t n", t=2)

                for out, bank in projected_tiles():
                    steps.done(nc.vector.tensor_tensor(out, bank, proj_b[:, :].unsqueeze(1).broadcast_to([P, 2, D]), ALU.add))
                steps.settle()
                normalise(nc, steps, tile(hidden), tile(xhat), *small)
                nc.vector.tensor_copy(t6[:, :], y6[:, :]).then_inc(to_pe, 1)
                dve.wait_ge(turned, 3)
                nc.vector.tensor_copy(xhat_t[:, :, :], pt[0:96, 0:2, 0:TOK]).then_inc(to_pe, 1)
                steps.done(nc.vector.tensor_tensor(hidden[:, :, :], hidden[:, :, :], out_b[:, :].unsqueeze(1)
                                                   .broadcast_to([P, TT, D]), ALU.add))

                def rows(n, first, second, out):
                    marks = []
                    for i in range(n + 1):
                        if i < n:
                            a, b = first(i), second(i)
                            size = 1
                            for x in a.shape[1:]:
                                size *= x
                            at = rowt[:, i % 2, 0:size].rearrange("p (a b c) -> p a b c", a=a.shape[1], b=a.shape[2])
                            if i >= 2:
                                steps.until(marks[i - 2][1])
                            steps.done(nc.vector.tensor_tensor(at, a, b, ALU.mult))
                            marks.append([steps.mark(), None, at])
                        if i >= 1:
                            m = marks[i - 1]
                            steps.until(m[0])
                            steps.done(nc.vector.tensor_reduce(out(i - 1), m[2], AX.X, ALU.add))
                            m[1] = steps.mark()
                    steps.settle()

                dve.wait_ge(lanes_in, 32)
                shape = [P, HL, SEQ, DH]
                per_head = lambda x: x.rearrange("p j (h d) -> p h j d", d=DH)
                rows(SEQ, lambda i: q_l[:, i, :].rearrange("p (h d) -> p h d", d=DH).unsqueeze(2).broadcast_to(shape),
                     lambda i: per_head(k_l), lambda i: scores[:, :, i, :])
                steps.done(nc.vector.tensor_reduce(peak[:, :, :], scores[:, :, :, :], AX.X, ALU.max))
                steps.settle()
                steps.done(nc.vector.tensor_scalar(peak[:, :, :], peak[:, :, :], 0.0, None, ALU.max))
                steps.settle()
                square = [P, HL, SEQ, SEQ]
                nc.vector.tensor_tensor(scores[:, :, :, :], scores[:, :, :, :], peak[:, :, :].unsqueeze(3).broadcast_to(square),
                                        ALU.subtract).then_inc(scores_ready, 1)
                dve.wait_ge(exp_done, 2)
                steps.done(nc.vector.tensor_reduce(den[:, :, :], scores[:, :, :, :], AX.X, ALU.add))
                steps.settle()
                flat = lambda x: x[:, :, :].rearrange("p h i -> p (h i)")
                steps.done(nc.vector.scalar_tensor_tensor(out=flat(den), in0=flat(epad), scalar=float(PADS), in1=flat(den),
                                                          op0=ALU.mult, op1=ALU.add))
                steps.settle()
                steps.done(nc.vector.reciprocal(flat(rden), flat(den)))
                steps.settle()
                dve.wait_ge(eye_ready, 4)
                real = smat[:, :, 1:R, 1:R]
                steps.done(nc.vector.tensor_tensor(real, scores[:, :, :, :], rden[:, :, :].unsqueeze(3).broadcast_to(square), ALU.mult))
                steps.done(nc.vector.scalar_tensor_tensor(out=smat[:, :, 1:R, 0], in0=epad[:, :, :], scalar=ROOT, in1=rden[:, :, :],
                                                          op0=ALU.mult, op1=ALU.mult))
                steps.settle()
                steps.done(nc.vector.tensor_reduce(den[:, :, :], real, AX.X, ALU.add))
                steps.done(nc.vector.tensor_reduce(peak[:, :, :], real.rearrange("p h i j -> p h j i"), AX.X, ALU.add))
                steps.done(nc.vector.tensor_reduce(padsum[:, :], smat[:, :, 1:R, 0], AX.X, ALU.add))
                steps.settle()
                steps.done(nc.vector.scalar_tensor_tensor(out=den[:, :, :], in0=smat[:, :, 1:R, 0], scalar=ROOT, in1=den[:, :, :],
                                                          op0=ALU.mult, op1=ALU.add))
                steps.done(nc.vector.tensor_scalar(padsum[:, :], padsum[:, :], 1.0 / ROOT, None, ALU.mult))
                steps.settle()
                steps.done(nc.vector.tensor_reduce(norms[:, 0:1], flat(den), AX.X, ALU.max))
                steps.done(nc.vector.tensor_reduce(norms[:, 1:2], flat(peak), AX.X, ALU.max))
                steps.done(nc.vector.tensor_reduce(scale[:, 0:1], padsum[:, :], AX.X, ALU.max))
                steps.settle()
                nc.vector.tensor_scalar(norms[:, 0:1], norms[:, 0:1], 1.0, None, ALU.max).then_inc(peaks, 1)
                nc.vector.tensor_scalar(norms[:, 1:2], norms[:, 1:2], scale[:, 0:1], PADS / LANDMARKS,
                                        ALU.max, ALU.add).then_inc(peaks, 1)
                wide = [P, HL, DH, SEQ]
                v_t = v_l.rearrange("p j (h d) -> p h d j", d=DH)
                rows(R, lambda i: smat[:, :, i, 1:R].unsqueeze(2).broadcast_to(wide), lambda i: v_t, lambda i: wv[:, :, i, :])

                def product(a, b, out, before):
                    lines = lambda i: [P, HL, R - i, R]
                    marks = []
                    for i in range(R + 1):
                        if i < R:
                            at = rowt[:, i % 2, 0:HL * (R - i) * R].rearrange("p (a b c) -> p a b c", a=HL, b=R - i)
                            if i >= 2:
                                dve.wait_ge(row_done, before + i - 1)
                            steps.done(nc.vector.tensor_tensor(at, a[:, :, i, :].unsqueeze(2).broadcast_to(lines(i)),
                                                               b[:, :, i:R, :], ALU.mult))
                            marks.append((steps.mark(), at))
                        if i >= 1:
                            steps.until(marks[i - 1][0])
                            ins = nc.vector.tensor_reduce(out[:, :, i - 1, i - 1:R], marks[i - 1][1], AX.X, ALU.add)
                            if i - 1 < R - 1:
                                ins.then_inc(row_done, 1)
                            else:
                                steps.done(ins)
                    steps.settle()
                    dve.wait_ge(mirrored, before + R - 1)

                lined = lambda x: x[:, :, :, :].rearrange("p h i j -> p (h i j)")
                product(smat, smat, e2, 0)
                dve.wait_ge(peaks, 3)
                steps.done(nc.vector.tensor_tensor(scale[:, 0:1], all_norms[:, 0:1], all_norms[:, 1:2], ALU.mult))
                steps.settle()
                steps.done(nc.vector.reciprocal(scale[:, 1:2], scale[:, 0:1]))
                steps.settle()
                steps.done(nc.vector.tensor_scalar(scale[:, 1:2], scale[:, 1:2], -1.0, None, ALU.mult))
                steps.settle()
                heads = lambda x: x[:, :, :, :].rearrange("p h i j -> p h (i j)")
                steps.done(nc.vector.scalar_tensor_tensor(
                    out=heads(e1), in0=heads(e2), scalar=scale[:, 1:2],
                    in1=eye[:, :, :].rearrange("p i j -> p (i j)").unsqueeze(1).broadcast_to([P, HL, R * R]),
                    op0=ALU.mult, op1=ALU.add))
                steps.settle()
                start = steps.n
                STEPS_EACH = 2 * (R + 1) + 2
                with dve.Fori(0, PINV_ITERS) as n:
                    steps.at(start + STEPS_EACH * n)
                    product(e1, e1, e2, (R - 1) + ROWS_EACH * n)
                    steps.done(nc.vector.scalar_tensor_tensor(out=lined(c4), in0=lined(e1), scalar=3.0, in1=lined(e2),
                                                              op0=ALU.mult, op1=ALU.add))
                    steps.settle()
                    steps.done(nc.vector.tensor_scalar(lined(c4), lined(c4), 0.25, None, ALU.mult))
                    steps.settle()
                    product(e2, c4, e1, 2 * (R - 1) + ROWS_EACH * n)
                    assert steps.n == STEPS_EACH
                steps.at(start + STEPS_EACH * PINV_ITERS)
                deep = [P, HL, DH, R]
                w_t = wv[:, :, :, :].rearrange("p h k d -> p h d k")
                rows(SEQ, lambda i: e1[:, :, i + 1, :].unsqueeze(2).broadcast_to(deep), lambda i: w_t,
                     lambda i: attn[:, i, :].rearrange("p (h d) -> p h d", d=DH))
                nc.vector.tensor_tensor(attn[:, :, :].rearrange("p i (h d) -> p i h d", d=DH),
                                        wv[:, :, 1:R, :].rearrange("p h i d -> p i h d"),
                                        attn[:, :, :].rearrange("p i (h d) -> p i h d", d=DH), ALU.subtract).then_inc(out_lanes, 1)
                dve.wait_ge(turned, 4)
                nc.vector.tensor_copy(xhat_t[:, :, :], pt[0:96, 0:2, 0:TOK]).then_inc(to_pe, 1)
                dve.wait_ge(projected, 2)
                for out, bank in projected_tiles():
                    steps.done(nc.vector.tensor_tensor(out, out, bank, ALU.add))
                steps.settle()


def experts(nc, io, res, top):
    sem = lambda n: top.enter_context(nc.semaphore(n))
    f_in = sem("f_in")
    f_steps = sem("f_steps")
    f_pe = sem("f_pe")
    f_turned = sem("f_turned")
    routed = sem("routed")
    logits_ready = sem("logits_ready")
    f_exp = sem("f_exp")
    iota_ready = sem("iota_ready")
    up_ready = sem("up_ready")
    silu_done = sem("silu_done")
    act_ready = sem("act_ready")
    down_ready = sem("down_ready")
    summed = sem("summed")
    out_done = sem("out_done")
    N_HID = EXPERTS * HID + SHID
    MT = N_HID // P
    ROUTED_T = EXPERTS * HID // P
    ident, hidden = res["ident"], res["hidden"]
    gate_w, up_w, down_w, router_w, gate_b = (res[k] for k in ("gate_w", "up_w", "down_w", "router_w", "gate_b"))

    def parts_of(unit):
        if unit == 0:
            return [(ROUTED_T + i, 0, P) for i in range(SHID // P)]
        a, b = (unit - 1) * HID, unit * HID
        out = []
        while a < b:
            end = min(b, (a // P + 1) * P)
            out.append((a // P, a % P, a % P + end - a))
            a = end
        return out

    with ExitStack() as ctx:
        sb = lambda n, s, d=F32: ctx.enter_context(nc.sbuf_tensor(n, s, d))
        pf = ctx.enter_context(nc.psum_tensor("pf", [P, 4, 1024], F32))
        stats, mv = sb("f_stats", [P, TT, 6]), sb("f_mv", [P, TT, 2])
        y6, t6, u6 = sb("f_y6", [P, TT]), sb("f_t6", [P, TT]), sb("f_u6", [P, TT])
        xhat = sb("f_xhat", [P, TT, D])
        xhat_t = sb("f_xhat_t", [96, KD, TOK])
        NE = EXPERTS + 1
        logit, prob = sb("logit", [P, TT, NE]), sb("prob", [P, TT, NE])
        top = sb("top", [P, TT, 8])
        where = sb("where", [P, TT, 8], U32)
        wheref = sb("wheref", [P, TT, 8])
        iota_i, iota_f = sb("iota_i", [P, 8], I32), sb("iota_f", [P, 8])
        one, two = sb("one", [P, TT, 8]), sb("two", [P, TT, 8])
        peak, total = sb("f_peak", [P, TT]), sb("f_total", [P, TT])
        mix = sb("mix", [P, TT, NE])
        silu = sb("silu", [P, 2, TOK])
        acts = sb("acts", [P, MT, TOK])

        with nc.Block() as block:

            @block.sync
            def _(sp):
                for t in range(TT):
                    sp.wait_ge(summed, TT * EXPERTS + t + 1)
                    sp.dma_start(io["out"][t * P:(t + 1) * P, :], hidden[:, t, :]).then_inc(out_done, 16)
                sp.wait_ge(out_done, 16 * TT)

            @block.gpsimd
            def _(pool):
                pool.iota(iota_i[:, :], pattern=[[1, 8]], base=0, channel_multiplier=0).then_inc(iota_ready, 1)

            @block.tensor
            def _(pe):
                pe.wait_ge(f_pe, 1)
                turn(pe, pf, xhat, ident, f_turned)
                pe.wait_ge(f_pe, 2)
                pe.wait_ge(res["f_in"], 16 * res["f_loads"])
                for t in range(TT):
                    for k in range(KD):
                        mm = pe.matmul(pf[:, 2, t * NE:(t + 1) * NE], xhat_t[:, k, t * P:(t + 1) * P], router_w[:, k, :],
                                       start=(k == 0), stop=(k == KD - 1))
                mm.then_inc(routed, 1)
                pe.wait_ge(logits_ready, 1)
                for m in range(MT):
                    if m >= 2:
                        pe.wait_ge(act_ready, m - 1)
                    for g, w in ((0, gate_w), (1, up_w)):
                        for n in range(2):
                            for k in range(KD):
                                mm = pe.matmul(pf[:, 2 * (m % 2) + g, n * 512:n * 512 + TOK // 2], w[:, k, m * P:(m + 1) * P],
                                               xhat_t[:, k, n * TOK // 2:(n + 1) * TOK // 2],
                                               start=(k == 0), stop=(k == KD - 1))
                    mm.then_inc(up_ready, 1)
                for unit in range(NE):
                    for t in range(TT):
                        n = unit * TT + t
                        if unit == 0:
                            pe.wait_ge(act_ready, MT)
                        if n >= 8:
                            pe.wait_ge(summed, n - 7)
                        rows = parts_of(unit)
                        for j, (tile, a, b) in enumerate(rows):
                            mm = pe.matmul(pf[:, n % 8 // 2, (n % 2) * 512:(n % 2) * 512 + D], acts[a:b, tile, t * P:(t + 1) * P],
                                           down_w[a:b, tile, :], start=(j == 0), stop=(j == len(rows) - 1))
                        mm.then_inc(down_ready, 1)

            @block.scalar
            def _(act):
                act.wait_ge(logits_ready, 1)
                act.activation(prob[:, :, :], logit[:, :, :], ACT.Exp).then_inc(f_exp, 1)
                for m in range(MT):
                    act.wait_ge(up_ready, m + 1)
                    if m >= 2:
                        act.wait_ge(act_ready, m - 1)
                    act.activation(silu[:, m % 2, :].rearrange("p (n c) -> p n c", n=2),
                                   pf[:, 2 * (m % 2), :].rearrange("p (n c) -> p n c", n=2)[:, :, 0:TOK // 2],
                                   ACT.Silu).then_inc(silu_done, 1)

            @block.vector
            def _(dve):
                steps = Steps(dve, f_steps)
                tile = lambda x: [x[:, t, :] for t in range(TT)]
                normalise(nc, steps, tile(hidden), tile(xhat), stats, mv, y6[:, :], t6[:, :], u6[:, :])
                nc.vector.tensor_copy(t6[:, :], y6[:, :]).then_inc(f_pe, 1)
                dve.wait_ge(f_turned, 1)
                nc.vector.tensor_copy(xhat_t[:, :, :], pf[0:96, 0:2, 0:TOK]).then_inc(f_pe, 1)
                dve.wait_ge(res["f_in"], 16 * res["f_loads"])
                dve.wait_ge(routed, 1)
                raw = pf[:, 2, 0:TT * NE].rearrange("p (t e) -> p t e", t=TT)
                over = lambda x, n=8: x.unsqueeze(2).broadcast_to([P, TT, n])
                steps.done(nc.vector.tensor_reduce(peak[:, :], raw[:, :, 0:EXPERTS], AX.X, ALU.max))
                steps.settle()
                steps.done(nc.vector.tensor_tensor(logit[:, :, 0:EXPERTS], raw[:, :, 0:EXPERTS], over(peak[:, :]), ALU.subtract))
                nc.vector.tensor_scalar(logit[:, :, EXPERTS], raw[:, :, EXPERTS], gate_b[:, 0:1], -1.0, ALU.add, ALU.mult)\
                    .then_inc(logits_ready, 1)
                dve.wait_ge(f_exp, 1)
                steps.done(nc.vector.tensor_reduce(total[:, :], prob[:, :, 0:EXPERTS], AX.X, ALU.add))
                steps.done(nc.vector.tensor_scalar(peak[:, :], prob[:, :, EXPERTS], 1.0, None, ALU.add))
                steps.settle()
                steps.done(nc.vector.reciprocal(total[:, :], total[:, :]))
                steps.done(nc.vector.reciprocal(mix[:, :, 0], peak[:, :]))
                steps.settle()
                steps.done(nc.vector.tensor_tensor(prob[:, :, 0:EXPERTS], prob[:, :, 0:EXPERTS], over(total[:, :]), ALU.mult))
                steps.settle()
                for t in range(TT):
                    steps.done(nc.vector.max(top[:, t, :], prob[:, t, 0:EXPERTS]))
                steps.settle()
                for t in range(TT):
                    steps.done(nc.vector.max_index(where[:, t, :], top[:, t, :], prob[:, t, 0:EXPERTS]))
                steps.done(nc.vector.tensor_tensor(total[:, :], top[:, :, 0], top[:, :, 1], ALU.add))
                dve.wait_ge(iota_ready, 1)
                steps.done(nc.vector.tensor_copy(iota_f[:, :], iota_i[:, :]))
                steps.settle()
                steps.done(nc.vector.tensor_copy(wheref[:, :, :], where[:, :, :]))
                steps.done(nc.vector.reciprocal(peak[:, :], total[:, :]))
                steps.settle()
                steps.done(nc.vector.tensor_tensor(top[:, :, :], top[:, :, :], over(peak[:, :]), ALU.mult))
                each = iota_f[:, :].unsqueeze(1).broadcast_to([P, TT, 8])
                steps.done(nc.vector.tensor_tensor(one[:, :, :], each, over(wheref[:, :, 0]), ALU.is_equal))
                steps.done(nc.vector.tensor_tensor(two[:, :, :], each, over(wheref[:, :, 1]), ALU.is_equal))
                steps.done(nc.vector.tensor_scalar(total[:, :], mix[:, :, 0], -1.0, 1.0, ALU.mult, ALU.add))
                steps.settle()
                steps.done(nc.vector.tensor_tensor(one[:, :, :], one[:, :, :], over(top[:, :, 0]), ALU.mult))
                steps.done(nc.vector.tensor_tensor(two[:, :, :], two[:, :, :], over(top[:, :, 1]), ALU.mult))
                steps.settle()
                steps.done(nc.vector.tensor_tensor(one[:, :, :], one[:, :, :], two[:, :, :], ALU.add))
                steps.settle()
                steps.done(nc.vector.tensor_tensor(mix[:, :, 1:NE], one[:, :, :], over(total[:, :]), ALU.mult))
                for m in range(MT):
                    dve.wait_ge(silu_done, m + 1)
                    two_halves = lambda x: x.rearrange("p (n c) -> p n c", n=2)
                    nc.vector.tensor_tensor(two_halves(acts[:, m, :]), two_halves(silu[:, m % 2, :]),
                                            two_halves(pf[:, 2 * (m % 2) + 1, :])[:, :, 0:TOK // 2], ALU.mult).then_inc(act_ready, 1)
                steps.settle()
                for unit in range(NE):
                    for t in range(TT):
                        n = unit * TT + t
                        dve.wait_ge(down_ready, n + 1)
                        if unit:
                            dve.wait_ge(summed, n - TT + 1)
                        nc.vector.scalar_tensor_tensor(out=hidden[:, t, :], in0=pf[:, n % 8 // 2, (n % 2) * 512:(n % 2) * 512 + D],
                                                       scalar=mix[:, t, unit:unit + 1], in1=hidden[:, t, :],
                                                       op0=ALU.mult, op1=ALU.add).then_inc(summed, 1)


def shared_tensors(nc, ctx):
    sb = lambda n, s, d=F32: ctx.enter_context(nc.sbuf_tensor(n, s, d))
    return {"ident": sb("ident", [P, P]), "h6": sb("h6", [P, TOK]), "lnp": sb("lnp", [P, 16]),
            "hidden": sb("hidden", [P, TT, D])}


def expert_weights(nc, io, res, ctx):
    sb = lambda n, s, d=F32: ctx.enter_context(nc.sbuf_tensor(n, s, d))
    N = EXPERTS * HID + SHID
    res.update(gate_w=sb("gate_w", [96, KD, N]), up_w=sb("up_w", [96, KD, N]), down_w=sb("down_w", [P, N // P, D]),
               router_w=sb("router_w", [96, KD, EXPERTS + 1]), gate_b=sb("gate_b", [P, 1]),
               f_in=ctx.enter_context(nc.semaphore("experts_in")), f_loads=5)
    with nc.Block() as block:

        @block.sync
        def _(sp):
            halves = lambda x: x.rearrange("(k p) n -> p k n", k=KD)
            sp.dma_start(res["router_w"][:, :, :], halves(io["router_w"])).then_inc(res["f_in"], 16)
            sp.dma_start(res["gate_b"][:, :], io["gate_b"].partition_broadcast(P)).then_inc(res["f_in"], 16)
            sp.dma_start(res["gate_w"][:, :, :], halves(io["gate_w"])).then_inc(res["f_in"], 16)
            sp.dma_start(res["up_w"][:, :, :], halves(io["up_w"])).then_inc(res["f_in"], 16)
            sp.dma_start(res["down_w"][:, :, :], io["down_w"].rearrange("(t p) n -> p t n", p=P)).then_inc(res["f_in"], 16)


def audio_tower(nc, io):
    with ExitStack() as top:
        res = shared_tensors(nc, top)
        conv_tower(nc, io, res, top)
        expert_weights(nc, io, res, top)
        attention(nc, io, res, top)
        experts(nc, io, res, top)


def kernel(**a):
    import concourse.bacc as bacc
    from concourse.bass_utils import run_bass_kernel_spmd

    g = {k: np.asarray(v) for k, v in a.items()}
    conv = [g[f"L0_tok_conv_w{i}"] for i in range(7)]
    names = [(f"L0_tok_ln_g{i}", f"L0_tok_ln_b{i}") for i in range(7)] + [("L0_tok_fln_g", "L0_tok_fln_b")]
    by_hidden = lambda x: x.transpose(1, 0, 2).reshape(D, EXPERTS * HID)
    arrays = {
        "x": np.pad(g["x"], ((0, 0), (0, STRIDE0))),
        "w0": conv[0][:, 0, :],
        "w": np.concatenate([c.transpose(1, 2, 0) for c in conv[1:]], 1),
        "lnp": np.stack([g[n] for pair in names for n in pair], 1),
        "proj_w": g["L0_tok_proj_w"],
        "proj_b": g["L0_tok_proj_b"],
        "qkv_w": g["L0_attn_w_qkv"].T,
        "out_w": g["L0_attn_w_proj"].T,
        "out_b": g["L0_attn_b_proj"],
        "router_w": np.concatenate([g["L0_ffn_router_w"], g["L0_ffn_sg_w"]], 1),
        "gate_b": g["L0_ffn_sg_b"],
        "gate_w": np.concatenate([by_hidden(g["L0_ffn_w_gate"]), g["L0_ffn_ws_gate"]], 1),
        "up_w": np.concatenate([by_hidden(g["L0_ffn_w_up"]), g["L0_ffn_ws_up"]], 1),
        "down_w": np.concatenate([g["L0_ffn_w_down"].reshape(EXPERTS * HID, D), g["L0_ffn_ws_down"]], 0),
    }
    nc = bacc.Bacc("TRN2", target_bir_lowering=False, num_devices=1)
    io, sent = {}, {}
    for name, x in arrays.items():
        x = np.ascontiguousarray(x)
        sent[f"in_{name}"] = x
        io[name] = nc.dram_tensor(f"in_{name}", x.shape, mybir.dt.from_np(x.dtype), kind="ExternalInput").ap()
    io["out"] = nc.dram_tensor("out_tokens", (TOK, D), F32, kind="ExternalOutput").ap()
    audio_tower(nc, io)
    r = run_bass_kernel_spmd(nc, [sent], core_ids=[0])
    return r.results[0]["out_tokens"].reshape(BATCH, SEQ, D)
```

```python
from contextlib import ExitStack
from math import sqrt

import numpy as np
import concourse.bass as bass
from concourse import mybir

ALU = mybir.AluOpType
ACT = mybir.ActivationFunctionType
F32 = mybir.dt.float32
BF16 = mybir.dt.bfloat16
I32 = mybir.dt.int32
U32 = mybir.dt.uint32
AX = mybir.AxisListType

P = 128
BATCH, SAMPLES = 64, 4000
CH = 128
K0, STRIDE0 = 10, 5
CENTRE_EPS = 1e-5
RSQRT_GUESS = float(0x5F3759DF)

GROUP = 8
ROUND = 2 * GROUP
ROUNDS = BATCH // ROUND
AHEAD = GROUP + 1

POS0, ROW0 = 800, 802
SLICES = 8
SL = POS0 // SLICES
XROW = SAMPLES + STRIDE0
PARTS = 3


class Layer:

    def __init__(self, n, taps, pos, row, per_chunk, chunks, slot_chunks):
        self.n, self.taps, self.pos, self.row = n, taps, pos, row
        self.per_chunk = per_chunk
        self.chunks = chunks
        self.cols = per_chunk * pos
        self.w = self.cols // 4
        self.first_tap = slot_chunks


L1 = Layer(1, 3, 400, 402, 1, 8, 0)
L2 = Layer(2, 3, 200, 202, 2, 4, 3)
L3 = Layer(3, 3, 100, 102, 4, 2, 6)
L4 = Layer(4, 3, 50, 50, 8, 4, 9)
L5 = Layer(5, 2, 24, 24, 16, 2, 12)
L6 = Layer(6, 2, 12, 12, 16, 2, 14)
LAYERS = {x.n: x for x in (L1, L2, L3, L4, L5, L6)}
TAPS = 16

TOK = BATCH * L6.pos
TT = TOK // P
SEQ = L6.pos
D, HEADS, DH = 192, 12, 16
KD = D // 96
LANDMARKS = 64
PADS = LANDMARKS - SEQ
PINV_ITERS = 6
EXPERTS, HID, SHID = 8, 192, 768


class Steps:

    def __init__(self, eng, sem):
        self.eng, self.sem, self.base, self.n = eng, sem, 0, 0

    def done(self, ins):
        ins.then_inc(self.sem, 1)
        self.n += 1

    def settle(self):
        self.eng.wait_ge(self.sem, self.base + self.n)

    def at(self, base):
        self.base, self.n = base, 0


def newton_rsqrt(nc, steps, v, y, t, u):
    steps.done(nc.vector.tensor_scalar(y.bitcast(I32), v.bitcast(I32), -0.5, RSQRT_GUESS, ALU.mult, ALU.add))
    for _ in range(3):
        steps.settle()
        steps.done(nc.vector.tensor_tensor(t, v, y, ALU.mult))
        steps.settle()
        steps.done(nc.vector.scalar_tensor_tensor(out=u, in0=t, scalar=-0.5, in1=y, op0=ALU.mult, op1=ALU.mult))
        steps.settle()
        steps.done(nc.vector.scalar_tensor_tensor(out=y, in0=u, scalar=1.5, in1=y, op0=ALU.add, op1=ALU.mult))
    steps.settle()



def round_plan(last):
    order = []

    def conv(l, s, p, *between):
        order.append(("half", l, s, p))
        for step in between:
            step()
        order.append(("conv", l, s, p))

    def step(what, l, s, p=0):
        return lambda: order.append((what, l, s, p))

    var = lambda l, s, p: step("var", l, s, p)
    norm = lambda l, s: step("norm", l, s)
    rows = lambda l, s: step("rows", l, s)

    def scale(l, s, *chunks):
        def add():
            for c in chunks:
                order.append(("scale", l, s, c))
                if c % 2:
                    order.append(("gelu", l, s, c // 2))
        return add

    def first(batch):
        return step("first", 0, batch // GROUP, batch % GROUP)

    def ahead(*batches):
        def add():
            for b in batches:
                if not last:
                    order.append(("first", 1, b // GROUP, b % GROUP))
        return add

    def prep(a, b):
        for k in range(a, b):
            if not last:
                order.append(("prep", 0, 0, k))

    conv(1, 0, 0, first(9))
    prep(0, 3)
    conv(1, 0, 1, first(10), var(1, 0, 0))
    prep(3, 8)
    conv(1, 0, 2, first(11), var(1, 0, 1))
    prep(8, 11)
    conv(1, 0, 3, first(12), var(1, 0, 2))
    prep(11, 12)
    conv(1, 1, 0, first(13), var(1, 0, 3), norm(1, 0))
    prep(12, 13)
    conv(1, 1, 1, first(14), rows(1, 0), scale(1, 0, 0, 1), var(1, 1, 0))
    scale(1, 0, 2, 3)()
    prep(13, 14)
    conv(1, 1, 2, first(15), var(1, 1, 1), scale(1, 0, 4, 5))
    scale(1, 0, 6, 7)()
    conv(1, 1, 3, var(1, 1, 2))
    conv(2, 0, 0, var(1, 1, 3), norm(1, 1))
    conv(2, 0, 1, var(2, 0, 0), rows(1, 1), scale(1, 1, 0, 1))
    scale(1, 1, 2, 3)()
    conv(2, 1, 0, ahead(0), scale(1, 1, 4, 5), var(2, 0, 1), norm(2, 0))
    scale(1, 1, 6, 7)()
    conv(2, 1, 1, ahead(1), rows(2, 0), scale(2, 0, 0, 1), var(2, 1, 0))
    scale(2, 0, 2, 3)()
    conv(3, 0, 0, ahead(2), var(2, 1, 1), norm(2, 1))
    ahead(3, 4)()
    rows(2, 1)()
    scale(2, 1, 0, 1)()
    var(3, 0, 0)()
    scale(2, 1, 2, 3)()
    norm(3, 0)()
    conv(3, 1, 0, ahead(5), rows(3, 0), scale(3, 0, 0, 1), ahead(6))
    if not last:
        ahead(7)()
        var(3, 1, 0)()
        norm(3, 1)()
        ahead(8)()
        rows(3, 1)()
        scale(3, 1, 0, 1)()
        return counted(order)
    conv(4, 0, 0, var(3, 1, 0), norm(3, 1))
    conv(4, 0, 1, var(4, 0, 0), rows(3, 1), scale(3, 1, 0, 1))
    conv(4, 1, 0, var(4, 0, 1), norm(4, 0))
    conv(4, 1, 1, rows(4, 0), scale(4, 0, 0, 1), var(4, 1, 0))
    scale(4, 0, 2, 3)()
    conv(5, 0, 0, var(4, 1, 1), norm(4, 1))
    rows(4, 1)()
    scale(4, 1, 0, 1)()
    var(5, 0, 0)()
    scale(4, 1, 2, 3)()
    norm(5, 0)()
    conv(5, 1, 0, rows(5, 0), scale(5, 0, 0, 1))
    conv(6, 0, 0, var(5, 1, 0), norm(5, 1))
    rows(5, 1)()
    scale(5, 1, 0, 1)()
    var(6, 0, 0)()
    norm(6, 0)()
    conv(6, 1, 0, rows(6, 0), scale(6, 0, 0, 1))
    var(6, 1, 0)()
    norm(6, 1)()
    rows(6, 1)()
    scale(6, 1, 0, 1)()
    return counted(order)


def counted(order):
    n = dict.fromkeys(("pair", "half", "conv", "var", "norm", "rows", "scale", "gelu", "first", "prep"), 0)
    out, bank, held = [], 0, None
    users = [("first", -2), ("first", -1)]
    for what, l, s, p in order:
        step = dict(n)
        if what in ("half", "first"):
            step["bank"], step["before"] = bank, users[bank]
            if what == "first":
                users[bank] = ("first", n["pair"])
            else:
                users[bank] = ("conv", n["conv"])
                held = bank
            if held is None or what == "half":
                bank = 1 - bank
        elif what == "conv":
            step["bank"], held = held, None
        out.append((what, l, s, p, step))
        n[what] += 1
        n["pair"] += what in ("conv", "first")
    assert bank == 0 or not n["prep"]
    return out, n


class Origin:

    def __init__(self, rounds, per):
        self.pair = AHEAD + per["pair"] * rounds
        self.conv, self.sets = per["conv"] * rounds, per["norm"] * rounds
        self.scale, self.gelu = per["scale"] * rounds, per["gelu"] * rounds


def number_of(plan, what, layer, slot, p, kind):
    return next(n[kind] for a, b, c, d, n in plan if (a, b, c, d) == (what, layer, slot, p))


def gelus_before(plan, layer, slot):
    return {p: n["gelu"] for what, l, s, p, n in plan if (what, l, s) == ("gelu", layer, slot)}


def conv_tower(nc, io, res, top):
    body, per = round_plan(False)
    last, _ = round_plan(True)
    sem = lambda n: top.enter_context(nc.semaphore(n))
    x_in = sem("x_in")
    w_in = sem("w_in")
    s_const = sem("s_const")
    s_w0 = sem("s_w0")
    w0_in = sem("w0_in")
    weights_ready = sem("weights_ready")
    parts_ready = sem("parts_ready")
    parts_out = sem("parts_out")
    win_in = [sem("win_in0"), sem("win_in1")]
    y_ready = sem("y_ready")
    y_copied = sem("y_copied")
    y_taken = sem("y_taken")
    var_read = sem("var_read")
    var_done = sem("var_done")
    rstd_ready = sem("rstd_ready")
    rstd_turned = sem("rstd_turned")
    rows_ready = sem("rows_ready")
    bc_ready = sem("bc_ready")
    scaled = sem("scaled")
    gelu_done = sem("gelu_done")
    steps_sem = sem("steps_sem")

    ident, h6, lnp = res["ident"], res["h6"], res["lnp"]
    with ExitStack() as ctx:
        sb = lambda n, s, d=F32: ctx.enter_context(nc.sbuf_tensor(n, s, d))
        ps = ctx.enter_context(nc.psum_tensor("ps", [P, 8, 512], F32))
        ypair = [ps[:, 0:2, :], ps[:, 2:4, :]]
        spread = [ps[:, 4, :], ps[:, 5, :]]
        var_ps = ps[:, 6, :]
        rows_ps = ps[:, 7, :].bitcast(BF16)

        h0 = sb("h0", [P, 2, GROUP, ROW0])
        h1 = sb("h1", [P, 2, GROUP, L1.row])
        h2 = sb("h2", [P, 2, GROUP, L2.row])
        h3 = sb("h3", [P, ROUNDS, 2, GROUP, L3.row])
        h4 = sb("h4", [P, BATCH, L4.row])
        h5 = sb("h5", [P, BATCH, L5.row])
        sq = sb("sq", [P, 2, 2, 400])
        win = sb("win", [PARTS * PARTS * K0, ROUND * POS0], BF16)
        w = sb("w", [P, TAPS, CH])
        wmean = sb("wmean", [P, TAPS])
        w0 = sb("w0", [P, K0])
        w0_parts = sb("w0_parts", [K0, PARTS, CH], BF16)
        w0_rest = sb("w0_rest", [K0, CH])
        w0_stack = sb("w0_stack", [PARTS * PARTS * K0, CH], BF16)
        w0_pairs = sb("w0_pairs", [P, K0, K0])
        gram = sb("gram", [P, K0, K0])
        averager = sb("averager", [P, P])
        pick = sb("pick", [96, 8, P], BF16)
        ident16 = sb("ident16", [P, P], BF16)
        xs = sb("xs", [P, STRIDE0 * (SL + 1)])
        u = sb("u", [P, K0, SL])
        scaled_win = sb("scaled_win", [P, K0, SL])
        parts = sb("parts", [P, PARTS, K0, SL], BF16)
        v0, r0, t0, t1 = (sb(n, [P, SL]) for n in ("v0", "r0", "t0", "t1"))
        vs, rs, ts, us, rest = (sb(n, [100, 2, 32]) for n in ("vs", "rs", "ts", "us", "rest"))
        rparts = sb("rparts", [100, 2, 4, 96], BF16)
        rows = sb("rows", [96, 2, 400], BF16)

        windows_dram = nc.dram_tensor("windows_dram", [ROUNDS, PARTS * K0, ROUND * POS0], BF16, kind="Internal").ap()
        xwin = xs[:, :].rearrange("p (t k) -> p k t", k=STRIDE0)
        tap = lambda k: xwin[:, k % STRIDE0, k // STRIDE0:k // STRIDE0 + SL]

        def chunk(l, slot, c, r):
            L = LAYERS[l]
            a, n = c * L.per_chunk, L.per_chunk
            if l >= 4:
                a += slot * BATCH // 2
            if l <= 2:
                return (h1, h2)[l - 1][:, slot, a:a + n, 0:L.pos]
            if l == 3:
                return h3[:, bass.ds(r, 1), slot, a:a + n, 0:L.pos].rearrange("p o b t -> p (o b) t")
            if l == 4:
                return h4[:, a:a + n, 0:L.pos]
            if l == 5:
                return h5[:, a:a + n, 0:L.pos]
            return h6[:, :].rearrange("p (b t) -> p b t", t=L.pos)[:, a:a + n, :]

        def source(l, slot, c, t):
            L = LAYERS[l]
            a, n = c * L.per_chunk, L.per_chunk
            if l >= 4:
                a += slot * BATCH // 2
            cut = slice(t, t + 2 * L.pos - 1, 2)
            if l <= 3:
                return (h0, h1, h2)[l - 1][:, slot, a:a + n, cut]
            if l == 4:
                return h3[:, :, :, :, :].rearrange("p r s b t -> p (r s b) t")[:, a:a + n, cut]
            return (h4, h5)[l - 5][:, a:a + n, cut]

        def for_rounds(eng, run):
            run(body, 0, Origin(0, per))
            with eng.Fori(1, ROUNDS - 1) as r:
                run(body, r, Origin(r, per))
            run(last, ROUNDS - 1, Origin(ROUNDS - 1, per))

        def joined(l, s, p, r):
            L = LAYERS[l]
            a, n = 2 * p * L.per_chunk, 2 * L.per_chunk
            if l >= 4:
                a += s * BATCH // 2
            if l <= 2:
                return (h1, h2)[l - 1][:, s, a:a + n, 0:L.pos]
            if l == 3:
                return h3[:, bass.ds(r, 1), s, a:a + n, 0:L.pos].rearrange("p o b t -> p (o b) t")
            if l == 4:
                return h4[:, a:a + n, 0:L.pos]
            if l == 5:
                return h5[:, a:a + n, 0:L.pos]
            return h6[:, :].rearrange("p (b t) -> p b t", t=L.pos)[:, a:a + n, :]

        with nc.Block() as block:

            @block.sync
            def _(sp):
                def samples(r):
                    b0 = ROUND * r
                    src = io["x"][bass.ds(b0, ROUND), :]
                    lanes = bass.AP(src.tensor, src.offset, [[XROW, ROUND], [STRIDE0 * SL, SLICES], [1, STRIDE0 * (SL + 1)]])
                    sp.dma_start(xs[:, :], lanes).then_inc(x_in, 16)

                def windows(r, more):
                    sp.wait_ge(parts_ready, r + 1)
                    if more:
                        samples(r + 1)
                    scratch = windows_dram[bass.ds(r, 1), :, :].rearrange("o k c -> (o k) c")
                    sp.dma_start(scratch.rearrange("k (l t) -> l k t", t=SL),
                                 parts[:, :, :, :].rearrange("p a k t -> p (a k) t")).then_inc(parts_out, 16)
                    sp.wait_ge(parts_out, 16 * (r + 1))
                    return scratch

                def back(scratch, slot):
                    cut = slice(slot * GROUP * POS0, (slot + 1) * GROUP * POS0)
                    for a in range(PARTS):
                        sp.dma_start(win[a * PARTS * K0:(a + 1) * PARTS * K0, cut], scratch[:, cut]).then_inc(win_in[slot], 16)

                samples(0)
                sp.dma_start(w0[:, :], io["w0"]).then_inc(w_in, 16)
                sp.dma_start(lnp[:, :], io["lnp"]).then_inc(w_in, 16)
                sp.dma_start(w[:, :, :], io["w"]).then_inc(w_in, 16)
                sp.wait_ge(s_w0, 5)
                for a in range(PARTS):
                    for b in range(PARTS):
                        row = (a * PARTS + b) * K0
                        sp.dma_start(w0_stack[row:row + K0, :], w0_parts[:, a, :]).then_inc(w0_in, 16)
                scratch = windows(0, True)
                back(scratch, 0)
                back(scratch, 1)

                read = number_of(body, "first", 0, 1, GROUP - 1, "pair") + 1

                def middle(r, more):
                    scratch = windows(r, more)
                    sp.wait_ge(y_ready, AHEAD + per["pair"] * (r - 1))
                    back(scratch, 0)
                    sp.wait_ge(y_ready, AHEAD + per["pair"] * (r - 1) + read)
                    back(scratch, 1)

                with sp.Fori(1, ROUNDS - 1) as r:
                    middle(r, True)
                middle(ROUNDS - 1, False)

            @block.gpsimd
            def _(pool):
                pool.memset(averager[:, :], 1.0 / CH).then_inc(s_const, 1)
                pool.memset(ident[:, :], 0.0).then_inc(s_const, 1)
                pool.memset(ident16[:, :], 0.0).then_inc(s_const, 1)
                pool.memset(pick[:, :, :], 0.0).then_inc(s_const, 1)
                pool.memset(rparts[:, :, :, :], 0.0).then_inc(s_const, 1)
                pool.memset(h0[:, :, :, POS0:ROW0], 0.0).then_inc(s_const, 1)
                pool.memset(h1[:, :, :, L1.pos:L1.row], 0.0).then_inc(s_const, 1)
                pool.memset(h2[:, :, :, L2.pos:L2.row], 0.0).then_inc(s_const, 1)
                pool.memset(h3[:, :, :, :, L3.pos:L3.row], 0.0).then_inc(s_const, 1)
                pool.wait_ge(s_const, 4)
                for m in (ident, ident16):
                    pool.affine_select(out=m[:, :], in_=m[:, :], compare_op=ALU.not_equal, fill=1.0, base=0,
                                       pattern=[[-1, P]], channel_multiplier=1).then_inc(s_const, 1)
                for a in range(PARTS):
                    if a:
                        pool.wait_ge(s_const, 11 + a)
                    pool.affine_select(out=pick[:, :, :], in_=pick[:, :, :], compare_op=ALU.not_equal, fill=1.0,
                                       base=-32 * a, pattern=[[-1, 8], [0, P]], channel_multiplier=1).then_inc(s_const, 1)

            CONSTS = 14
            SLOT_IN = 16 * PARTS

            @block.tensor
            def _(pe):
                pe.wait_ge(s_const, CONSTS)
                pe.wait_ge(w_in, 48)
                pe.matmul(spread[0][:, 0:K0], averager[:, :], w0[:, :], start=True, stop=True).then_inc(s_w0, 1)
                pe.wait_ge(s_w0, 3)
                pe.matmul(spread[1][:, 0:K0 * K0], averager[:, :], w0_pairs[:, :, :], start=True, stop=True).then_inc(s_w0, 1)
                pe.transpose(ps[0:K0, 6, 0:CH], w0[:, :], ident[:, :]).then_inc(weights_ready, 1)

                def first(b, bank):
                    for h in range(2):
                        mm = pe.matmul(ypair[bank][:, h, 0:400], w0_stack[:, :],
                                       win[:, b * POS0 + h * 400:b * POS0 + h * 400 + 400], start=True, stop=True)
                    mm.then_inc(y_ready, 1)

                pe.wait_ge(w0_in, 16 * PARTS * PARTS)
                for b in range(AHEAD):
                    if b % GROUP == 0:
                        pe.wait_ge(win_in[b // GROUP], SLOT_IN)
                    if b >= 2:
                        pe.wait_ge(y_taken, b - 1)
                    first(b, (b + AHEAD) % 2)
                pe.wait_ge(weights_ready, 2)

                def run(plan, r, o):
                    for what, l, s, p, n in plan:
                        L = LAYERS.get(l)
                        if what in ("half", "first"):
                            user, number = n["before"]
                            if user == "first":
                                pe.wait_ge(y_taken, o.pair + number + 1)
                            else:
                                pe.wait_ge(y_copied, o.conv + number + 1)
                        if what == "first":
                            if l == 1 and p == 0:
                                pe.wait_ge(win_in[s], SLOT_IN * (r + 2))
                            first(s * GROUP + p, n["bank"])
                        elif what in ("half", "conv"):
                            c = int(what == "conv")
                            if l == 1:
                                batch = GROUP * s + 2 * p + c
                                if batch >= AHEAD:
                                    at = o.pair + number_of(plan, "first", 0, s, batch % GROUP, "pair")
                                elif isinstance(r, int) and r == 0:
                                    at = batch
                                else:
                                    at = o.pair - per["pair"] + number_of(body, "first", 1, s, batch % GROUP, "pair")
                                pe.wait_ge(y_taken, at + 1)
                            elif l == 4:
                                behind = 0 if (s, p) < (1, 1) else gelus_before(plan, 3, 1)[0] + 1
                                pe.wait_ge(gelu_done, o.gelu + behind)
                            else:
                                done = gelus_before(plan, l - 1, s)
                                pe.wait_ge(gelu_done, o.gelu + done[min(2 * p + c, max(done))] + 1)
                            out = ypair[n["bank"]][:, c, 0:L.cols].rearrange("p (b t) -> p b t", t=L.pos)
                            for t in range(L.taps):
                                mm = pe.matmul(out, w[:, L.first_tap + t, :], source(l, s, 2 * p + c, t),
                                               start=(t == 0), stop=(t == L.taps - 1))
                            if c:
                                mm.then_inc(y_ready, 1)
                        elif what == "var":
                            pe.wait_ge(y_taken, o.pair + number_of(plan, "conv", l, s, p, "pair") + 1)
                            before = o.sets + n["norm"]
                            if p == 0 and not (isinstance(before, int) and before < 1):
                                pe.wait_ge(var_read, before)
                            for c in range(2):
                                for q in range(4):
                                    at = q * L.chunks + 2 * p + c
                                    mm = pe.matmul(var_ps[0:L.w, at:at + 1],
                                                   sq[:, n["var"] % 2, c, q * L.w:(q + 1) * L.w], averager[:, 0:1],
                                                   start=True, stop=True)
                            mm.then_inc(var_done, 1)
                        elif what == "rows":
                            pe.wait_ge(rstd_ready, o.sets + n["rows"] + 1)
                            for q in range(4):
                                mm = pe.transpose(rows_ps[0:96, q * L.w:(q + 1) * L.w],
                                                  rparts[0:L.w, s, q, :], ident16[0:L.w, 0:L.w])
                            mm.then_inc(rstd_turned, 1)
                        elif what == "scale":
                            if p == 0:
                                pe.wait_ge(rows_ready, o.sets + n["rows"])
                            used = o.scale + n["scale"] - 1
                            if not (isinstance(used, int) and used < 1):
                                pe.wait_ge(scaled, used)
                            pe.matmul(spread[n["scale"] % 2][:, 0:L.cols], pick[:, p, :],
                                      rows[:, s, 0:L.cols], start=True, stop=True).then_inc(bc_ready, 1)

                for_rounds(pe, run)

            @block.scalar
            def _(act):
                act.wait_ge(w_in, 48)

                def first(s, p, b, pair):
                    act.wait_ge(y_ready, pair + 1)
                    act.activation(h0[:, s, p, 0:POS0].rearrange("p (h t) -> p h t", h=2), ypair[b][:, :, 0:400],
                                   ACT.Gelu, scale=lnp[:, 0:1], bias=lnp[:, 1:2]).then_inc(y_taken, 1)

                for b in range(AHEAD):
                    first(b // GROUP, b % GROUP, (b + AHEAD) % 2, b)

                def run(plan, r, o):
                    for what, l, s, p, n in plan:
                        L = LAYERS.get(l)
                        if what == "first":
                            first(s, p, n["bank"], o.pair + n["pair"])
                        elif what == "conv":
                            act.wait_ge(y_copied, o.conv + n["conv"] + 1)
                            used = o.conv + n["conv"] - 1
                            if not (isinstance(used, int) and used < 1):
                                act.wait_ge(var_done, used)
                            if l == 3:
                                act.nop(nofuse=True)
                            act.activation(sq[:, n["conv"] % 2, :, 0:L.cols].rearrange("p c (b t) -> p c b t", t=L.pos),
                                           joined(l, s, p, r).rearrange("p (c b) t -> p c b t", c=2), ACT.Square).then_inc(y_taken, 1)
                        elif what == "gelu":
                            act.wait_ge(scaled, o.scale + n["scale"])
                            if l == 3:
                                act.nop(nofuse=True)
                            both = joined(l, s, p, r)
                            act.activation(both, both, ACT.Gelu, scale=lnp[:, 2 * l:2 * l + 1],
                                           bias=lnp[:, 2 * l + 1:2 * l + 2]).then_inc(gelu_done, 1)

                for_rounds(act, run)

            @block.vector
            def _(dve):
                steps = Steps(dve, steps_sem)
                dve.wait_ge(s_w0, 1)
                nc.vector.tensor_tensor(w0[:, :], w0[:, :], spread[0][:, 0:K0], ALU.subtract).then_inc(s_w0, 1)
                dve.wait_ge(s_w0, 2)
                nc.vector.tensor_tensor(w0_pairs[:, :, :], w0[:, :].unsqueeze(2).broadcast_to([P, K0, K0]),
                                        w0[:, :].unsqueeze(1).broadcast_to([P, K0, K0]), ALU.mult).then_inc(s_w0, 1)
                dve.wait_ge(s_w0, 4)
                steps.done(nc.vector.tensor_scalar(gram[:, :, :], spread[1][:, 0:K0 * K0].rearrange("p (a b) -> p a b", a=K0), 2.0, None, ALU.mult))
                dve.wait_ge(weights_ready, 1)
                turned = ps[0:K0, 6, 0:CH]
                steps.done(nc.vector.tensor_copy(w0_parts[:, 0, :], turned))
                steps.settle()
                steps.done(nc.vector.tensor_tensor(w0_rest[:, :], turned, w0_parts[:, 0, :], ALU.subtract))
                steps.settle()
                steps.done(nc.vector.tensor_copy(w0_parts[:, 1, :], w0_rest[:, :]))
                steps.settle()
                nc.vector.tensor_tensor(w0_parts[:, 2, :], w0_rest[:, :], w0_parts[:, 1, :], ALU.subtract).then_inc(s_w0, 1)

                def prepare(r, part):
                    if part == 0:
                        dve.wait_ge(x_in, 16 * (r + 1))
                    if part < K0:
                        steps.settle()
                        for k in range(K0 - part):
                            l = k + part
                            if part == 0:
                                steps.done(nc.vector.tensor_scalar(u[:, k, :], tap(l), gram[:, k, l:l + 1], 0.5, ALU.mult, ALU.mult))
                            else:
                                steps.done(nc.vector.scalar_tensor_tensor(out=u[:, k, :], in0=tap(l), scalar=gram[:, k, l:l + 1],
                                                                          in1=u[:, k, :], op0=ALU.mult, op1=ALU.add))
                    elif part == K0:
                        steps.settle()
                        for h in range(2):
                            steps.done(nc.vector.tensor_tensor(u[:, 5 * h:5 * h + 5, :], u[:, 5 * h:5 * h + 5, :],
                                                               xwin[:, :, h:h + SL], ALU.mult))
                        steps.settle()
                        steps.done(nc.vector.tensor_reduce(v0[:, :], u[:, :, :].rearrange("p k t -> p t k"), AX.X, ALU.add))
                        steps.settle()
                        steps.done(nc.vector.tensor_scalar(v0[:, :], v0[:, :], 0.0, CENTRE_EPS, ALU.max, ALU.add))
                        steps.settle()
                    elif part == K0 + 1:
                        newton_rsqrt(nc, steps, v0[:, :], r0[:, :], t0[:, :], t1[:, :])
                    elif part == K0 + 2:
                        for h in range(2):
                            steps.done(nc.vector.tensor_tensor(scaled_win[:, 5 * h:5 * h + 5, :], xwin[:, :, h:h + SL],
                                                               r0[:, :].unsqueeze(1).broadcast_to([P, 5, SL]), ALU.mult))
                        steps.settle()
                        if not (isinstance(r, int) and r == 0):
                            dve.wait_ge(parts_out, 16 * r)
                        steps.done(nc.vector.tensor_copy(parts[:, 0, :, :], scaled_win[:, :, :]))
                        steps.settle()
                    else:
                        steps.done(nc.vector.tensor_tensor(scaled_win[:, :, :], scaled_win[:, :, :], parts[:, 0, :, :], ALU.subtract))
                        steps.settle()
                        steps.done(nc.vector.tensor_copy(parts[:, 1, :, :], scaled_win[:, :, :]))
                        steps.settle()
                        nc.vector.tensor_tensor(parts[:, 2, :, :], scaled_win[:, :, :], parts[:, 1, :, :],
                                                ALU.subtract).then_inc(parts_ready, 1)

                PREP = K0 + 4
                steps.settle()
                for part in range(PREP):
                    prepare(0, part)
                dve.wait_ge(w_in, 48)
                steps.done(nc.vector.tensor_reduce(wmean[:, :], w[:, :, :], AX.X, ALU.add))
                steps.settle()
                steps.done(nc.vector.tensor_scalar(wmean[:, :], wmean[:, :], 1.0 / CH, None, ALU.mult))
                steps.settle()
                nc.vector.tensor_tensor(w[:, :, :], w[:, :, :], wmean[:, :].unsqueeze(2).broadcast_to([P, TAPS, CH]),
                                        ALU.subtract).then_inc(weights_ready, 1)
                dve.wait_ge(s_const, CONSTS)

                def run(plan, r, o):
                    for what, l, s, p, n in plan:
                        L = LAYERS.get(l)
                        if what == "conv":
                            dve.wait_ge(y_ready, o.pair + n["pair"] + 1)
                            nc.vector.tensor_copy(
                                joined(l, s, p, r).rearrange("p (c b) t -> p c b t", c=2),
                                ypair[n["bank"]][:, :, 0:L.cols].rearrange("p c (b t) -> p c b t", t=L.pos)).then_inc(y_copied, 1)
                        elif what == "prep":
                            prepare(r + 1, p)
                        elif what == "norm":
                            k, sl, wide = 4 * L.chunks, s, L.w
                            v, y, t, q, left = (x[0:wide, sl, 0:k] for x in (vs, rs, ts, us, rest))
                            part = lambda a: rparts[0:wide, sl, :, 32 * a:32 * a + L.chunks]
                            four = lambda x: x.rearrange("p (q c) -> p q c", q=4)
                            dve.wait_ge(var_done, o.conv + n["var"])
                            nc.vector.tensor_scalar(v, var_ps[0:wide, 0:k], CENTRE_EPS, None, ALU.add).then_inc(var_read, 1)
                            dve.wait_ge(var_read, o.sets + n["norm"] + 1)
                            newton_rsqrt(nc, steps, v, y, t, q)
                            steps.done(nc.vector.tensor_copy(part(0), four(y)))
                            steps.settle()
                            steps.done(nc.vector.tensor_tensor(four(left), four(y), part(0), ALU.subtract))
                            steps.settle()
                            steps.done(nc.vector.tensor_copy(part(1), four(left)))
                            steps.settle()
                            nc.vector.tensor_tensor(part(2), four(left), part(1), ALU.subtract).then_inc(rstd_ready, 1)
                        elif what == "rows":
                            dve.wait_ge(rstd_turned, o.sets + n["rows"] + 1)
                            nc.vector.tensor_copy(rows[:, s, 0:L.cols],
                                                  rows_ps[0:96, 0:L.cols]).then_inc(rows_ready, 1)
                        elif what == "scale":
                            dve.wait_ge(bc_ready, o.scale + n["scale"] + 1)
                            if p % 2 == 0:
                                dve.wait_ge(y_copied, o.conv + number_of(plan, "conv", l, s, p // 2, "conv") + 1)
                            h = chunk(l, s, p, r)
                            nc.vector.tensor_tensor(h, h, spread[n["scale"] % 2][:, 0:L.cols].rearrange(
                                "p (b t) -> p b t", t=L.pos), ALU.mult).then_inc(scaled, 1)

                start = steps.n
                run(body, 0, Origin(0, per))
                each = steps.n - start
                with dve.Fori(1, ROUNDS - 1) as r:
                    steps.at(start + each * r)
                    run(body, r, Origin(r, per))
                    assert steps.n == each
                steps.at(start + each * (ROUNDS - 1))
                run(last, ROUNDS - 1, Origin(ROUNDS - 1, per))



class RowSums:

    def __init__(self, terms, width, sum_pe, sum_pe_pool, by_vector, by_pool, first, second, out, mirror=None):
        self.terms, self.width = terms, width
        self.sum_pe, self.sum_pe_pool, self.by_vector, self.by_pool = sum_pe, sum_pe_pool, by_vector, by_pool
        self.first, self.second, self.out, self.mirror = first, second, out, mirror
        self.reduced = by_vector + by_pool
        self.pooled = len(sum_pe_pool) + len(by_pool)

    def places(self, rows):
        at, out = 0, {}
        for i in rows:
            out[i] = slice(at, at + self.width(i))
            at += self.width(i)
        return out, at

    def by_term(self, buffer, rows, i):
        places, wide = self.places(rows)
        full = buffer[:, 0:self.terms * wide].rearrange("p (k n) -> p k n", k=self.terms)[:, :, places[i]]
        return full.rearrange("p k (a b) -> p a b k", a=self.first(i).shape[1])

    def copies(self, bank, rows):
        places, wide = self.places(rows)
        for i in rows:
            src = bank[:, places[i]].rearrange("p (a b) -> p a b", a=self.first(i).shape[1])
            yield self.out(i), src
            if self.mirror and self.mirror(i) is not None:
                yield self.mirror(i)[0], src[:, :, 1:]

    def mirrors(self):
        return [i for i in self.reduced if self.mirror and self.mirror(i) is not None]

    def copied(self):
        batch = list(self.sum_pe) + list(self.sum_pe_pool)
        return len(batch) + (sum(self.mirror(i) is not None for i in batch) if self.mirror else 0) + len(self.mirrors())


class Before:

    def __init__(self, sums=0, reduced=0, copied=0, pooled=0):
        self.sums, self.reduced, self.copied, self.pooled = sums, reduced, copied, pooled

    def after(self, *jobs, times=1):
        add = lambda f: sum(f(j) for j in jobs)
        return Before(self.sums + len(jobs) * times, self.reduced + add(lambda j: len(j.reduced)) * times,
                      self.copied + add(lambda j: j.copied()) * times, self.pooled + add(lambda j: j.pooled) * times)


def normalise(nc, steps, src, dst, stats, mv, y, t, u):
    for i in range(TT):
        steps.done(nc.vector.bn_stats(stats[:, i, :], src[i]))
    steps.settle()
    for i in range(TT):
        steps.done(nc.vector.bn_aggr(mv[:, i, :], stats[:, i, :]))
    steps.settle()
    steps.done(nc.vector.tensor_scalar(mv[:, :, 1], mv[:, :, 1], CENTRE_EPS, None, ALU.add))
    steps.settle()
    steps.done(nc.vector.tensor_copy(stats[:, :, 0], mv[:, :, 1]))
    steps.settle()
    newton_rsqrt(nc, steps, stats[:, :, 0], y, t, u)
    for i in range(TT):
        steps.done(nc.vector.tensor_scalar(dst[i], src[i], mv[:, i, 0:1], y[:, i:i + 1], ALU.subtract, ALU.mult))
    steps.settle()


def turn(pe, ps, src, ident, done):
    for k in range(KD):
        for t in range(TT):
            mm = pe.transpose(ps[0:96, k, t * P:(t + 1) * P], src[:, t, 96 * k:96 * k + 96], ident[:, :])
    mm.then_inc(done, 1)


def attention(nc, io, res, top):
    sem = lambda n: top.enter_context(nc.semaphore(n))
    a_in = sem("a_in")
    turned = sem("turned")
    a_steps = sem("a_steps")
    to_pe = sem("to_pe")
    projected = sem("projected")
    qkv_ready = sem("qkv_ready")
    qkv_copied = sem("qkv_copied")
    qkv_out = sem("qkv_out")
    lanes_in = sem("lanes_in")
    scores_ready = sem("scores_ready")
    exp_done = sem("exp_done")
    peaks = sem("peaks")
    eye_ready = sem("eye_ready")
    multiplied = sem("multiplied")
    pool_multiplied = sem("pool_multiplied")
    pe_summed = sem("pe_summed")
    row_done = sem("row_done")
    copied = sem("copied")
    cubic_ready = sem("cubic_ready")
    share_ready = sem("share_ready")
    e_ready = sem("e_ready")
    out_lanes = sem("out_lanes")
    o_out = sem("o_out")
    o_in = sem("o_in")
    R = SEQ + 1
    HL = HEADS // 2
    ROOT = sqrt(PADS)
    ident, h6, lnp, hidden = (res[k] for k in ("ident", "h6", "lnp", "hidden"))
    with ExitStack() as ctx:
        sb = lambda n, s, d=F32: ctx.enter_context(nc.sbuf_tensor(n, s, d))
        pt = ctx.enter_context(nc.psum_tensor("pt", [P, 4, 1024], F32))
        proj_w = sb("proj_w", [CH, D])
        qkv_w = sb("qkv_w", [96, KD, 3 * D])
        out_w = sb("out_w", [96, KD, D])
        proj_b, out_b = sb("proj_b", [P, D]), sb("out_b", [P, D])
        norm6 = sb("norm6", [P, TT, CH])
        norm6t = sb("norm6t", [CH, TOK])
        stats, mv = sb("a_stats", [P, TT, 6]), sb("a_mv", [P, TT, 2])
        y6, t6, u6 = sb("a_y6", [P, TT]), sb("a_t6", [P, TT]), sb("a_u6", [P, TT])
        xhat = sb("a_xhat", [P, TT, D])
        xhat_t = sb("a_xhat_t", [96, KD, TOK])
        qkv = sb("qkv", [P, TT, 3 * D])
        lanes = sb("lanes", [P, SEQ, 3, HL * DH])
        rowt = sb("rowt", [P, 2, HL * R * DH])
        for_pe = sb("for_pe", [P, 3 * HL * R * DH])
        pool_for_pe = sb("pool_for_pe", [P, 3 * HL * R * DH])
        from_pool = sb("from_pool", [P, 2 * HL * R * DH])
        scores = sb("scores", [P, HL, SEQ, SEQ])
        peak, epad, den, rden = (sb(n, [P, HL, SEQ]) for n in ("peak", "epad", "den", "rden"))
        smat = sb("smat", [P, HL, R, R])
        e1, e2, c4 = (sb(n, [P, HL, R, R]) for n in ("e1", "e2", "c4"))
        e34 = sb("e34", [P, HL, R, R])
        eye = sb("eye", [P, R, R])
        norms, all_norms, scale = sb("norms", [P, 2]), sb("all_norms", [P, 2]), sb("scale", [P, 2])
        padsum = sb("padsum", [P, HL])
        wv = sb("wv", [P, HL, R, DH])
        attn = sb("attn", [P, SEQ, HL * DH])
        attn_tok = sb("attn_tok", [P, TT, D])
        qkv_dram = nc.dram_tensor("qkv_dram", [TOK, 3 * D], F32, kind="Internal").ap()
        attn_dram = nc.dram_tensor("attn_dram", [TOK, D], F32, kind="Internal").ap()
        q_l, k_l, v_l = (lanes[:, :, a, :] for a in range(3))
        LOADS = 5
        grid = lambda x: x.rearrange("p (h d) -> p h d", d=DH)

        scoring = RowSums(DH, lambda i: HL * SEQ, [0, 1, 2], [3, 4, 5], [6, 7, 8, 9], [10, 11],
                          lambda i: grid(q_l[:, i, :]).unsqueeze(2).broadcast_to([P, HL, SEQ, DH]),
                          lambda i: k_l.rearrange("p j (h d) -> p h j d", d=DH), lambda i: scores[:, :, i, :])
        valuing = RowSums(SEQ, lambda i: HL * DH, [0, 1, 2], [3, 4, 5], [6, 7, 8, 9, 10], [11, 12],
                          lambda i: smat[:, :, i, 1:R].unsqueeze(2).broadcast_to([P, HL, DH, SEQ]),
                          lambda i: v_l.rearrange("p j (h d) -> p h d j", d=DH), lambda i: wv[:, :, i, :])
        applying = RowSums(R, lambda i: HL * DH, [0, 1, 2], [3, 4, 5], [6, 7, 8, 9], [10, 11],
                           lambda i: e1[:, :, i + 1, :].unsqueeze(2).broadcast_to([P, HL, DH, R]),
                           lambda i: wv[:, :, :, :].rearrange("p h k d -> p h d k"), lambda i: grid(attn[:, i, :]))

        def product(a, b, out):
            return RowSums(R, lambda i: HL * (R - i), [0, 1], [2, 3], [4, 5, 6, 7], [8, 9, 10, 11, 12],
                           lambda i: a[:, :, i, :].unsqueeze(2).broadcast_to([P, HL, R - i, R]),
                           lambda i: b[:, :, i:R, :], lambda i: out[:, :, i, i:R],
                           lambda i: (out[:, :, i + 1:R, i], out[:, :, i, i + 1:R]) if i < R - 1 else None)

        outer, squaring, closing = product(smat, smat, e2), product(e1, e1, e2), product(e2, c4, e1)
        at_scoring = Before()
        at_valuing = at_scoring.after(scoring)
        at_outer = at_valuing.after(valuing)
        at_first = at_outer.after(outer)
        at_iteration = lambda n: at_first.after(squaring, closing, times=n)
        at_applying = at_iteration(PINV_ITERS)

        lined = lambda x: x[:, :, :, :].rearrange("p h i j -> p (h i j)")

        def pooled_row(job, i):
            at = job.places(job.by_pool)[0][i].start * job.terms
            size = job.width(i) * job.terms
            return from_pool[:, at:at + size].rearrange("p (a b k) -> p a b k", a=job.first(i).shape[1], k=job.terms)

        with nc.Block() as block:

            @block.sync
            def _(sp):
                sp.dma_start(proj_w[:, :], io["proj_w"]).then_inc(a_in, 16)
                sp.dma_start(proj_b[:, :], io["proj_b"].partition_broadcast(P)).then_inc(a_in, 16)
                sp.dma_start(qkv_w[:, :, :], io["qkv_w"].rearrange("(k p) n -> p k n", k=KD)).then_inc(a_in, 16)
                sp.dma_start(out_w[:, :, :], io["out_w"].rearrange("(k p) n -> p k n", k=KD)).then_inc(a_in, 16)
                sp.dma_start(out_b[:, :], io["out_b"].partition_broadcast(P)).then_inc(a_in, 16)
                for t in range(TT):
                    sp.wait_ge(qkv_copied, t + 1)
                    sp.dma_start(qkv_dram[t * P:(t + 1) * P, :], qkv[:, t, :]).then_inc(qkv_out, 16)
                sp.wait_ge(qkv_out, 16 * TT)
                for half in range(2):
                    src = qkv_dram.rearrange("(b i) (a g c) -> b i a g c", i=SEQ, a=3, g=2)[:, :, :, half, :]
                    sp.dma_start(lanes[half * BATCH:(half + 1) * BATCH, :, :, :], src).then_inc(lanes_in, 16)
                sp.wait_ge(out_lanes, 1)
                for half in range(2):
                    dst = attn_dram.rearrange("(b i) (g c) -> b i g c", i=SEQ, g=2)[:, :, half, :]
                    sp.dma_start(dst, attn[half * BATCH:(half + 1) * BATCH, :, :]).then_inc(o_out, 16)
                sp.wait_ge(o_out, 32)
                sp.dma_start(attn_tok[:, :, :], attn_dram.rearrange("(t p) c -> p t c", p=P)).then_inc(o_in, 16)

            @block.tensor
            def _(pe):
                for t in range(TT):
                    mm = pe.transpose(pt[:, 0, t * P:(t + 1) * P], h6[:, t * P:(t + 1) * P], ident[:, :])
                mm.then_inc(turned, 1)
                pe.wait_ge(to_pe, 1)
                for t in range(TT):
                    mm = pe.transpose(pt[:, 1, t * P:(t + 1) * P], norm6[:, t, :], ident[:, :])
                mm.then_inc(turned, 1)
                pe.wait_ge(to_pe, 2)
                pe.wait_ge(a_in, 16 * LOADS)
                for t in range(TT):
                    mm = pe.matmul(pt[:, 2 + t // 4, (t % 4 // 2) * 512 + (t % 2) * D:(t % 4 // 2) * 512 + (t % 2) * D + D],
                                   norm6t[:, t * P:(t + 1) * P], proj_w[:, :], start=True, stop=True)
                mm.then_inc(projected, 1)
                pe.wait_ge(to_pe, 3)
                turn(pe, pt, xhat, ident, turned)
                pe.wait_ge(to_pe, 4)
                for t in range(TT):
                    if t >= 2:
                        pe.wait_ge(qkv_copied, t - 1)
                    for n in range(2):
                        for k in range(KD):
                            mm = pe.matmul(pt[:, 2 + t % 2, n * 512:n * 512 + 288], xhat_t[:, k, t * P:(t + 1) * P],
                                           qkv_w[:, k, n * 288:(n + 1) * 288], start=(k == 0), stop=(k == KD - 1))
                    mm.then_inc(qkv_ready, 1)

                def sums(job, at):
                    for n, (buffer, rows) in enumerate(((for_pe, job.sum_pe), (pool_for_pe, job.sum_pe_pool))):
                        if n == 0:
                            pe.wait_ge(multiplied, at.sums + 1)
                        else:
                            pe.wait_ge(pool_multiplied, at.pooled + len(rows))
                        wide = job.places(rows)[1]
                        for k in range(job.terms):
                            mm = pe.matmul(pt[:, n, 0:wide], ident[:, :], buffer[:, k * wide:(k + 1) * wide],
                                           start=(k == 0), stop=(k == job.terms - 1))
                        mm.then_inc(pe_summed, 1)

                sums(scoring, at_scoring)
                sums(valuing, at_valuing)
                sums(outer, at_outer)
                with pe.Fori(0, PINV_ITERS) as n:
                    sums(squaring, at_iteration(n))
                    sums(closing, at_iteration(n).after(squaring))
                sums(applying, at_applying)
                pe.wait_ge(o_in, 16)
                turn(pe, pt, attn_tok, ident, turned)
                pe.wait_ge(to_pe, 5)
                for t in range(TT):
                    for k in range(KD):
                        mm = pe.matmul(pt[:, 2 + t // 4, (t % 4 // 2) * 512 + (t % 2) * D:(t % 4 // 2) * 512 + (t % 2) * D + D],
                                       xhat_t[:, k, t * P:(t + 1) * P], out_w[:, k, :], start=(k == 0), stop=(k == KD - 1))
                mm.then_inc(projected, 1)

            @block.gpsimd
            def _(pool):
                pool.memset(eye[:, :, :], 0.0).then_inc(eye_ready, 1)
                pool.wait_ge(eye_ready, 1)
                pool.affine_select(out=eye[:, :, :], in_=eye[:, :, :], compare_op=ALU.not_equal, fill=1.0, base=0,
                                   pattern=[[1, R], [-1, R]], channel_multiplier=0).then_inc(eye_ready, 1)
                pool.memset(smat[:, :, 0, :], ROOT / LANDMARKS).then_inc(eye_ready, 1)
                pool.wait_ge(eye_ready, 3)
                pool.memset(smat[:, :, 0, 0], PADS / LANDMARKS).then_inc(eye_ready, 1)

                def multiply(job, at):
                    if at is not at_scoring:
                        pool.wait_ge(row_done, at.reduced)
                        pool.wait_ge(copied, at.copied)
                    for i in job.sum_pe_pool:
                        pool.tensor_tensor(job.by_term(pool_for_pe, job.sum_pe_pool, i), job.first(i), job.second(i),
                                           ALU.mult).then_inc(pool_multiplied, 1)
                    for i in job.by_pool:
                        pool.tensor_tensor(pooled_row(job, i), job.first(i), job.second(i), ALU.mult).then_inc(pool_multiplied, 1)

                pool.wait_ge(lanes_in, 32)
                multiply(scoring, at_scoring)
                pool.wait_ge(peaks, 2)
                pool.partition_all_reduce(all_norms[:, :], norms[:, :], P, bass.bass_isa.ReduceOp.max).then_inc(peaks, 1)
                multiply(valuing, at_valuing)
                multiply(outer, at_outer)
                pool.wait_ge(e_ready, 1)
                with pool.Fori(0, PINV_ITERS) as n:
                    multiply(squaring, at_iteration(n))
                    pool.tensor_scalar(lined(e34), lined(e1), 0.75, None, ALU.mult).then_inc(share_ready, 1)
                    pool.wait_ge(cubic_ready, n + 1)
                    multiply(closing, at_iteration(n).after(squaring))
                multiply(applying, at_applying)

            @block.scalar
            def _(act):
                for t in range(TT):
                    act.wait_ge(qkv_ready, t + 1)
                    act.copy(qkv[:, t, :].rearrange("p (n c) -> p n c", n=2),
                             pt[:, 2 + t % 2, :].rearrange("p (n c) -> p n c", n=2)[:, :, 0:288]).then_inc(qkv_copied, 1)
                def copies(job, at):
                    def mirror(rows):
                        for i in rows:
                            if i in job.mirrors():
                                act.wait_ge(row_done, at.reduced + job.reduced.index(i) + 1)
                                act.copy(*job.mirror(i)).then_inc(copied, 1)

                    def batch(n, rows):
                        act.wait_ge(pe_summed, 2 * at.sums + n + 1)
                        for to, src in job.copies(pt[:, n, :], rows):
                            act.copy(to, src).then_inc(copied, 1)

                    mirror(job.by_vector[:2])
                    batch(0, job.sum_pe)
                    mirror(job.by_vector[2:])
                    batch(1, job.sum_pe_pool)
                    mirror(job.by_pool)

                copies(scoring, at_scoring)
                act.wait_ge(scores_ready, 1)
                act.activation(scores[:, :, :, :], scores[:, :, :, :], ACT.Exp, scale=DH ** -0.5).then_inc(exp_done, 1)
                act.activation(epad[:, :, :], peak[:, :, :], ACT.Exp, scale=-(DH ** -0.5)).then_inc(exp_done, 1)
                copies(valuing, at_valuing)
                copies(outer, at_outer)
                with act.Fori(0, PINV_ITERS) as n:
                    copies(squaring, at_iteration(n))
                    copies(closing, at_iteration(n).after(squaring))
                copies(applying, at_applying)

            @block.vector
            def _(dve):
                steps = Steps(dve, a_steps)
                tile = lambda x: [x[:, t, :] for t in range(TT)]
                small = (stats, mv, y6[:, :], t6[:, :], u6[:, :])
                dve.wait_ge(turned, 1)
                normalise(nc, steps, [pt[:, 0, t * P:(t + 1) * P] for t in range(TT)], tile(norm6), *small)
                nc.vector.tensor_copy(t6[:, :], y6[:, :]).then_inc(to_pe, 1)
                dve.wait_ge(turned, 2)
                nc.vector.tensor_scalar(norm6t[:, :], pt[:, 1, 0:TOK], lnp[:, 14:15], lnp[:, 15:16],
                                        ALU.mult, ALU.add).then_inc(to_pe, 1)
                dve.wait_ge(projected, 1)
                dve.wait_ge(a_in, 16 * LOADS)

                def projected_tiles():
                    for c in range(TT // 2):
                        bank = pt[:, 2 + c // 2, (c % 2) * 512:(c % 2) * 512 + 2 * D]
                        yield hidden[:, 2 * c:2 * c + 2, :], bank.rearrange("p (t n) -> p t n", t=2)

                for out, bank in projected_tiles():
                    steps.done(nc.vector.tensor_tensor(out, bank, proj_b[:, :].unsqueeze(1).broadcast_to([P, 2, D]), ALU.add))
                steps.settle()
                normalise(nc, steps, tile(hidden), tile(xhat), *small)
                nc.vector.tensor_copy(t6[:, :], y6[:, :]).then_inc(to_pe, 1)
                dve.wait_ge(turned, 3)
                nc.vector.tensor_copy(xhat_t[:, :, :], pt[0:96, 0:2, 0:TOK]).then_inc(to_pe, 1)
                steps.done(nc.vector.tensor_tensor(hidden[:, :, :], hidden[:, :, :], out_b[:, :].unsqueeze(1)
                                                   .broadcast_to([P, TT, D]), ALU.add))

                def sums(job, at):
                    for i in job.sum_pe:
                        ins = nc.vector.tensor_tensor(job.by_term(for_pe, job.sum_pe, i), job.first(i), job.second(i), ALU.mult)
                    ins.then_inc(multiplied, 1)
                    n = len(job.by_vector)
                    for m in range(n + 1):
                        if m < n:
                            i = job.by_vector[m]
                            if m >= 2:
                                dve.wait_ge(row_done, at.reduced + m - 1)
                            row = job.first(i), job.second(i)
                            products = rowt[:, m % 2, 0:job.width(i) * job.terms].rearrange(
                                "p (a b k) -> p a b k", a=row[0].shape[1], k=job.terms)
                            steps.done(nc.vector.tensor_tensor(products, *row, ALU.mult))
                            settled = steps.base + steps.n
                        if m >= 1:
                            dve.wait_ge(a_steps, settled - (m < n))
                            nc.vector.tensor_reduce(job.out(job.by_vector[m - 1]), ready, AX.X, ALU.add).then_inc(row_done, 1)
                        ready = products
                    for m, i in enumerate(job.by_pool):
                        dve.wait_ge(pool_multiplied, at.pooled + len(job.sum_pe_pool) + m + 1)
                        nc.vector.tensor_reduce(job.out(i), pooled_row(job, i), AX.X, ALU.add).then_inc(row_done, 1)
                    dve.wait_ge(row_done, at.reduced + len(job.reduced))
                    dve.wait_ge(copied, at.copied + job.copied())

                dve.wait_ge(lanes_in, 32)
                sums(scoring, at_scoring)
                steps.done(nc.vector.tensor_reduce(peak[:, :, :], scores[:, :, :, :], AX.X, ALU.max))
                steps.settle()
                steps.done(nc.vector.tensor_scalar(peak[:, :, :], peak[:, :, :], 0.0, None, ALU.max))
                steps.settle()
                square = [P, HL, SEQ, SEQ]
                nc.vector.tensor_tensor(scores[:, :, :, :], scores[:, :, :, :], peak[:, :, :].unsqueeze(3).broadcast_to(square),
                                        ALU.subtract).then_inc(scores_ready, 1)
                dve.wait_ge(exp_done, 2)
                steps.done(nc.vector.tensor_reduce(den[:, :, :], scores[:, :, :, :], AX.X, ALU.add))
                steps.settle()
                flat = lambda x: x[:, :, :].rearrange("p h i -> p (h i)")
                steps.done(nc.vector.scalar_tensor_tensor(out=flat(den), in0=flat(epad), scalar=float(PADS), in1=flat(den),
                                                          op0=ALU.mult, op1=ALU.add))
                steps.settle()
                steps.done(nc.vector.reciprocal(flat(rden), flat(den)))
                steps.settle()
                dve.wait_ge(eye_ready, 4)
                real = smat[:, :, 1:R, 1:R]
                steps.done(nc.vector.tensor_tensor(real, scores[:, :, :, :], rden[:, :, :].unsqueeze(3).broadcast_to(square), ALU.mult))
                steps.done(nc.vector.scalar_tensor_tensor(out=smat[:, :, 1:R, 0], in0=epad[:, :, :], scalar=ROOT, in1=rden[:, :, :],
                                                          op0=ALU.mult, op1=ALU.mult))
                steps.settle()
                steps.done(nc.vector.tensor_reduce(den[:, :, :], real, AX.X, ALU.add))
                steps.done(nc.vector.tensor_reduce(peak[:, :, :], real.rearrange("p h i j -> p h j i"), AX.X, ALU.add))
                steps.done(nc.vector.tensor_reduce(padsum[:, :], smat[:, :, 1:R, 0], AX.X, ALU.add))
                steps.settle()
                steps.done(nc.vector.scalar_tensor_tensor(out=den[:, :, :], in0=smat[:, :, 1:R, 0], scalar=ROOT, in1=den[:, :, :],
                                                          op0=ALU.mult, op1=ALU.add))
                steps.done(nc.vector.tensor_scalar(padsum[:, :], padsum[:, :], 1.0 / ROOT, None, ALU.mult))
                steps.settle()
                steps.done(nc.vector.tensor_reduce(norms[:, 0:1], flat(den), AX.X, ALU.max))
                steps.done(nc.vector.tensor_reduce(norms[:, 1:2], flat(peak), AX.X, ALU.max))
                steps.done(nc.vector.tensor_reduce(scale[:, 0:1], padsum[:, :], AX.X, ALU.max))
                steps.settle()
                nc.vector.tensor_scalar(norms[:, 0:1], norms[:, 0:1], 1.0, None, ALU.max).then_inc(peaks, 1)
                nc.vector.tensor_scalar(norms[:, 1:2], norms[:, 1:2], scale[:, 0:1], PADS / LANDMARKS,
                                        ALU.max, ALU.add).then_inc(peaks, 1)
                sums(valuing, at_valuing)

                sums(outer, at_outer)
                dve.wait_ge(peaks, 3)
                steps.done(nc.vector.tensor_tensor(scale[:, 0:1], all_norms[:, 0:1], all_norms[:, 1:2], ALU.mult))
                steps.settle()
                steps.done(nc.vector.reciprocal(scale[:, 1:2], scale[:, 0:1]))
                steps.settle()
                steps.done(nc.vector.tensor_scalar(scale[:, 1:2], scale[:, 1:2], -1.0, None, ALU.mult))
                steps.settle()
                heads = lambda x: x[:, :, :, :].rearrange("p h i j -> p h (i j)")
                nc.vector.scalar_tensor_tensor(
                    out=heads(e1), in0=heads(e2), scalar=scale[:, 1:2],
                    in1=eye[:, :, :].rearrange("p i j -> p (i j)").unsqueeze(1).broadcast_to([P, HL, R * R]),
                    op0=ALU.mult, op1=ALU.add).then_inc(e_ready, 1)
                dve.wait_ge(e_ready, 1)
                start = steps.n
                each = len(squaring.by_vector) + len(closing.by_vector)
                with dve.Fori(0, PINV_ITERS) as n:
                    steps.at(start + each * n)
                    sums(squaring, at_iteration(n))
                    dve.wait_ge(share_ready, n + 1)
                    nc.vector.scalar_tensor_tensor(out=lined(c4), in0=lined(e2), scalar=0.25, in1=lined(e34),
                                                   op0=ALU.mult, op1=ALU.add).then_inc(cubic_ready, 1)
                    dve.wait_ge(cubic_ready, n + 1)
                    sums(closing, at_iteration(n).after(squaring))
                    assert steps.n == each
                steps.at(start + each * PINV_ITERS)
                sums(applying, at_applying)
                nc.vector.tensor_tensor(attn[:, :, :].rearrange("p i (h d) -> p i h d", d=DH),
                                        wv[:, :, 1:R, :].rearrange("p h i d -> p i h d"),
                                        attn[:, :, :].rearrange("p i (h d) -> p i h d", d=DH), ALU.subtract).then_inc(out_lanes, 1)
                dve.wait_ge(turned, 4)
                nc.vector.tensor_copy(xhat_t[:, :, :], pt[0:96, 0:2, 0:TOK]).then_inc(to_pe, 1)
                dve.wait_ge(projected, 2)
                for out, bank in projected_tiles():
                    steps.done(nc.vector.tensor_tensor(out, out, bank, ALU.add))
                steps.settle()


def experts(nc, io, res, top):
    sem = lambda n: top.enter_context(nc.semaphore(n))
    f_in = sem("f_in")
    f_steps = sem("f_steps")
    f_pe = sem("f_pe")
    f_turned = sem("f_turned")
    routed = sem("routed")
    logits_ready = sem("logits_ready")
    f_exp = sem("f_exp")
    iota_ready = sem("iota_ready")
    up_ready = sem("up_ready")
    silu_done = sem("silu_done")
    act_ready = sem("act_ready")
    down_ready = sem("down_ready")
    summed = sem("summed")
    out_done = sem("out_done")
    N_HID = EXPERTS * HID + SHID
    MT = N_HID // P
    ROUTED_T = EXPERTS * HID // P
    ident, hidden = res["ident"], res["hidden"]
    gate_w, up_w, down_w, router_w, gate_b = (res[k] for k in ("gate_w", "up_w", "down_w", "router_w", "gate_b"))

    def parts_of(unit):
        if unit == 0:
            return [(ROUTED_T + i, 0, P) for i in range(SHID // P)]
        a, b = (unit - 1) * HID, unit * HID
        out = []
        while a < b:
            end = min(b, (a // P + 1) * P)
            out.append((a // P, a % P, a % P + end - a))
            a = end
        return out

    with ExitStack() as ctx:
        sb = lambda n, s, d=F32: ctx.enter_context(nc.sbuf_tensor(n, s, d))
        pf = ctx.enter_context(nc.psum_tensor("pf", [P, 4, 1024], F32))
        stats, mv = sb("f_stats", [P, TT, 6]), sb("f_mv", [P, TT, 2])
        y6, t6, u6 = sb("f_y6", [P, TT]), sb("f_t6", [P, TT]), sb("f_u6", [P, TT])
        xhat = sb("f_xhat", [P, TT, D])
        xhat_t = sb("f_xhat_t", [96, KD, TOK])
        NE = EXPERTS + 1
        logit, prob = sb("logit", [P, TT, NE]), sb("prob", [P, TT, NE])
        top = sb("top", [P, TT, 8])
        where = sb("where", [P, TT, 8], U32)
        wheref = sb("wheref", [P, TT, 8])
        iota_i, iota_f = sb("iota_i", [P, 8], I32), sb("iota_f", [P, 8])
        one, two = sb("one", [P, TT, 8]), sb("two", [P, TT, 8])
        peak, total = sb("f_peak", [P, TT]), sb("f_total", [P, TT])
        mix = sb("mix", [P, TT, NE])
        silu = sb("silu", [P, 2, TOK])
        acts = sb("acts", [P, MT, TOK])

        with nc.Block() as block:

            @block.sync
            def _(sp):
                for t in range(TT):
                    sp.wait_ge(summed, TT * EXPERTS + t + 1)
                    sp.dma_start(io["out"][t * P:(t + 1) * P, :], hidden[:, t, :]).then_inc(out_done, 16)
                sp.wait_ge(out_done, 16 * TT)

            @block.gpsimd
            def _(pool):
                pool.iota(iota_i[:, :], pattern=[[1, 8]], base=0, channel_multiplier=0).then_inc(iota_ready, 1)

            @block.tensor
            def _(pe):
                pe.wait_ge(f_pe, 1)
                turn(pe, pf, xhat, ident, f_turned)
                pe.wait_ge(f_pe, 2)
                pe.wait_ge(res["f_in"], 16 * res["f_loads"])
                for t in range(TT):
                    for k in range(KD):
                        mm = pe.matmul(pf[:, 2, t * NE:(t + 1) * NE], xhat_t[:, k, t * P:(t + 1) * P], router_w[:, k, :],
                                       start=(k == 0), stop=(k == KD - 1))
                mm.then_inc(routed, 1)
                pe.wait_ge(logits_ready, 1)
                for m in range(MT):
                    if m >= 2:
                        pe.wait_ge(act_ready, m - 1)
                    for g, w in ((0, gate_w), (1, up_w)):
                        for n in range(2):
                            for k in range(KD):
                                mm = pe.matmul(pf[:, 2 * (m % 2) + g, n * 512:n * 512 + TOK // 2], w[:, k, m * P:(m + 1) * P],
                                               xhat_t[:, k, n * TOK // 2:(n + 1) * TOK // 2],
                                               start=(k == 0), stop=(k == KD - 1))
                    mm.then_inc(up_ready, 1)
                for unit in range(NE):
                    for t in range(TT):
                        n = unit * TT + t
                        if unit == 0:
                            pe.wait_ge(act_ready, MT)
                        if n >= 8:
                            pe.wait_ge(summed, n - 7)
                        rows = parts_of(unit)
                        for j, (tile, a, b) in enumerate(rows):
                            mm = pe.matmul(pf[:, n % 8 // 2, (n % 2) * 512:(n % 2) * 512 + D], acts[a:b, tile, t * P:(t + 1) * P],
                                           down_w[a:b, tile, :], start=(j == 0), stop=(j == len(rows) - 1))
                        mm.then_inc(down_ready, 1)

            @block.scalar
            def _(act):
                act.wait_ge(logits_ready, 1)
                act.activation(prob[:, :, :], logit[:, :, :], ACT.Exp).then_inc(f_exp, 1)
                for m in range(MT):
                    act.wait_ge(up_ready, m + 1)
                    if m >= 2:
                        act.wait_ge(act_ready, m - 1)
                    act.activation(silu[:, m % 2, :].rearrange("p (n c) -> p n c", n=2),
                                   pf[:, 2 * (m % 2), :].rearrange("p (n c) -> p n c", n=2)[:, :, 0:TOK // 2],
                                   ACT.Silu).then_inc(silu_done, 1)

            @block.vector
            def _(dve):
                steps = Steps(dve, f_steps)
                tile = lambda x: [x[:, t, :] for t in range(TT)]
                normalise(nc, steps, tile(hidden), tile(xhat), stats, mv, y6[:, :], t6[:, :], u6[:, :])
                nc.vector.tensor_copy(t6[:, :], y6[:, :]).then_inc(f_pe, 1)
                dve.wait_ge(f_turned, 1)
                nc.vector.tensor_copy(xhat_t[:, :, :], pf[0:96, 0:2, 0:TOK]).then_inc(f_pe, 1)
                dve.wait_ge(res["f_in"], 16 * res["f_loads"])
                dve.wait_ge(routed, 1)
                raw = pf[:, 2, 0:TT * NE].rearrange("p (t e) -> p t e", t=TT)
                over = lambda x, n=8: x.unsqueeze(2).broadcast_to([P, TT, n])
                steps.done(nc.vector.tensor_reduce(peak[:, :], raw[:, :, 0:EXPERTS], AX.X, ALU.max))
                steps.settle()
                steps.done(nc.vector.tensor_tensor(logit[:, :, 0:EXPERTS], raw[:, :, 0:EXPERTS], over(peak[:, :]), ALU.subtract))
                nc.vector.tensor_scalar(logit[:, :, EXPERTS], raw[:, :, EXPERTS], gate_b[:, 0:1], -1.0, ALU.add, ALU.mult)\
                    .then_inc(logits_ready, 1)
                dve.wait_ge(f_exp, 1)
                steps.done(nc.vector.tensor_reduce(total[:, :], prob[:, :, 0:EXPERTS], AX.X, ALU.add))
                steps.done(nc.vector.tensor_scalar(peak[:, :], prob[:, :, EXPERTS], 1.0, None, ALU.add))
                steps.settle()
                steps.done(nc.vector.reciprocal(total[:, :], total[:, :]))
                steps.done(nc.vector.reciprocal(mix[:, :, 0], peak[:, :]))
                steps.settle()
                steps.done(nc.vector.tensor_tensor(prob[:, :, 0:EXPERTS], prob[:, :, 0:EXPERTS], over(total[:, :]), ALU.mult))
                steps.settle()
                for t in range(TT):
                    steps.done(nc.vector.max(top[:, t, :], prob[:, t, 0:EXPERTS]))
                steps.settle()
                for t in range(TT):
                    steps.done(nc.vector.max_index(where[:, t, :], top[:, t, :], prob[:, t, 0:EXPERTS]))
                steps.done(nc.vector.tensor_tensor(total[:, :], top[:, :, 0], top[:, :, 1], ALU.add))
                dve.wait_ge(iota_ready, 1)
                steps.done(nc.vector.tensor_copy(iota_f[:, :], iota_i[:, :]))
                steps.settle()
                steps.done(nc.vector.tensor_copy(wheref[:, :, :], where[:, :, :]))
                steps.done(nc.vector.reciprocal(peak[:, :], total[:, :]))
                steps.settle()
                steps.done(nc.vector.tensor_tensor(top[:, :, :], top[:, :, :], over(peak[:, :]), ALU.mult))
                each = iota_f[:, :].unsqueeze(1).broadcast_to([P, TT, 8])
                steps.done(nc.vector.tensor_tensor(one[:, :, :], each, over(wheref[:, :, 0]), ALU.is_equal))
                steps.done(nc.vector.tensor_tensor(two[:, :, :], each, over(wheref[:, :, 1]), ALU.is_equal))
                steps.done(nc.vector.tensor_scalar(total[:, :], mix[:, :, 0], -1.0, 1.0, ALU.mult, ALU.add))
                steps.settle()
                steps.done(nc.vector.tensor_tensor(one[:, :, :], one[:, :, :], over(top[:, :, 0]), ALU.mult))
                steps.done(nc.vector.tensor_tensor(two[:, :, :], two[:, :, :], over(top[:, :, 1]), ALU.mult))
                steps.settle()
                steps.done(nc.vector.tensor_tensor(one[:, :, :], one[:, :, :], two[:, :, :], ALU.add))
                steps.settle()
                steps.done(nc.vector.tensor_tensor(mix[:, :, 1:NE], one[:, :, :], over(total[:, :]), ALU.mult))
                for m in range(MT):
                    dve.wait_ge(silu_done, m + 1)
                    two_halves = lambda x: x.rearrange("p (n c) -> p n c", n=2)
                    nc.vector.tensor_tensor(two_halves(acts[:, m, :]), two_halves(silu[:, m % 2, :]),
                                            two_halves(pf[:, 2 * (m % 2) + 1, :])[:, :, 0:TOK // 2], ALU.mult).then_inc(act_ready, 1)
                steps.settle()
                for unit in range(NE):
                    for t in range(TT):
                        n = unit * TT + t
                        dve.wait_ge(down_ready, n + 1)
                        if unit:
                            dve.wait_ge(summed, n - TT + 1)
                        nc.vector.scalar_tensor_tensor(out=hidden[:, t, :], in0=pf[:, n % 8 // 2, (n % 2) * 512:(n % 2) * 512 + D],
                                                       scalar=mix[:, t, unit:unit + 1], in1=hidden[:, t, :],
                                                       op0=ALU.mult, op1=ALU.add).then_inc(summed, 1)


def shared_tensors(nc, ctx):
    sb = lambda n, s, d=F32: ctx.enter_context(nc.sbuf_tensor(n, s, d))
    return {"ident": sb("ident", [P, P]), "h6": sb("h6", [P, TOK]), "lnp": sb("lnp", [P, 16]),
            "hidden": sb("hidden", [P, TT, D])}


def expert_weights(nc, io, res, ctx):
    sb = lambda n, s, d=F32: ctx.enter_context(nc.sbuf_tensor(n, s, d))
    N = EXPERTS * HID + SHID
    res.update(gate_w=sb("gate_w", [96, KD, N]), up_w=sb("up_w", [96, KD, N]), down_w=sb("down_w", [P, N // P, D]),
               router_w=sb("router_w", [96, KD, EXPERTS + 1]), gate_b=sb("gate_b", [P, 1]),
               f_in=ctx.enter_context(nc.semaphore("experts_in")), f_loads=5)
    with nc.Block() as block:

        @block.sync
        def _(sp):
            halves = lambda x: x.rearrange("(k p) n -> p k n", k=KD)
            sp.dma_start(res["router_w"][:, :, :], halves(io["router_w"])).then_inc(res["f_in"], 16)
            sp.dma_start(res["gate_b"][:, :], io["gate_b"].partition_broadcast(P)).then_inc(res["f_in"], 16)
            sp.dma_start(res["gate_w"][:, :, :], halves(io["gate_w"])).then_inc(res["f_in"], 16)
            sp.dma_start(res["up_w"][:, :, :], halves(io["up_w"])).then_inc(res["f_in"], 16)
            sp.dma_start(res["down_w"][:, :, :], io["down_w"].rearrange("(t p) n -> p t n", p=P)).then_inc(res["f_in"], 16)


def audio_tower(nc, io):
    with ExitStack() as top:
        res = shared_tensors(nc, top)
        conv_tower(nc, io, res, top)
        expert_weights(nc, io, res, top)
        attention(nc, io, res, top)
        experts(nc, io, res, top)


def kernel(**a):
    import concourse.bacc as bacc
    from concourse.bass_utils import run_bass_kernel_spmd

    g = {k: np.asarray(v) for k, v in a.items()}
    conv = [g[f"L0_tok_conv_w{i}"] for i in range(7)]
    names = [(f"L0_tok_ln_g{i}", f"L0_tok_ln_b{i}") for i in range(7)] + [("L0_tok_fln_g", "L0_tok_fln_b")]
    by_hidden = lambda x: x.transpose(1, 0, 2).reshape(D, EXPERTS * HID)
    arrays = {
        "x": np.pad(g["x"], ((0, 0), (0, STRIDE0))),
        "w0": conv[0][:, 0, :],
        "w": np.concatenate([c.transpose(1, 2, 0) for c in conv[1:]], 1),
        "lnp": np.stack([g[n] for pair in names for n in pair], 1),
        "proj_w": g["L0_tok_proj_w"],
        "proj_b": g["L0_tok_proj_b"],
        "qkv_w": g["L0_attn_w_qkv"].T,
        "out_w": g["L0_attn_w_proj"].T,
        "out_b": g["L0_attn_b_proj"],
        "router_w": np.concatenate([g["L0_ffn_router_w"], g["L0_ffn_sg_w"]], 1),
        "gate_b": g["L0_ffn_sg_b"],
        "gate_w": np.concatenate([by_hidden(g["L0_ffn_w_gate"]), g["L0_ffn_ws_gate"]], 1),
        "up_w": np.concatenate([by_hidden(g["L0_ffn_w_up"]), g["L0_ffn_ws_up"]], 1),
        "down_w": np.concatenate([g["L0_ffn_w_down"].reshape(EXPERTS * HID, D), g["L0_ffn_ws_down"]], 0),
    }
    nc = bacc.Bacc("TRN2", target_bir_lowering=False, num_devices=1)
    io, sent = {}, {}
    for name, x in arrays.items():
        x = np.ascontiguousarray(x)
        sent[f"in_{name}"] = x
        io[name] = nc.dram_tensor(f"in_{name}", x.shape, mybir.dt.from_np(x.dtype), kind="ExternalInput").ap()
    io["out"] = nc.dram_tensor("out_tokens", (TOK, D), F32, kind="ExternalOutput").ap()
    audio_tower(nc, io)
    r = run_bass_kernel_spmd(nc, [sent], core_ids=[0])
    return r.results[0]["out_tokens"].reshape(BATCH, SEQ, D)
```

```python
from contextlib import ExitStack
from math import sqrt

import numpy as np
import concourse.bass as bass
from concourse import mybir

ALU = mybir.AluOpType
ACT = mybir.ActivationFunctionType
F32 = mybir.dt.float32
BF16 = mybir.dt.bfloat16
F32R = mybir.dt.float32r
I32 = mybir.dt.int32
U32 = mybir.dt.uint32
AX = mybir.AxisListType

P = 128
BATCH, SAMPLES = 64, 4000
CH = 128
K0, STRIDE0 = 10, 5
EPS = 1e-5
RSQRT_GUESS = float(0x5F3759DF)

GROUP = 8
ROUND = 2 * GROUP
ROUNDS = BATCH // ROUND
SPLIT_AHEAD = 3
HI_TURNS, LO_TURNS = 4, 2
AHEAD = GROUP + 1

POS0, ROW0 = 800, 802
SLICES = 8
SL = POS0 // SLICES
XROW = SAMPLES + STRIDE0
PARTS = 3


class Layer:

    def __init__(self, n, taps, pos, row, per_chunk, chunks, first_tap):
        self.n, self.taps, self.pos, self.row = n, taps, pos, row
        self.per_chunk = per_chunk
        self.chunks = chunks
        self.cols = per_chunk * pos
        self.w = self.cols // 4
        self.first_tap = first_tap


L1 = Layer(1, 3, 400, 402, 1, 8, 0)
L2 = Layer(2, 3, 200, 202, 2, 4, 3)
L3 = Layer(3, 3, 100, 102, 4, 2, 6)
L4 = Layer(4, 3, 50, 50, 8, 4, 9)
L5 = Layer(5, 2, 24, 24, 16, 2, 12)
L6 = Layer(6, 2, 12, 12, 16, 2, 14)
LAYERS = {x.n: x for x in (L1, L2, L3, L4, L5, L6)}
TAPS = 16

TOK = BATCH * L6.pos
TT = TOK // P
SEQ = L6.pos
D, HEADS, DH = 192, 12, 16
KD = D // 96
LANDMARKS = 64
PADS = LANDMARKS - SEQ
PINV_ITERS = 6
EXPERTS, HID, SHID = 8, 192, 768


class Steps:

    def __init__(self, eng, sem):
        self.eng, self.sem, self.base, self.n = eng, sem, 0, 0

    def done(self, ins):
        ins.then_inc(self.sem, 1)
        self.n += 1

    def settle(self):
        self.eng.wait_ge(self.sem, self.base + self.n)

    def at(self, base):
        self.base, self.n = base, 0


def newton_rsqrt(nc, steps, v, y, t, u):
    steps.done(nc.vector.tensor_scalar(y.bitcast(I32), v.bitcast(I32), -0.5, RSQRT_GUESS, ALU.mult, ALU.add))
    for _ in range(3):
        steps.settle()
        steps.done(nc.vector.tensor_tensor(t, v, y, ALU.mult))
        steps.settle()
        steps.done(nc.vector.scalar_tensor_tensor(out=u, in0=t, scalar=-0.5, in1=y, op0=ALU.mult, op1=ALU.mult))
        steps.settle()
        steps.done(nc.vector.scalar_tensor_tensor(out=y, in0=u, scalar=1.5, in1=y, op0=ALU.add, op1=ALU.mult))
    steps.settle()



def round_plan(last):
    order = []

    def conv(l, s, p, *between):
        order.append(("half", l, s, p))
        for step in between:
            step()
        order.append(("conv", l, s, p))

    def step(what, l, s, p=0):
        return lambda: order.append((what, l, s, p))

    var = lambda l, s, p: step("var", l, s, p)
    norm = lambda l, s: step("norm", l, s)
    rows = lambda l, s: step("rows", l, s)

    def scale(l, s, *chunks):
        def add():
            for c in chunks:
                order.append(("scale", l, s, c))
                if c % 2:
                    order.append(("gelu", l, s, c // 2))
        return add

    def first(batch):
        return step("first", 0, batch // GROUP, batch % GROUP)

    def ahead(*batches):
        def add():
            for b in batches:
                if not last:
                    order.append(("first", 1, b // GROUP, b % GROUP))
        return add

    def prep(a, b):
        for k in range(a, b):
            if not last:
                order.append(("prep", 0, 0, k))

    def split(*batches, of=0):
        def add():
            for b in batches:
                order.append(("split", of, b // GROUP, b % GROUP))
        return add

    split(3)()
    prep(0, 2)
    conv(1, 0, 0, first(9), split(4))
    prep(2, 4)
    split(5)()
    conv(1, 0, 1, first(10), split(6), var(1, 0, 0))
    prep(4, 7)
    split(7)()
    conv(1, 0, 2, first(11), split(8), var(1, 0, 1))
    prep(7, 11)
    split(9)()
    conv(1, 0, 3, first(12), split(10), var(1, 0, 2))
    prep(11, 12)
    split(11)()
    conv(1, 1, 0, first(13), split(12), var(1, 0, 3), norm(1, 0))
    prep(12, 13)
    split(13)()
    conv(1, 1, 1, first(14), split(14), rows(1, 0), var(1, 1, 0), scale(1, 0, 0, 1))
    scale(1, 0, 2, 3)()
    prep(13, 14)
    conv(1, 1, 2, first(15), split(15), var(1, 1, 1), scale(1, 0, 4, 5))
    scale(1, 0, 6, 7)()
    conv(1, 1, 3, var(1, 1, 2))
    conv(2, 0, 0, var(1, 1, 3), norm(1, 1))
    conv(2, 0, 1, rows(1, 1), var(2, 0, 0), scale(1, 1, 0, 1))
    scale(1, 1, 2, 3)()
    conv(2, 1, 0, ahead(0), scale(1, 1, 4, 5), var(2, 0, 1), norm(2, 0))
    scale(1, 1, 6, 7)()
    conv(2, 1, 1, ahead(1), rows(2, 0), var(2, 1, 0), scale(2, 0, 0, 1))
    scale(2, 0, 2, 3)()
    conv(3, 0, 0, ahead(2), var(2, 1, 1), norm(2, 1))
    ahead(3)()
    rows(2, 1)()
    ahead(4)()
    scale(2, 1, 0, 1)()
    var(3, 0, 0)()
    scale(2, 1, 2, 3)()
    norm(3, 0)()
    conv(3, 1, 0, rows(3, 0), scale(3, 0, 0, 1))
    if not last:
        ahead(5, 6)()
        var(3, 1, 0)()
        norm(3, 1)()
        ahead(7, 8)()
        split(*range(SPLIT_AHEAD), of=1)()
        rows(3, 1)()
        scale(3, 1, 0, 1)()
        return counted(order)
    conv(4, 0, 0, var(3, 1, 0), norm(3, 1))
    conv(4, 0, 1, rows(3, 1), var(4, 0, 0), scale(3, 1, 0, 1))
    conv(4, 1, 0, var(4, 0, 1), norm(4, 0))
    conv(4, 1, 1, rows(4, 0), scale(4, 0, 0, 1), var(4, 1, 0))
    scale(4, 0, 2, 3)()
    conv(5, 0, 0, var(4, 1, 1), norm(4, 1))
    rows(4, 1)()
    scale(4, 1, 0, 1)()
    var(5, 0, 0)()
    scale(4, 1, 2, 3)()
    norm(5, 0)()
    conv(5, 1, 0, rows(5, 0), scale(5, 0, 0, 1))
    conv(6, 0, 0, var(5, 1, 0), norm(5, 1))
    rows(5, 1)()
    scale(5, 1, 0, 1)()
    var(6, 0, 0)()
    norm(6, 0)()
    conv(6, 1, 0, rows(6, 0), scale(6, 0, 0, 1))
    var(6, 1, 0)()
    norm(6, 1)()
    rows(6, 1)()
    scale(6, 1, 0, 1)()
    return counted(order)


def counted(order):
    n = dict.fromkeys(("pair", "half", "conv", "var", "norm", "rows", "scale", "gelu", "first", "prep", "split"), 0)
    out, bank, held = [], 0, None
    users = [("first", -2), ("first", -1)]
    for what, l, s, p in order:
        step = dict(n)
        if what in ("half", "first"):
            step["bank"], step["before"] = bank, users[bank]
            if what == "first":
                users[bank] = ("first", n["pair"])
            else:
                users[bank] = ("conv", n["conv"])
                held = bank
            if held is None or what == "half":
                bank = 1 - bank
        elif what == "conv":
            step["bank"], held = held, None
        out.append((what, l, s, p, step))
        n[what] += 1
        n["pair"] += what in ("conv", "first")
    assert bank == 0 or not n["prep"]
    return out, n


class Origin:

    def __init__(self, rounds, per):
        self.pair = AHEAD + per["pair"] * rounds
        self.conv, self.sets = per["conv"] * rounds, per["norm"] * rounds
        self.split, self.halves = ROUND * rounds, GROUP * rounds
        self.scale, self.gelu = per["scale"] * rounds, per["gelu"] * rounds


def number_of(plan, what, layer, slot, p, kind):
    return next(n[kind] for a, b, c, d, n in plan if (a, b, c, d) == (what, layer, slot, p))


def gelus_before(plan, layer, slot):
    return {p: n["gelu"] for what, l, s, p, n in plan if (what, l, s) == ("gelu", layer, slot)}


def conv_tower(nc, io, res, top):
    body, per = round_plan(False)
    last, _ = round_plan(True)
    sem = lambda n: top.enter_context(nc.semaphore(n))
    x_in = sem("x_in")
    w_in = sem("w_in")
    s_const = sem("s_const")
    s_w0 = sem("s_w0")
    w0_in = sem("w0_in")
    weights_ready = sem("weights_ready")
    parts_ready = sem("parts_ready")
    parts_out = sem("parts_out")
    win_in = [sem("win_in0"), sem("win_in1")]
    y_ready = sem("y_ready")
    y_copied = sem("y_copied")
    y_taken = sem("y_taken")
    var_read = sem("var_read")
    var_done = sem("var_done")
    rstd_ready = sem("rstd_ready")
    rstd_turned = sem("rstd_turned")
    rows_ready = sem("rows_ready")
    bc_ready = sem("bc_ready")
    scaled = sem("scaled")
    gelu_done = sem("gelu_done")
    hi_done = sem("hi_done")
    lo_done = sem("lo_done")
    half_done = sem("half_done")
    steps_sem = sem("steps_sem")

    ident, h6, lnp = res["ident"], res["h6"], res["lnp"]
    with ExitStack() as ctx:
        sb = lambda n, s, d=F32: ctx.enter_context(nc.sbuf_tensor(n, s, d))
        ps = ctx.enter_context(nc.psum_tensor("ps", [P, 8, 512], F32))
        ypair = [ps[:, 0:2, :], ps[:, 2:4, :]]
        spread = [ps[:, 4, :], ps[:, 5, :]]
        var_ps = ps[:, 6, :]
        rows_ps = ps[:, 7, :].bitcast(BF16)

        h0 = sb("h0", [P, 2, GROUP, ROW0])
        h1 = sb("h1", [P, 2, GROUP, L1.row])
        h2 = sb("h2", [P, 2, GROUP, L2.row])
        h3 = sb("h3", [P, ROUNDS, 2, GROUP, L3.row])
        sq = sb("sq", [P, 2, 2, 400])
        late = sb("late", [P, ROUND * POS0 // 2])
        win = late[0:PARTS * PARTS * K0, :].bitcast(BF16)
        h4 = late[:, 0:BATCH * L4.row].rearrange("p (b t) -> p b t", t=L4.row)
        h5 = late[:, BATCH * L4.row:BATCH * (L4.row + L5.row)].rearrange("p (b t) -> p b t", t=L5.row)
        h0_hi, h0_lo = sb("h0_hi", [P, HI_TURNS, ROW0], F32R), sb("h0_lo", [P, LO_TURNS, ROW0], F32R)
        w1_hi, w1_lo = sb("w1_hi", [P, L1.taps, CH], F32R), sb("w1_lo", [P, L1.taps, CH], F32R)
        w = sb("w", [P, TAPS, CH])
        wmean = sb("wmean", [P, TAPS])
        w0 = sb("w0", [P, K0])
        w0_parts = sb("w0_parts", [K0, PARTS, CH], BF16)
        w0_rest = sb("w0_rest", [K0, CH])
        w0_stack = sb("w0_stack", [PARTS * PARTS * K0, CH], BF16)
        w0_pairs = sb("w0_pairs", [P, K0, K0])
        gram = sb("gram", [P, K0, K0])
        averager = sb("averager", [P, P])
        pick = sb("pick", [96, 8, P], BF16)
        ident16 = sb("ident16", [P, P], BF16)
        xs = sb("xs", [P, STRIDE0 * (SL + 1)])
        u = sb("u", [P, K0, SL])
        scaled_win = u
        parts = sb("parts", [P, PARTS, K0, SL], BF16)
        warm = sb("warm", [P, 1])
        v0, r0, t0, t1 = (sb(n, [P, SL]) for n in ("v0", "r0", "t0", "t1"))
        vs, rs, ts, us, rest = (sb(n, [100, 2, 32]) for n in ("vs", "rs", "ts", "us", "rest"))
        rparts = sb("rparts", [100, 2, 4, 96], BF16)
        rows = sb("rows", [96, 2, 400], BF16)

        windows_dram = nc.dram_tensor("windows_dram", [ROUNDS, PARTS * K0, ROUND * POS0], BF16, kind="Internal").ap()
        xwin = xs[:, :].rearrange("p (t k) -> p k t", k=STRIDE0)
        tap = lambda k: xwin[:, k % STRIDE0, k // STRIDE0:k // STRIDE0 + SL]

        def chunk(l, slot, c, r):
            L = LAYERS[l]
            a, n = c * L.per_chunk, L.per_chunk
            if l >= 4:
                a += slot * BATCH // 2
            if l <= 2:
                return (h1, h2)[l - 1][:, slot, a:a + n, 0:L.pos]
            if l == 3:
                return h3[:, bass.ds(r, 1), slot, a:a + n, 0:L.pos].rearrange("p o b t -> p (o b) t")
            if l == 4:
                return h4[:, a:a + n, 0:L.pos]
            if l == 5:
                return h5[:, a:a + n, 0:L.pos]
            return h6[:, :].rearrange("p (b t) -> p b t", t=L.pos)[:, a:a + n, :]

        def source(l, slot, c, t):
            L = LAYERS[l]
            a, n = c * L.per_chunk, L.per_chunk
            if l >= 4:
                a += slot * BATCH // 2
            cut = slice(t, t + 2 * L.pos - 1, 2)
            if l <= 3:
                return (h0, h1, h2)[l - 1][:, slot, a:a + n, cut]
            if l == 4:
                return h3[:, :, :, :, :].rearrange("p r s b t -> p (r s b) t")[:, a:a + n, cut]
            return (h4, h5)[l - 5][:, a:a + n, cut]

        def batch_taken(plan, r, o, batch, of=0):
            s, b = batch // GROUP, batch % GROUP
            if of == 1:
                return o.pair + number_of(plan, "first", 1, s, b, "pair") + 1
            if batch >= AHEAD:
                return o.pair + number_of(plan, "first", 0, s, b, "pair") + 1
            if isinstance(r, int) and r == 0:
                return batch + 1
            return o.pair - per["pair"] + number_of(body, "first", 1, s, b, "pair") + 1

        def wait_batch_read(eng, plan, r, o, batch):
            if batch < 0 and isinstance(r, int) and r == 0:
                return
            of, base, halves = (plan, o.pair, o.halves) if batch >= 0 else (body, o.pair - per["pair"], o.halves - GROUP)
            b = batch % ROUND
            if batch >= ROUND:
                assert b % 2 == 0
                eng.wait_ge(half_done, o.halves + GROUP + b // 2 + 1)
            elif b % 2:
                eng.wait_ge(y_ready, base + number_of(of, "conv", 1, b // GROUP, b % GROUP // 2, "pair") + 1)
            else:
                eng.wait_ge(half_done, halves + b // 2 + 1)

        def for_rounds(eng, run):
            run(body, 0, Origin(0, per))
            with eng.Fori(1, ROUNDS - 1) as r:
                run(body, r, Origin(r, per))
            run(last, ROUNDS - 1, Origin(ROUNDS - 1, per))

        def joined(l, s, p, r):
            L = LAYERS[l]
            a, n = 2 * p * L.per_chunk, 2 * L.per_chunk
            if l >= 4:
                a += s * BATCH // 2
            if l <= 2:
                return (h1, h2)[l - 1][:, s, a:a + n, 0:L.pos]
            if l == 3:
                return h3[:, bass.ds(r, 1), s, a:a + n, 0:L.pos].rearrange("p o b t -> p (o b) t")
            if l == 4:
                return h4[:, a:a + n, 0:L.pos]
            if l == 5:
                return h5[:, a:a + n, 0:L.pos]
            return h6[:, :].rearrange("p (b t) -> p b t", t=L.pos)[:, a:a + n, :]

        with nc.Block() as block:

            @block.sync
            def _(sp):
                def samples(r):
                    b0 = ROUND * r
                    src = io["x"][bass.ds(b0, ROUND), :]
                    lanes = bass.AP(src.tensor, src.offset, [[XROW, ROUND], [STRIDE0 * SL, SLICES], [1, STRIDE0 * (SL + 1)]])
                    sp.dma_start(xs[:, :], lanes).then_inc(x_in, 16)

                def windows(r, more):
                    scratch = windows_dram[bass.ds(r, 1), :, :].rearrange("o k c -> (o k) c")
                    for a in range(PARTS):
                        sp.wait_ge(parts_ready, PARTS * r + a + 1)
                        sp.dma_start(scratch[a * K0:(a + 1) * K0, :].rearrange("k (l t) -> l k t", t=SL),
                                     parts[:, a, :, :]).then_inc(parts_out, 16)
                        if more and a == 0:
                            samples(r + 1)
                    sp.wait_ge(parts_out, 16 * PARTS * (r + 1))
                    return scratch

                def back(scratch, slot):
                    cut = slice(slot * GROUP * POS0, (slot + 1) * GROUP * POS0)
                    for a in range(PARTS):
                        sp.dma_start(win[a * PARTS * K0:(a + 1) * PARTS * K0, cut], scratch[:, cut]).then_inc(win_in[slot], 16)

                samples(0)
                sp.dma_start(w0[:, :], io["w0"]).then_inc(w_in, 16)
                sp.dma_start(lnp[:, :], io["lnp"]).then_inc(w_in, 16)
                sp.dma_start(w[:, :, :], io["w"]).then_inc(w_in, 16)
                sp.wait_ge(s_w0, 5)
                for a in range(PARTS):
                    for b in range(PARTS):
                        row = (a * PARTS + b) * K0
                        sp.dma_start(w0_stack[row:row + K0, :], w0_parts[:, a, :]).then_inc(w0_in, 16)
                scratch = windows(0, True)
                back(scratch, 0)
                back(scratch, 1)
                attention_weights(sp, io, res)

                read = number_of(body, "first", 0, 1, GROUP - 1, "pair") + 1

                def middle(r, more):
                    scratch = windows(r, more)
                    sp.wait_ge(y_ready, AHEAD + per["pair"] * (r - 1))
                    back(scratch, 0)
                    sp.wait_ge(y_ready, AHEAD + per["pair"] * (r - 1) + read)
                    back(scratch, 1)

                with sp.Fori(1, ROUNDS - 1) as r:
                    middle(r, True)
                middle(ROUNDS - 1, False)

            @block.gpsimd
            def _(pool):
                pool.memset(averager[:, :], 1.0 / CH).then_inc(s_const, 1)
                pool.memset(ident[:, :], 0.0).then_inc(s_const, 1)
                pool.memset(ident16[:, :], 0.0).then_inc(s_const, 1)
                pool.memset(pick[:, :, :], 0.0).then_inc(s_const, 1)
                pool.memset(rparts[:, :, :, :], 0.0).then_inc(s_const, 1)
                pool.memset(h0[:, :, :, POS0:ROW0], 0.0).then_inc(s_const, 1)
                pool.memset(h1[:, :, :, L1.pos:L1.row], 0.0).then_inc(s_const, 1)
                pool.memset(h2[:, :, :, L2.pos:L2.row], 0.0).then_inc(s_const, 1)
                pool.memset(h3[:, :, :, :, L3.pos:L3.row], 0.0).then_inc(s_const, 1)
                pool.wait_ge(s_const, 4)
                for m in (ident, ident16):
                    pool.affine_select(out=m[:, :], in_=m[:, :], compare_op=ALU.not_equal, fill=1.0, base=0,
                                       pattern=[[-1, P]], channel_multiplier=1).then_inc(s_const, 1)
                for a in range(PARTS):
                    if a:
                        pool.wait_ge(s_const, 11 + a)
                    pool.affine_select(out=pick[:, :, :], in_=pick[:, :, :], compare_op=ALU.not_equal, fill=1.0,
                                       base=-32 * a, pattern=[[-1, 8], [0, P]], channel_multiplier=1).then_inc(s_const, 1)

                def left(g, batch):
                    s, b = batch // GROUP, batch % GROUP
                    pool.tensor_tensor(h0_lo[:, g % LO_TURNS, :], h0[:, s, b, :], h0_hi[:, g % HI_TURNS, :].bitcast(F32),
                                       ALU.subtract).then_inc(lo_done, 1)

                for b in range(SPLIT_AHEAD):
                    pool.wait_ge(hi_done, b + 1)
                    if b >= LO_TURNS:
                        pool.wait_ge(half_done, b // LO_TURNS)
                    left(b, b)

                def run(plan, r, o):
                    for what, of, s, b, n in plan:
                        if what == "split":
                            number, batch = n["split"] + SPLIT_AHEAD, GROUP * s + b
                            pool.wait_ge(hi_done, o.split + number + 1)
                            wait_batch_read(pool, plan, r, o, number - LO_TURNS)
                            left(number, batch)

                for_rounds(pool, run)

            CONSTS = 14
            SLOT_IN = 16 * PARTS

            @block.tensor
            def _(pe):
                pe.wait_ge(s_const, CONSTS)
                pe.wait_ge(w_in, 48)
                pe.matmul(spread[0][:, 0:K0], averager[:, :], w0[:, :], start=True, stop=True).then_inc(s_w0, 1)
                pe.wait_ge(s_w0, 3)
                pe.matmul(spread[1][:, 0:K0 * K0], averager[:, :], w0_pairs[:, :, :], start=True, stop=True).then_inc(s_w0, 1)
                pe.transpose(ps[0:K0, 6, 0:CH], w0[:, :], ident[:, :]).then_inc(weights_ready, 1)

                def first(b, bank):
                    for h in range(2):
                        mm = pe.matmul(ypair[bank][:, h, 0:400], w0_stack[:, :],
                                       win[:, b * POS0 + h * 400:b * POS0 + h * 400 + 400], start=True, stop=True)
                    mm.then_inc(y_ready, 1)

                pe.wait_ge(w0_in, 16 * PARTS * PARTS)
                for b in range(AHEAD):
                    if b % GROUP == 0:
                        pe.wait_ge(win_in[b // GROUP], SLOT_IN)
                    if b >= 2:
                        pe.wait_ge(y_taken, b - 1)
                    first(b, (b + AHEAD) % 2)
                pe.wait_ge(weights_ready, 2)

                def run(plan, r, o):
                    for what, l, s, p, n in plan:
                        L = LAYERS.get(l)
                        if what in ("half", "first"):
                            user, number = n["before"]
                            if user == "first":
                                pe.wait_ge(y_taken, o.pair + number + 1)
                            else:
                                pe.wait_ge(y_copied, o.conv + number + 1)
                        if what == "first":
                            if l == 1 and p == 0:
                                pe.wait_ge(win_in[s], SLOT_IN * (r + 2))
                            first(s * GROUP + p, n["bank"])
                        elif what in ("half", "conv"):
                            c = int(what == "conv")
                            if l == 1:
                                pe.wait_ge(lo_done, o.split + GROUP * s + 2 * p + c + 1)
                            elif l == 4:
                                behind = 0 if (s, p) < (1, 1) else gelus_before(plan, 3, 1)[0] + 1
                                pe.wait_ge(gelu_done, o.gelu + behind)
                            else:
                                done = gelus_before(plan, l - 1, s)
                                pe.wait_ge(gelu_done, o.gelu + done[min(2 * p + c, max(done))] + 1)
                            out = ypair[n["bank"]][:, c, 0:L.cols].rearrange("p (b t) -> p b t", t=L.pos)
                            if l == 1:
                                hi, lo = h0_hi[:, (2 * p + c) % HI_TURNS, :], h0_lo[:, c % LO_TURNS, :]
                                products = [(a, b, t) for a, b in ((w1_hi, hi), (w1_lo, hi), (w1_hi, lo)) for t in range(L.taps)]
                                for j, (a, b, t) in enumerate(products):
                                    mm = pe.matmul(ypair[n["bank"]][:, c, 0:L.cols], a[:, t, :], b[:, t:t + 2 * L.pos - 1:2],
                                                   start=(j == 0), stop=(j == len(products) - 1))
                                if not c:
                                    mm.then_inc(half_done, 1)
                            else:
                                for t in range(L.taps):
                                    mm = pe.matmul(out, w[:, L.first_tap + t, :], source(l, s, 2 * p + c, t),
                                                   start=(t == 0), stop=(t == L.taps - 1))
                            if c:
                                mm.then_inc(y_ready, 1)
                        elif what == "var":
                            pe.wait_ge(y_taken, o.pair + number_of(plan, "conv", l, s, p, "pair") + 1)
                            before = o.sets + n["norm"]
                            if p == 0 and not (isinstance(before, int) and before < 1):
                                pe.wait_ge(var_read, before)
                            for c in range(2):
                                for q in range(4):
                                    at = q * L.chunks + 2 * p + c
                                    mm = pe.matmul(var_ps[0:L.w, at:at + 1],
                                                   sq[:, n["var"] % 2, c, q * L.w:(q + 1) * L.w], averager[:, 0:1],
                                                   start=True, stop=True)
                            mm.then_inc(var_done, 1)
                        elif what == "rows":
                            pe.wait_ge(rstd_ready, o.sets + n["rows"] + 1)
                            for q in range(4):
                                mm = pe.transpose(rows_ps[0:96, q * L.w:(q + 1) * L.w],
                                                  rparts[0:L.w, s, q, :], ident16[0:L.w, 0:L.w])
                            mm.then_inc(rstd_turned, 1)
                        elif what == "scale":
                            if p == 0:
                                pe.wait_ge(rows_ready, o.sets + n["rows"])
                            used = o.scale + n["scale"] - 1
                            if not (isinstance(used, int) and used < 1):
                                pe.wait_ge(scaled, used)
                            pe.matmul(spread[n["scale"] % 2][:, 0:L.cols], pick[:, p, :],
                                      rows[:, s, 0:L.cols], start=True, stop=True).then_inc(bc_ready, 1)

                for_rounds(pe, run)

            @block.scalar
            def _(act):
                act.wait_ge(w_in, 48)

                def first(s, p, b, pair):
                    act.wait_ge(y_ready, pair + 1)
                    act.activation(h0[:, s, p, 0:POS0].rearrange("p (h t) -> p h t", h=2), ypair[b][:, :, 0:400],
                                   ACT.Gelu, scale=lnp[:, 0:1], bias=lnp[:, 1:2]).then_inc(y_taken, 1)

                def rounded(g, batch):
                    act.copy(h0_hi[:, g % HI_TURNS, :], h0[:, batch // GROUP, batch % GROUP, :]).then_inc(hi_done, 1)

                act.wait_ge(s_const, CONSTS)
                act.activation(warm[:, :], ident[:, 0:1], ACT.Gelu)
                for b in range(AHEAD):
                    first(b // GROUP, b % GROUP, (b + AHEAD) % 2, b)
                    if 0 < b <= SPLIT_AHEAD:
                        act.wait_ge(y_taken, b)
                        rounded(b - 1, b - 1)

                def run(plan, r, o):
                    for what, l, s, p, n in plan:
                        L = LAYERS.get(l)
                        if what == "first":
                            first(s, p, n["bank"], o.pair + n["pair"])
                        elif what == "split":
                            number, batch = n["split"] + SPLIT_AHEAD, GROUP * s + p
                            act.wait_ge(y_taken, batch_taken(plan, r, o, batch, l))
                            wait_batch_read(act, plan, r, o, number - HI_TURNS)
                            rounded(number, batch)
                        elif what == "conv":
                            act.wait_ge(y_copied, o.conv + n["conv"] + 1)
                            used = o.conv + n["conv"] - 1
                            if not (isinstance(used, int) and used < 1):
                                act.wait_ge(var_done, used)
                            if l == 3:
                                act.nop(nofuse=True)
                            act.activation(sq[:, n["conv"] % 2, :, 0:L.cols].rearrange("p c (b t) -> p c b t", t=L.pos),
                                           joined(l, s, p, r).rearrange("p (c b) t -> p c b t", c=2), ACT.Square).then_inc(y_taken, 1)
                        elif what == "gelu":
                            act.wait_ge(scaled, o.scale + n["scale"])
                            if l == 3:
                                act.nop(nofuse=True)
                            both = joined(l, s, p, r)
                            act.activation(both, both, ACT.Gelu, scale=lnp[:, 2 * l:2 * l + 1],
                                           bias=lnp[:, 2 * l + 1:2 * l + 2]).then_inc(gelu_done, 1)

                for_rounds(act, run)

            @block.vector
            def _(dve):
                steps = Steps(dve, steps_sem)
                dve.wait_ge(s_w0, 1)
                nc.vector.tensor_tensor(w0[:, :], w0[:, :], spread[0][:, 0:K0], ALU.subtract).then_inc(s_w0, 1)
                dve.wait_ge(s_w0, 2)
                nc.vector.tensor_tensor(w0_pairs[:, :, :], w0[:, :].unsqueeze(2).broadcast_to([P, K0, K0]),
                                        w0[:, :].unsqueeze(1).broadcast_to([P, K0, K0]), ALU.mult).then_inc(s_w0, 1)
                dve.wait_ge(s_w0, 4)
                steps.done(nc.vector.tensor_scalar(gram[:, :, :], spread[1][:, 0:K0 * K0].rearrange("p (a b) -> p a b", a=K0), 2.0, None, ALU.mult))
                dve.wait_ge(weights_ready, 1)
                turned = ps[0:K0, 6, 0:CH]
                steps.done(nc.vector.tensor_copy(w0_parts[:, 0, :], turned))
                steps.settle()
                steps.done(nc.vector.tensor_tensor(w0_rest[:, :], turned, w0_parts[:, 0, :], ALU.subtract))
                steps.settle()
                steps.done(nc.vector.tensor_copy(w0_parts[:, 1, :], w0_rest[:, :]))
                steps.settle()
                nc.vector.tensor_tensor(w0_parts[:, 2, :], w0_rest[:, :], w0_parts[:, 1, :], ALU.subtract).then_inc(s_w0, 1)

                def prepare(r, part):
                    if part == 0:
                        dve.wait_ge(x_in, 16 * (r + 1))
                    if part < K0:
                        steps.settle()
                        for k in range(K0 - part):
                            l = k + part
                            if part == 0:
                                steps.done(nc.vector.tensor_scalar(u[:, k, :], tap(l), gram[:, k, l:l + 1], 0.5, ALU.mult, ALU.mult))
                            else:
                                steps.done(nc.vector.scalar_tensor_tensor(out=u[:, k, :], in0=tap(l), scalar=gram[:, k, l:l + 1],
                                                                          in1=u[:, k, :], op0=ALU.mult, op1=ALU.add))
                    elif part == K0:
                        steps.settle()
                        for h in range(2):
                            steps.done(nc.vector.tensor_tensor(u[:, 5 * h:5 * h + 5, :], u[:, 5 * h:5 * h + 5, :],
                                                               xwin[:, :, h:h + SL], ALU.mult))
                        steps.settle()
                        steps.done(nc.vector.tensor_reduce(v0[:, :], u[:, :, :].rearrange("p k t -> p t k"), AX.X, ALU.add))
                        steps.settle()
                        steps.done(nc.vector.tensor_scalar(v0[:, :], v0[:, :], 0.0, EPS, ALU.max, ALU.add))
                        steps.settle()
                    elif part == K0 + 1:
                        newton_rsqrt(nc, steps, v0[:, :], r0[:, :], t0[:, :], t1[:, :])
                    elif part == K0 + 2:
                        for h in range(2):
                            steps.done(nc.vector.tensor_tensor(scaled_win[:, 5 * h:5 * h + 5, :], xwin[:, :, h:h + SL],
                                                               r0[:, :].unsqueeze(1).broadcast_to([P, 5, SL]), ALU.mult))
                        steps.settle()
                        if not (isinstance(r, int) and r == 0):
                            dve.wait_ge(parts_out, 16 * PARTS * r)
                        nc.vector.tensor_copy(parts[:, 0, :, :], scaled_win[:, :, :]).then_inc(parts_ready, 1)
                        dve.wait_ge(parts_ready, PARTS * r + 1)
                    else:
                        steps.done(nc.vector.tensor_tensor(scaled_win[:, :, :], scaled_win[:, :, :], parts[:, 0, :, :], ALU.subtract))
                        steps.settle()
                        nc.vector.tensor_copy(parts[:, 1, :, :], scaled_win[:, :, :]).then_inc(parts_ready, 1)
                        dve.wait_ge(parts_ready, PARTS * r + 2)
                        nc.vector.tensor_tensor(parts[:, 2, :, :], scaled_win[:, :, :], parts[:, 1, :, :],
                                                ALU.subtract).then_inc(parts_ready, 1)

                PREP = K0 + 4
                steps.settle()
                for part in range(PREP):
                    prepare(0, part)
                dve.wait_ge(w_in, 48)
                steps.done(nc.vector.tensor_reduce(wmean[:, :], w[:, :, :], AX.X, ALU.add))
                steps.settle()
                steps.done(nc.vector.tensor_scalar(wmean[:, :], wmean[:, :], 1.0 / CH, None, ALU.mult))
                steps.settle()
                steps.done(nc.vector.tensor_tensor(w[:, :, :], w[:, :, :], wmean[:, :].unsqueeze(2).broadcast_to([P, TAPS, CH]),
                                                   ALU.subtract))
                steps.settle()
                steps.done(nc.vector.tensor_copy(w1_hi[:, :, :], w[:, 0:L1.taps, :]))
                steps.settle()
                nc.vector.tensor_tensor(w1_lo[:, :, :], w[:, 0:L1.taps, :], w1_hi[:, :, :].bitcast(F32),
                                        ALU.subtract).then_inc(weights_ready, 1)
                dve.wait_ge(s_const, CONSTS)

                def run(plan, r, o):
                    for what, l, s, p, n in plan:
                        L = LAYERS.get(l)
                        if what == "conv":
                            dve.wait_ge(y_ready, o.pair + n["pair"] + 1)
                            nc.vector.tensor_copy(
                                joined(l, s, p, r).rearrange("p (c b) t -> p c b t", c=2),
                                ypair[n["bank"]][:, :, 0:L.cols].rearrange("p c (b t) -> p c b t", t=L.pos)).then_inc(y_copied, 1)
                        elif what == "prep":
                            prepare(r + 1, p)
                        elif what == "norm":
                            k, sl, wide = 4 * L.chunks, s, L.w
                            v, y, t, q, left = (x[0:wide, sl, 0:k] for x in (vs, rs, ts, us, rest))
                            part = lambda a: rparts[0:wide, sl, :, 32 * a:32 * a + L.chunks]
                            four = lambda x: x.rearrange("p (q c) -> p q c", q=4)
                            dve.wait_ge(var_done, o.conv + n["var"])
                            nc.vector.tensor_scalar(v, var_ps[0:wide, 0:k], EPS, None, ALU.add).then_inc(var_read, 1)
                            dve.wait_ge(var_read, o.sets + n["norm"] + 1)
                            newton_rsqrt(nc, steps, v, y, t, q)
                            steps.done(nc.vector.tensor_copy(part(0), four(y)))
                            steps.settle()
                            steps.done(nc.vector.tensor_tensor(four(left), four(y), part(0), ALU.subtract))
                            steps.settle()
                            steps.done(nc.vector.tensor_copy(part(1), four(left)))
                            steps.settle()
                            nc.vector.tensor_tensor(part(2), four(left), part(1), ALU.subtract).then_inc(rstd_ready, 1)
                        elif what == "rows":
                            dve.wait_ge(rstd_turned, o.sets + n["rows"] + 1)
                            nc.vector.tensor_copy(rows[:, s, 0:L.cols],
                                                  rows_ps[0:96, 0:L.cols]).then_inc(rows_ready, 1)
                        elif what == "scale":
                            dve.wait_ge(bc_ready, o.scale + n["scale"] + 1)
                            if p % 2 == 0:
                                dve.wait_ge(y_copied, o.conv + number_of(plan, "conv", l, s, p // 2, "conv") + 1)
                            h = chunk(l, s, p, r)
                            nc.vector.tensor_tensor(h, h, spread[n["scale"] % 2][:, 0:L.cols].rearrange(
                                "p (b t) -> p b t", t=L.pos), ALU.mult).then_inc(scaled, 1)

                start = steps.n
                run(body, 0, Origin(0, per))
                each = steps.n - start
                with dve.Fori(1, ROUNDS - 1) as r:
                    steps.at(start + each * r)
                    run(body, r, Origin(r, per))
                    assert steps.n == each
                steps.at(start + each * (ROUNDS - 1))
                run(last, ROUNDS - 1, Origin(ROUNDS - 1, per))



class RowSums:

    def __init__(self, terms, width, sum_pe, sum_pe_pool, by_vector, by_pool, first, second, out, mirror=None):
        self.batches = [sum_pe + sum_pe_pool] if mirror else [sum_pe, sum_pe_pool]
        self.terms, self.width = terms, width
        self.sum_pe, self.sum_pe_pool, self.by_vector, self.by_pool = sum_pe, sum_pe_pool, by_vector, by_pool
        self.first, self.second, self.out, self.mirror = first, second, out, mirror
        self.reduced = by_vector + by_pool
        self.pooled = len(sum_pe_pool) + len(by_pool)

    def places(self, rows):
        at, out = 0, {}
        for i in rows:
            out[i] = slice(at, at + self.width(i))
            at += self.width(i)
        return out, at

    def by_term(self, buffers, i):
        batch = next(n for n, rows in enumerate(self.batches) if i in rows)
        places, wide = self.places(self.batches[batch])
        full = buffers[batch][:, 0:self.terms * wide].rearrange("p (k n) -> p k n", k=self.terms)[:, :, places[i]]
        return full.rearrange("p k (a b) -> p a b k", a=self.first(i).shape[1])

    def copies(self, bank, rows):
        places, wide = self.places(rows)
        for i in rows:
            src = bank[:, places[i]].rearrange("p (a b) -> p a b", a=self.first(i).shape[1])
            yield self.out(i), src
            if self.mirror and self.mirror(i) is not None:
                yield self.mirror(i)[0], src[:, :, 1:]

    def mirrors(self):
        return [i for i in self.reduced if self.mirror and self.mirror(i) is not None]

    def copied(self):
        batch = list(self.sum_pe) + list(self.sum_pe_pool)
        return len(batch) + (sum(self.mirror(i) is not None for i in batch) if self.mirror else 0) + len(self.mirrors())


class Before:

    def __init__(self, jobs=0, sums=0, reduced=0, copied=0, pooled=0):
        self.jobs, self.sums, self.reduced, self.copied, self.pooled = jobs, sums, reduced, copied, pooled

    def after(self, *jobs, times=1):
        add = lambda f: sum(f(j) for j in jobs)
        return Before(self.jobs + len(jobs) * times, self.sums + add(lambda j: len(j.batches)) * times, self.reduced + add(lambda j: len(j.reduced)) * times,
                      self.copied + add(lambda j: j.copied()) * times, self.pooled + add(lambda j: j.pooled) * times)


def normalise(nc, steps, src, dst, stats, mv, y, t, u):
    for i in range(TT):
        steps.done(nc.vector.bn_stats(stats[:, i, :], src[i]))
    steps.settle()
    for i in range(TT):
        steps.done(nc.vector.bn_aggr(mv[:, i, :], stats[:, i, :]))
    steps.settle()
    steps.done(nc.vector.tensor_scalar(mv[:, :, 1], mv[:, :, 1], EPS, None, ALU.add))
    steps.settle()
    steps.done(nc.vector.tensor_copy(stats[:, :, 0], mv[:, :, 1]))
    steps.settle()
    newton_rsqrt(nc, steps, stats[:, :, 0], y, t, u)
    for i in range(TT):
        steps.done(nc.vector.tensor_scalar(dst[i], src[i], mv[:, i, 0:1], y[:, i:i + 1], ALU.subtract, ALU.mult))
    steps.settle()


def turn(pe, ps, src, ident, done):
    for k in range(KD):
        for t in range(TT):
            mm = pe.transpose(ps[0:96, k, t * P:(t + 1) * P], src[:, t, 96 * k:96 * k + 96], ident[:, :])
    mm.then_inc(done, 1)


def attention(nc, io, res, top):
    sem = lambda n: top.enter_context(nc.semaphore(n))
    a_in = res["attention_in"]
    turned = sem("turned")
    a_steps = sem("a_steps")
    to_pe = sem("to_pe")
    projected = sem("projected")
    qkv_ready = sem("qkv_ready")
    qkv_copied = [sem("qkv_copied0"), sem("qkv_copied1")]
    scores_ready = sem("scores_ready")
    exp_done = sem("exp_done")
    peaks = sem("peaks")
    eye_ready = sem("eye_ready")
    multiplied = sem("multiplied")
    pool_multiplied = sem("pool_multiplied")
    pe_summed = sem("pe_summed")
    row_done = sem("row_done")
    copied = sem("copied")
    cubic_ready = sem("cubic_ready")
    share_ready = sem("share_ready")
    e_ready = sem("e_ready")
    out_lanes = sem("out_lanes")
    heads_ready = sem("heads_ready")
    R = SEQ + 1
    HL = HEADS // 2
    ROOT = sqrt(PADS)
    ident, h6, lnp, hidden = (res[k] for k in ("ident", "h6", "lnp", "hidden"))
    with ExitStack() as ctx:
        sb = lambda n, s, d=F32: ctx.enter_context(nc.sbuf_tensor(n, s, d))
        pt = ctx.enter_context(nc.psum_tensor("pt", [P, 4, 1024], F32))
        proj_w, qkv_w, out_w, proj_b, out_b = (res[k] for k in ("proj_w", "qkv_w", "out_w", "proj_b", "out_b"))
        stats, mv = sb("a_stats", [P, TT, 6]), sb("a_mv", [P, TT, 2])
        y6, t6, u6 = sb("a_y6", [P, TT]), sb("a_t6", [P, TT]), sb("a_u6", [P, TT])
        xhat_t = sb("a_xhat_t", [96, KD, TOK])
        lanes = sb("lanes", [P, SEQ, 3, HL * DH])
        rowt = sb("rowt", [P, 2, HL * R * DH])
        for_pe = sb("for_pe", [P, 3 * HL * R * DH])
        norm6 = for_pe[:, 0:TOK].rearrange("p (t c) -> p t c", t=TT)
        norm6t = for_pe[:, TOK:2 * TOK]
        xhat = for_pe[:, 2 * TOK:2 * TOK + TT * D].rearrange("p (t c) -> p t c", t=TT)
        pool_for_pe = sb("pool_for_pe", [P, 3 * HL * R * DH])
        sum_buffers = [for_pe, pool_for_pe]
        from_pool = sb("from_pool", [P, 2 * HL * R * DH])
        scores = sb("scores", [P, HL, SEQ, SEQ])
        peak, epad, den, rden = (sb(n, [P, HL, SEQ]) for n in ("peak", "epad", "den", "rden"))
        smat = sb("smat", [P, HL, R, R])
        e1, e2, c4 = (sb(n, [P, HL, R, R]) for n in ("e1", "e2", "c4"))
        e34 = sb("e34", [P, HL, R, R])
        eye = sb("eye", [P, R, R])
        norms, all_norms, scale = sb("norms", [P, 2]), sb("all_norms", [P, 2]), sb("scale", [P, 2])
        padsum = sb("padsum", [P, HL])
        wv = sb("wv", [P, HL, R, DH])
        attn = sb("attn", [P, SEQ, HL * DH])
        warm = sb("a_warm", [P, 1])
        q_l, k_l, v_l = (lanes[:, :, a, :] for a in range(3))
        LOADS = 5
        grid = lambda x: x.rearrange("p (h d) -> p h d", d=DH)

        scoring = RowSums(DH, lambda i: HL * SEQ, [0, 1, 2], [3, 4, 5], [6, 7, 8, 9], [10, 11],
                          lambda i: grid(q_l[:, i, :]).unsqueeze(2).broadcast_to([P, HL, SEQ, DH]),
                          lambda i: k_l.rearrange("p j (h d) -> p h j d", d=DH), lambda i: scores[:, :, i, :])
        valuing = RowSums(SEQ, lambda i: HL * DH, [0, 1, 2], [3, 4, 5], [6, 7, 8, 9, 10], [11, 12],
                          lambda i: smat[:, :, i, 1:R].unsqueeze(2).broadcast_to([P, HL, DH, SEQ]),
                          lambda i: v_l.rearrange("p j (h d) -> p h d j", d=DH), lambda i: wv[:, :, i, :])
        applying = RowSums(R, lambda i: HL * DH, [0, 1, 2], [3, 4, 5], [6, 7, 8, 9], [10, 11],
                           lambda i: e1[:, :, i + 1, :].unsqueeze(2).broadcast_to([P, HL, DH, R]),
                           lambda i: wv[:, :, :, :].rearrange("p h k d -> p h d k"), lambda i: grid(attn[:, i, :]))

        def product(a, b, out):
            return RowSums(R, lambda i: HL * (R - i), [0, 1], [3], [4, 5, 6], [2, 7, 8, 9, 10, 11, 12],
                           lambda i: a[:, :, i, :].unsqueeze(2).broadcast_to([P, HL, R - i, R]),
                           lambda i: b[:, :, i:R, :], lambda i: out[:, :, i, i:R],
                           lambda i: (out[:, :, i + 1:R, i], out[:, :, i, i + 1:R]) if i < R - 1 else None)

        outer, squaring, closing = product(smat, smat, e2), product(e1, e1, e2), product(e2, c4, e1)
        at_scoring = Before()
        at_valuing = at_scoring.after(scoring)
        at_outer = at_valuing.after(valuing)
        at_first = at_outer.after(outer)
        at_iteration = lambda n: at_first.after(squaring, closing, times=n)
        at_applying = at_iteration(PINV_ITERS)

        lined = lambda x: x[:, :, :, :].rearrange("p h i j -> p (h i j)")

        def to_lanes(t, odd, half):
            return (lanes[half * BATCH:(half + 1) * BATCH, 2 * t + odd, :, :].rearrange("p a c -> p (a c)"),
                    pt[odd * BATCH:(odd + 1) * BATCH, 2 + t % 2, half * 512:half * 512 + 3 * HL * DH])

        def heads_turned(positions, half):
            n = SEQ // 2
            return (xhat_t[:, half, :].rearrange("p (b i) -> p i b", i=SEQ)[:, positions * n:(positions + 1) * n, :],
                    pt[0:96, positions, 0:n * P].rearrange("p (i g b) -> p g i b", g=2, b=BATCH)[:, half, :, :])

        def pooled_row(job, i):
            at = job.places(job.by_pool)[0][i].start * job.terms
            size = job.width(i) * job.terms
            return from_pool[:, at:at + size].rearrange("p (a b k) -> p a b k", a=job.first(i).shape[1], k=job.terms)

        with nc.Block() as block:

            @block.tensor
            def _(pe):
                for t in range(TT):
                    mm = pe.transpose(pt[:, 0, t * P:(t + 1) * P], h6[:, t * P:(t + 1) * P], ident[:, :])
                mm.then_inc(turned, 1)
                pe.wait_ge(to_pe, 1)
                for t in range(TT):
                    mm = pe.transpose(pt[:, 1, t * P:(t + 1) * P], norm6[:, t, :], ident[:, :])
                mm.then_inc(turned, 1)
                pe.wait_ge(to_pe, 2)
                pe.wait_ge(a_in, 16 * LOADS)
                for t in range(TT):
                    mm = pe.matmul(pt[:, 2 + t // 4, (t % 4 // 2) * 512 + (t % 2) * D:(t % 4 // 2) * 512 + (t % 2) * D + D],
                                   norm6t[:, t * P:(t + 1) * P], proj_w[:, :], start=True, stop=True)
                mm.then_inc(projected, 1)
                pe.wait_ge(to_pe, 3)
                turn(pe, pt, xhat, ident, turned)
                pe.wait_ge(to_pe, 4)
                for t in range(TT):
                    for n in range(2):
                        if t >= 2:
                            pe.wait_ge(qkv_copied[n], 2 * (t - 1))
                        for k in range(KD):
                            mm = pe.matmul(pt[:, 2 + t % 2, n * 512:n * 512 + 288], xhat_t[:, k, t * P:(t + 1) * P],
                                           qkv_w[:, k, n * 288:(n + 1) * 288], start=(k == 0), stop=(k == KD - 1))
                    mm.then_inc(qkv_ready, 1)

                def sums(job, at):
                    for n, rows in enumerate(job.batches):
                        if n == 0:
                            pe.wait_ge(multiplied, at.jobs + 1)
                        if n == len(job.batches) - 1:
                            pe.wait_ge(pool_multiplied, at.pooled + len(job.sum_pe_pool))
                        wide = job.places(rows)[1]
                        for k in range(job.terms):
                            mm = pe.matmul(pt[:, n, 0:wide], ident[:, :], sum_buffers[n][:, k * wide:(k + 1) * wide],
                                           start=(k == 0), stop=(k == job.terms - 1))
                        mm.then_inc(pe_summed, 1)

                sums(scoring, at_scoring)
                sums(valuing, at_valuing)
                sums(outer, at_outer)
                with pe.Fori(0, PINV_ITERS) as n:
                    sums(squaring, at_iteration(n))
                    sums(closing, at_iteration(n).after(squaring))
                sums(applying, at_applying)
                pe.wait_ge(out_lanes, 1)
                for i in range(SEQ):
                    at = i % (SEQ // 2) * P
                    mm = pe.transpose(pt[0:96, i // (SEQ // 2), at:at + P], attn[:, i, :], ident[:, :])
                mm.then_inc(turned, 1)
                pe.wait_ge(to_pe, 5)
                pe.wait_ge(heads_ready, 2)
                for t in range(TT):
                    for k in range(KD):
                        mm = pe.matmul(pt[:, 2 + t // 4, (t % 4 // 2) * 512 + (t % 2) * D:(t % 4 // 2) * 512 + (t % 2) * D + D],
                                       xhat_t[:, k, t * P:(t + 1) * P], out_w[:, k, :], start=(k == 0), stop=(k == KD - 1))
                mm.then_inc(projected, 1)

            @block.gpsimd
            def _(pool):
                pool.memset(eye[:, :, :], 0.0).then_inc(eye_ready, 1)
                pool.wait_ge(eye_ready, 1)
                pool.affine_select(out=eye[:, :, :], in_=eye[:, :, :], compare_op=ALU.not_equal, fill=1.0, base=0,
                                   pattern=[[1, R], [-1, R]], channel_multiplier=0).then_inc(eye_ready, 1)
                pool.memset(smat[:, :, 0, :], ROOT / LANDMARKS).then_inc(eye_ready, 1)
                pool.wait_ge(eye_ready, 3)
                pool.memset(smat[:, :, 0, 0], PADS / LANDMARKS).then_inc(eye_ready, 1)

                def multiply(job, at):
                    if at is not at_scoring:
                        pool.wait_ge(row_done, at.reduced)
                        pool.wait_ge(copied, at.copied)
                    for i in job.sum_pe_pool:
                        pool.tensor_tensor(job.by_term(sum_buffers, i), job.first(i), job.second(i),
                                           ALU.mult).then_inc(pool_multiplied, 1)
                    for i in job.by_pool:
                        pool.tensor_tensor(pooled_row(job, i), job.first(i), job.second(i), ALU.mult).then_inc(pool_multiplied, 1)

                for half in range(2):
                    pool.wait_ge(qkv_copied[half], 2 * TT)
                multiply(scoring, at_scoring)
                pool.wait_ge(peaks, 2)
                pool.partition_all_reduce(all_norms[:, :], norms[:, :], P, bass.bass_isa.ReduceOp.max).then_inc(peaks, 1)
                multiply(valuing, at_valuing)
                multiply(outer, at_outer)
                pool.wait_ge(e_ready, 1)
                with pool.Fori(0, PINV_ITERS) as n:
                    multiply(squaring, at_iteration(n))
                    pool.wait_ge(cubic_ready, n + 1)
                    multiply(closing, at_iteration(n).after(squaring))
                multiply(applying, at_applying)

            @block.scalar
            def _(act):
                act.activation(warm[:, :], ident[:, 0:1], ACT.Exp)
                for t in range(TT):
                    act.wait_ge(qkv_ready, t + 1)
                    for odd in range(2):
                        act.copy(*to_lanes(t, odd, 0)).then_inc(qkv_copied[0], 1)
                def copies(job, at):
                    def mirror(rows):
                        for i in rows:
                            if i in job.mirrors():
                                act.wait_ge(row_done, at.reduced + job.reduced.index(i) + 1)
                                act.copy(*job.mirror(i)).then_inc(copied, 1)

                    def batch(n, rows):
                        act.wait_ge(pe_summed, at.sums + n + 1)
                        for to, src in job.copies(pt[:, n, :], rows):
                            act.copy(to, src).then_inc(copied, 1)

                    mirror(job.by_vector[:2])
                    if len(job.batches) == 2:
                        batch(0, job.sum_pe)
                    mirror(job.by_vector[2:])
                    mirror(job.by_pool[:-3])
                    batch(len(job.batches) - 1, job.batches[-1])
                    mirror(job.by_pool[-3:])

                copies(scoring, at_scoring)
                act.wait_ge(scores_ready, 1)
                act.activation(scores[:, :, :, :], scores[:, :, :, :], ACT.Exp, scale=DH ** -0.5).then_inc(exp_done, 1)
                act.activation(epad[:, :, :], peak[:, :, :], ACT.Exp, scale=-(DH ** -0.5)).then_inc(exp_done, 1)
                copies(valuing, at_valuing)
                copies(outer, at_outer)
                act.wait_ge(e_ready, 1)
                with act.Fori(0, PINV_ITERS) as n:
                    act.wait_ge(row_done, at_iteration(n).reduced)
                    act.wait_ge(copied, at_iteration(n).copied)
                    act.activation(lined(e34), lined(e1), ACT.Copy, scale=0.75).then_inc(share_ready, 1)
                    copies(squaring, at_iteration(n))
                    copies(closing, at_iteration(n).after(squaring))
                copies(applying, at_applying)
                act.wait_ge(turned, 4)
                for half in range(2):
                    act.copy(*heads_turned(0, half)).then_inc(heads_ready, 1)

            @block.vector
            def _(dve):
                steps = Steps(dve, a_steps)
                tile = lambda x: [x[:, t, :] for t in range(TT)]
                small = (stats, mv, y6[:, :], t6[:, :], u6[:, :])
                dve.wait_ge(turned, 1)
                normalise(nc, steps, [pt[:, 0, t * P:(t + 1) * P] for t in range(TT)], tile(norm6), *small)
                nc.vector.tensor_copy(t6[:, :], y6[:, :]).then_inc(to_pe, 1)
                dve.wait_ge(turned, 2)
                nc.vector.tensor_scalar(norm6t[:, :], pt[:, 1, 0:TOK], lnp[:, 14:15], lnp[:, 15:16],
                                        ALU.mult, ALU.add).then_inc(to_pe, 1)
                dve.wait_ge(projected, 1)
                dve.wait_ge(a_in, 16 * LOADS)

                def projected_tiles():
                    for c in range(TT // 2):
                        bank = pt[:, 2 + c // 2, (c % 2) * 512:(c % 2) * 512 + 2 * D]
                        yield hidden[:, 2 * c:2 * c + 2, :], bank.rearrange("p (t n) -> p t n", t=2)

                for out, bank in projected_tiles():
                    steps.done(nc.vector.tensor_tensor(out, bank, proj_b[:, :].unsqueeze(1).broadcast_to([P, 2, D]), ALU.add))
                steps.settle()
                normalise(nc, steps, tile(hidden), tile(xhat), *small)
                nc.vector.tensor_copy(t6[:, :], y6[:, :]).then_inc(to_pe, 1)
                dve.wait_ge(turned, 3)
                nc.vector.tensor_copy(xhat_t[:, :, :].rearrange("p k (i b) -> p k b i", i=SEQ),
                                      pt[0:96, 0:2, 0:TOK].rearrange("p k (b i) -> p k b i", i=SEQ)).then_inc(to_pe, 1)
                steps.done(nc.vector.tensor_tensor(hidden[:, :, :], hidden[:, :, :], out_b[:, :].unsqueeze(1)
                                                   .broadcast_to([P, TT, D]), ALU.add))

                def sums(job, at):
                    for i in job.sum_pe:
                        ins = nc.vector.tensor_tensor(job.by_term(sum_buffers, i), job.first(i), job.second(i), ALU.mult)
                    ins.then_inc(multiplied, 1)
                    n = len(job.by_vector)
                    for m in range(n + 1):
                        if m < n:
                            i = job.by_vector[m]
                            if m >= 2:
                                dve.wait_ge(row_done, at.reduced + m - 1)
                            row = job.first(i), job.second(i)
                            products = rowt[:, m % 2, 0:job.width(i) * job.terms].rearrange(
                                "p (a b k) -> p a b k", a=row[0].shape[1], k=job.terms)
                            steps.done(nc.vector.tensor_tensor(products, *row, ALU.mult))
                            settled = steps.base + steps.n
                        if m >= 1:
                            dve.wait_ge(a_steps, settled - (m < n))
                            nc.vector.tensor_reduce(job.out(job.by_vector[m - 1]), ready, AX.X, ALU.add).then_inc(row_done, 1)
                        ready = products
                    for m, i in enumerate(job.by_pool):
                        dve.wait_ge(pool_multiplied, at.pooled + len(job.sum_pe_pool) + m + 1)
                        nc.vector.tensor_reduce(job.out(i), pooled_row(job, i), AX.X, ALU.add).then_inc(row_done, 1)
                    dve.wait_ge(row_done, at.reduced + len(job.reduced))
                    dve.wait_ge(copied, at.copied + job.copied())

                for t in range(TT):
                    dve.wait_ge(qkv_ready, t + 1)
                    for odd in range(2):
                        nc.vector.tensor_copy(*to_lanes(t, odd, 1)).then_inc(qkv_copied[1], 1)
                for half in range(2):
                    dve.wait_ge(qkv_copied[half], 2 * TT)
                sums(scoring, at_scoring)
                steps.done(nc.vector.tensor_reduce(peak[:, :, :], scores[:, :, :, :], AX.X, ALU.max))
                steps.settle()
                steps.done(nc.vector.tensor_scalar(peak[:, :, :], peak[:, :, :], 0.0, None, ALU.max))
                steps.settle()
                square = [P, HL, SEQ, SEQ]
                nc.vector.tensor_tensor(scores[:, :, :, :], scores[:, :, :, :], peak[:, :, :].unsqueeze(3).broadcast_to(square),
                                        ALU.subtract).then_inc(scores_ready, 1)
                dve.wait_ge(exp_done, 2)
                steps.done(nc.vector.tensor_reduce(den[:, :, :], scores[:, :, :, :], AX.X, ALU.add))
                steps.settle()
                flat = lambda x: x[:, :, :].rearrange("p h i -> p (h i)")
                steps.done(nc.vector.scalar_tensor_tensor(out=flat(den), in0=flat(epad), scalar=float(PADS), in1=flat(den),
                                                          op0=ALU.mult, op1=ALU.add))
                steps.settle()
                steps.done(nc.vector.reciprocal(flat(rden), flat(den)))
                steps.settle()
                dve.wait_ge(eye_ready, 4)
                real = smat[:, :, 1:R, 1:R]
                steps.done(nc.vector.tensor_tensor(real, scores[:, :, :, :], rden[:, :, :].unsqueeze(3).broadcast_to(square), ALU.mult))
                steps.done(nc.vector.scalar_tensor_tensor(out=smat[:, :, 1:R, 0], in0=epad[:, :, :], scalar=ROOT, in1=rden[:, :, :],
                                                          op0=ALU.mult, op1=ALU.mult))
                steps.settle()
                steps.done(nc.vector.tensor_reduce(den[:, :, :], real, AX.X, ALU.add))
                steps.done(nc.vector.tensor_reduce(peak[:, :, :], real.rearrange("p h i j -> p h j i"), AX.X, ALU.add))
                steps.done(nc.vector.tensor_reduce(padsum[:, :], smat[:, :, 1:R, 0], AX.X, ALU.add))
                steps.settle()
                steps.done(nc.vector.scalar_tensor_tensor(out=den[:, :, :], in0=smat[:, :, 1:R, 0], scalar=ROOT, in1=den[:, :, :],
                                                          op0=ALU.mult, op1=ALU.add))
                steps.done(nc.vector.tensor_scalar(padsum[:, :], padsum[:, :], 1.0 / ROOT, None, ALU.mult))
                steps.settle()
                steps.done(nc.vector.tensor_reduce(norms[:, 0:1], flat(den), AX.X, ALU.max))
                steps.done(nc.vector.tensor_reduce(norms[:, 1:2], flat(peak), AX.X, ALU.max))
                steps.done(nc.vector.tensor_reduce(scale[:, 0:1], padsum[:, :], AX.X, ALU.max))
                steps.settle()
                nc.vector.tensor_scalar(norms[:, 0:1], norms[:, 0:1], 1.0, None, ALU.max).then_inc(peaks, 1)
                nc.vector.tensor_scalar(norms[:, 1:2], norms[:, 1:2], scale[:, 0:1], PADS / LANDMARKS,
                                        ALU.max, ALU.add).then_inc(peaks, 1)
                sums(valuing, at_valuing)

                sums(outer, at_outer)
                dve.wait_ge(peaks, 3)
                steps.done(nc.vector.tensor_tensor(scale[:, 0:1], all_norms[:, 0:1], all_norms[:, 1:2], ALU.mult))
                steps.settle()
                steps.done(nc.vector.reciprocal(scale[:, 1:2], scale[:, 0:1]))
                steps.settle()
                steps.done(nc.vector.tensor_scalar(scale[:, 1:2], scale[:, 1:2], -1.0, None, ALU.mult))
                steps.settle()
                heads = lambda x: x[:, :, :, :].rearrange("p h i j -> p h (i j)")
                nc.vector.scalar_tensor_tensor(
                    out=heads(e1), in0=heads(e2), scalar=scale[:, 1:2],
                    in1=eye[:, :, :].rearrange("p i j -> p (i j)").unsqueeze(1).broadcast_to([P, HL, R * R]),
                    op0=ALU.mult, op1=ALU.add).then_inc(e_ready, 1)
                dve.wait_ge(e_ready, 1)
                start = steps.n
                each = len(squaring.by_vector) + len(closing.by_vector)
                with dve.Fori(0, PINV_ITERS) as n:
                    steps.at(start + each * n)
                    sums(squaring, at_iteration(n))
                    dve.wait_ge(share_ready, n + 1)
                    nc.vector.scalar_tensor_tensor(out=lined(c4), in0=lined(e2), scalar=0.25, in1=lined(e34),
                                                   op0=ALU.mult, op1=ALU.add).then_inc(cubic_ready, 1)
                    dve.wait_ge(cubic_ready, n + 1)
                    sums(closing, at_iteration(n).after(squaring))
                    assert steps.n == each
                steps.at(start + each * PINV_ITERS)
                sums(applying, at_applying)
                nc.vector.tensor_tensor(attn[:, :, :].rearrange("p i (h d) -> p i h d", d=DH),
                                        wv[:, :, 1:R, :].rearrange("p h i d -> p i h d"),
                                        attn[:, :, :].rearrange("p i (h d) -> p i h d", d=DH), ALU.subtract).then_inc(out_lanes, 1)
                dve.wait_ge(turned, 4)
                steps.done(nc.vector.tensor_copy(*heads_turned(1, 0)))
                nc.vector.tensor_copy(*heads_turned(1, 1)).then_inc(to_pe, 1)
                dve.wait_ge(projected, 2)
                for out, bank in projected_tiles():
                    steps.done(nc.vector.tensor_tensor(out, out, bank, ALU.add))
                steps.settle()


def experts(nc, io, res, top):
    sem = lambda n: top.enter_context(nc.semaphore(n))
    f_steps = sem("f_steps")
    f_pe = sem("f_pe")
    f_turned = sem("f_turned")
    routed = sem("routed")
    logits_ready = sem("logits_ready")
    f_exp = sem("f_exp")
    iota_ready = sem("iota_ready")
    hi_ready = sem("hi_ready")
    lo_ready = sem("lo_ready")
    up_ready = sem("up_ready")
    silu_done = sem("silu_done")
    act_ready = sem("act_ready")
    down_ready = sem("down_ready")
    summed = sem("summed")
    out_done = sem("out_done")
    N_HID = EXPERTS * HID + SHID
    MT = N_HID // P
    ROUTED_T = EXPERTS * HID // P
    ident, hidden = res["ident"], res["hidden"]
    gate_w, up_w, down_w, router_w, gate_b = (res[k] for k in ("gate_w", "up_w", "down_w", "router_w", "gate_b"))

    def parts_of(unit):
        if unit == 0:
            return [(ROUTED_T + i, 0, P) for i in range(SHID // P)]
        a, b = (unit - 1) * HID, unit * HID
        out = []
        while a < b:
            end = min(b, (a // P + 1) * P)
            out.append((a // P, a % P, a % P + end - a))
            a = end
        return out

    with ExitStack() as ctx:
        sb = lambda n, s, d=F32: ctx.enter_context(nc.sbuf_tensor(n, s, d))
        pf = ctx.enter_context(nc.psum_tensor("pf", [P, 4, 1024], F32))
        stats, mv = sb("f_stats", [P, TT, 6]), sb("f_mv", [P, TT, 2])
        y6, t6, u6 = sb("f_y6", [P, TT]), sb("f_t6", [P, TT]), sb("f_u6", [P, TT])
        xhat = sb("f_xhat", [P, TT, D])
        xhat_t = sb("f_xhat_t", [96, KD, TOK])
        x_hi, x_lo = sb("x_hi", [96, KD, TOK], F32R), sb("x_lo", [96, KD, TOK], F32R)
        SPLIT = 4
        w_hi, w_lo = (sb(n, [96, SPLIT, 2, KD, P], F32R) for n in ("w_hi", "w_lo"))
        whole = lambda m, g: (gate_w, up_w)[g][:, :, m * P:(m + 1) * P]
        NE = EXPERTS + 1
        logit, prob = sb("logit", [P, TT, NE]), sb("prob", [P, TT, NE])
        top = sb("top", [P, TT, 8])
        where = sb("where", [P, TT, 8], U32)
        wheref = sb("wheref", [P, TT, 8])
        iota_i, iota_f = sb("iota_i", [P, 8], I32), sb("iota_f", [P, 8])
        one, two = sb("one", [P, TT, 8]), sb("two", [P, TT, 8])
        peak, total = sb("f_peak", [P, TT]), sb("f_total", [P, TT])
        mix = sb("mix", [P, TT, NE])
        silu = sb("silu", [P, 2, TOK])
        acts = sb("acts", [P, MT, TOK])

        with nc.Block() as block:

            @block.sync
            def _(sp):
                for t in range(TT):
                    sp.wait_ge(summed, TT * EXPERTS + t + 1)
                    sp.dma_start(io["out"][t * P:(t + 1) * P, :], hidden[:, t, :]).then_inc(out_done, 16)
                sp.wait_ge(out_done, 16 * TT)

            @block.gpsimd
            def _(pool):
                pool.iota(iota_i[:, :], pattern=[[1, 8]], base=0, channel_multiplier=0).then_inc(iota_ready, 1)
                for m in range(MT):
                    if m >= SPLIT:
                        pool.wait_ge(up_ready, m - SPLIT + 1)
                    for g in range(2):
                        pool.wait_ge(hi_ready, 2 * m + g + 1)
                        pool.tensor_tensor(w_lo[:, m % SPLIT, g, :, :], whole(m, g), w_hi[:, m % SPLIT, g, :, :].bitcast(F32),
                                           ALU.subtract).then_inc(lo_ready, 1)

            @block.tensor
            def _(pe):
                pe.wait_ge(f_pe, 1)
                turn(pe, pf, xhat, ident, f_turned)
                pe.wait_ge(f_pe, 2)
                pe.wait_ge(res["f_in"], 16 * res["f_loads"])
                for t in range(TT):
                    for k in range(KD):
                        mm = pe.matmul(pf[:, 2, t * NE:(t + 1) * NE], xhat_t[:, k, t * P:(t + 1) * P], router_w[:, k, :],
                                       start=(k == 0), stop=(k == KD - 1))
                mm.then_inc(routed, 1)
                pe.wait_ge(f_pe, 4)
                for m in range(MT):
                    if m == 1:
                        pe.wait_ge(logits_ready, 1)
                    if m >= 2:
                        pe.wait_ge(act_ready, m - 1)
                    pe.wait_ge(lo_ready, 2 * (m + 1))
                    for g in range(2):
                        hi, lo = w_hi[:, m % SPLIT, g, :, :], w_lo[:, m % SPLIT, g, :, :]
                        for n in range(2):
                            products = [(w, x, k) for w, x in ((hi, x_hi), (hi, x_lo), (lo, x_hi)) for k in range(KD)]
                            for j, (w, x, k) in enumerate(products):
                                mm = pe.matmul(pf[:, 2 * (m % 2) + g, n * 512:n * 512 + TOK // 2], w[:, k, :],
                                               x[:, k, n * TOK // 2:(n + 1) * TOK // 2],
                                               start=(j == 0), stop=(j == len(products) - 1))
                    mm.then_inc(up_ready, 1)
                for unit in range(NE):
                    for t in range(TT):
                        n = unit * TT + t
                        if unit == 0:
                            pe.wait_ge(act_ready, MT)
                        if n >= 8:
                            pe.wait_ge(summed, n - 7)
                        rows = parts_of(unit)
                        for j, (tile, a, b) in enumerate(rows):
                            mm = pe.matmul(pf[:, n % 8 // 2, (n % 2) * 512:(n % 2) * 512 + D], acts[a:b, tile, t * P:(t + 1) * P],
                                           down_w[a:b, tile, :], start=(j == 0), stop=(j == len(rows) - 1))
                        mm.then_inc(down_ready, 1)

            @block.scalar
            def _(act):
                def rounded(m):
                    for g in range(2):
                        act.copy(w_hi[:, m % SPLIT, g, :, :], whole(m, g)).then_inc(hi_ready, 1)

                act.wait_ge(res["f_in"], 16 * res["f_loads"])
                for m in range(SPLIT - 1):
                    rounded(m)
                act.wait_ge(logits_ready, 1)
                act.activation(prob[:, :, :], logit[:, :, :], ACT.Exp).then_inc(f_exp, 1)
                for m in range(MT):
                    act.wait_ge(up_ready, m + 1)
                    if m >= 2:
                        act.wait_ge(act_ready, m - 1)
                    act.activation(silu[:, m % 2, :].rearrange("p (n c) -> p n c", n=2),
                                   pf[:, 2 * (m % 2), :].rearrange("p (n c) -> p n c", n=2)[:, :, 0:TOK // 2],
                                   ACT.Silu).then_inc(silu_done, 1)
                    if m + SPLIT - 1 < MT:
                        rounded(m + SPLIT - 1)

            @block.vector
            def _(dve):
                steps = Steps(dve, f_steps)
                tile = lambda x: [x[:, t, :] for t in range(TT)]
                normalise(nc, steps, tile(hidden), tile(xhat), stats, mv, y6[:, :], t6[:, :], u6[:, :])
                nc.vector.tensor_copy(t6[:, :], y6[:, :]).then_inc(f_pe, 1)
                dve.wait_ge(f_turned, 1)
                nc.vector.tensor_copy(xhat_t[:, :, :], pf[0:96, 0:2, 0:TOK]).then_inc(f_pe, 1)
                dve.wait_ge(f_pe, 2)
                nc.vector.tensor_copy(x_hi[:, :, :], xhat_t[:, :, :]).then_inc(f_pe, 1)
                dve.wait_ge(f_pe, 3)
                nc.vector.tensor_tensor(x_lo[:, :, :], xhat_t[:, :, :], x_hi[:, :, :].bitcast(F32), ALU.subtract).then_inc(f_pe, 1)
                dve.wait_ge(res["f_in"], 16 * res["f_loads"])
                dve.wait_ge(routed, 1)
                raw = pf[:, 2, 0:TT * NE].rearrange("p (t e) -> p t e", t=TT)
                over = lambda x, n=8: x.unsqueeze(2).broadcast_to([P, TT, n])
                steps.done(nc.vector.tensor_reduce(peak[:, :], raw[:, :, 0:EXPERTS], AX.X, ALU.max))
                steps.settle()
                steps.done(nc.vector.tensor_tensor(logit[:, :, 0:EXPERTS], raw[:, :, 0:EXPERTS], over(peak[:, :]), ALU.subtract))
                nc.vector.tensor_scalar(logit[:, :, EXPERTS], raw[:, :, EXPERTS], gate_b[:, 0:1], -1.0, ALU.add, ALU.mult)\
                    .then_inc(logits_ready, 1)
                dve.wait_ge(f_exp, 1)
                steps.done(nc.vector.tensor_reduce(total[:, :], prob[:, :, 0:EXPERTS], AX.X, ALU.add))
                steps.done(nc.vector.tensor_scalar(peak[:, :], prob[:, :, EXPERTS], 1.0, None, ALU.add))
                steps.settle()
                steps.done(nc.vector.reciprocal(total[:, :], total[:, :]))
                steps.done(nc.vector.reciprocal(mix[:, :, 0], peak[:, :]))
                steps.settle()
                steps.done(nc.vector.tensor_tensor(prob[:, :, 0:EXPERTS], prob[:, :, 0:EXPERTS], over(total[:, :]), ALU.mult))
                steps.settle()
                for t in range(TT):
                    steps.done(nc.vector.max(top[:, t, :], prob[:, t, 0:EXPERTS]))
                steps.settle()
                for t in range(TT):
                    steps.done(nc.vector.max_index(where[:, t, :], top[:, t, :], prob[:, t, 0:EXPERTS]))
                steps.done(nc.vector.tensor_tensor(total[:, :], top[:, :, 0], top[:, :, 1], ALU.add))
                dve.wait_ge(iota_ready, 1)
                steps.done(nc.vector.tensor_copy(iota_f[:, :], iota_i[:, :]))
                steps.settle()
                steps.done(nc.vector.tensor_copy(wheref[:, :, :], where[:, :, :]))
                steps.done(nc.vector.reciprocal(peak[:, :], total[:, :]))
                steps.settle()
                steps.done(nc.vector.tensor_tensor(top[:, :, :], top[:, :, :], over(peak[:, :]), ALU.mult))
                each = iota_f[:, :].unsqueeze(1).broadcast_to([P, TT, 8])
                steps.done(nc.vector.tensor_tensor(one[:, :, :], each, over(wheref[:, :, 0]), ALU.is_equal))
                steps.done(nc.vector.tensor_tensor(two[:, :, :], each, over(wheref[:, :, 1]), ALU.is_equal))
                steps.done(nc.vector.tensor_scalar(total[:, :], mix[:, :, 0], -1.0, 1.0, ALU.mult, ALU.add))
                steps.settle()
                steps.done(nc.vector.tensor_tensor(one[:, :, :], one[:, :, :], over(top[:, :, 0]), ALU.mult))
                steps.done(nc.vector.tensor_tensor(two[:, :, :], two[:, :, :], over(top[:, :, 1]), ALU.mult))
                steps.settle()
                steps.done(nc.vector.tensor_tensor(one[:, :, :], one[:, :, :], two[:, :, :], ALU.add))
                steps.settle()
                steps.done(nc.vector.tensor_tensor(mix[:, :, 1:NE], one[:, :, :], over(total[:, :]), ALU.mult))
                for m in range(MT):
                    dve.wait_ge(silu_done, m + 1)
                    two_halves = lambda x: x.rearrange("p (n c) -> p n c", n=2)
                    nc.vector.tensor_tensor(two_halves(acts[:, m, :]), two_halves(silu[:, m % 2, :]),
                                            two_halves(pf[:, 2 * (m % 2) + 1, :])[:, :, 0:TOK // 2], ALU.mult).then_inc(act_ready, 1)
                steps.settle()
                for unit in range(NE):
                    for t in range(TT):
                        n = unit * TT + t
                        dve.wait_ge(down_ready, n + 1)
                        if unit:
                            dve.wait_ge(summed, n - TT + 1)
                        nc.vector.scalar_tensor_tensor(out=hidden[:, t, :], in0=pf[:, n % 8 // 2, (n % 2) * 512:(n % 2) * 512 + D],
                                                       scalar=mix[:, t, unit:unit + 1], in1=hidden[:, t, :],
                                                       op0=ALU.mult, op1=ALU.add).then_inc(summed, 1)


def shared_tensors(nc, ctx):
    sb = lambda n, s, d=F32: ctx.enter_context(nc.sbuf_tensor(n, s, d))
    return {"ident": sb("ident", [P, P]), "h6": sb("h6", [P, TOK]), "lnp": sb("lnp", [P, 16]),
            "proj_w": sb("proj_w", [CH, D]), "qkv_w": sb("qkv_w", [96, KD, 3 * D]),
            "out_w": sb("out_w", [96, KD, D]),
            "attention_in": ctx.enter_context(nc.semaphore("attention_in"))}


def attention_weights(sp, io, res):
    halves = lambda x: x.rearrange("(k p) n -> p k n", k=KD)
    sp.dma_start(res["proj_w"][:, :], io["proj_w"]).then_inc(res["attention_in"], 16)
    sp.dma_start(res["qkv_w"][:, :, :], halves(io["qkv_w"])).then_inc(res["attention_in"], 16)
    sp.dma_start(res["out_w"][:, :, :], halves(io["out_w"])).then_inc(res["attention_in"], 16)


def expert_weights(nc, io, res, ctx):
    sb = lambda n, s, d=F32: ctx.enter_context(nc.sbuf_tensor(n, s, d))
    N = EXPERTS * HID + SHID
    res.update(hidden=sb("hidden", [P, TT, D]), proj_b=sb("proj_b", [P, D]), out_b=sb("out_b", [P, D]),
               gate_w=sb("gate_w", [96, KD, N]), up_w=sb("up_w", [96, KD, N]), down_w=sb("down_w", [P, N // P, D]),
               router_w=sb("router_w", [96, KD, EXPERTS + 1]), gate_b=sb("gate_b", [P, 1]),
               f_in=ctx.enter_context(nc.semaphore("experts_in")), f_loads=5)
    with nc.Block() as block:

        @block.sync
        def _(sp):
            halves = lambda x: x.rearrange("(k p) n -> p k n", k=KD)
            for bias in ("proj_b", "out_b"):
                sp.dma_start(res[bias][:, :], io[bias].partition_broadcast(P)).then_inc(res["attention_in"], 16)
            sp.dma_start(res["gate_w"][:, :, :], halves(io["gate_w"])).then_inc(res["f_in"], 16)
            sp.dma_start(res["up_w"][:, :, :], halves(io["up_w"])).then_inc(res["f_in"], 16)
            sp.dma_start(res["router_w"][:, :, :], halves(io["router_w"])).then_inc(res["f_in"], 16)
            sp.dma_start(res["gate_b"][:, :], io["gate_b"].partition_broadcast(P)).then_inc(res["f_in"], 16)
            sp.dma_start(res["down_w"][:, :, :], io["down_w"].rearrange("(t p) n -> p t n", p=P)).then_inc(res["f_in"], 16)


def audio_tower(nc, io):
    with ExitStack() as top:
        res = shared_tensors(nc, top)
        conv_tower(nc, io, res, top)
        expert_weights(nc, io, res, top)
        attention(nc, io, res, top)
        experts(nc, io, res, top)


def kernel(**a):
    import concourse.bacc as bacc
    from concourse.bass_utils import run_bass_kernel_spmd

    g = {k: np.asarray(v) for k, v in a.items()}
    conv = [g[f"L0_tok_conv_w{i}"] for i in range(7)]
    names = [(f"L0_tok_ln_g{i}", f"L0_tok_ln_b{i}") for i in range(7)] + [("L0_tok_fln_g", "L0_tok_fln_b")]
    by_hidden = lambda x: x.transpose(1, 0, 2).reshape(D, EXPERTS * HID)
    arrays = {
        "x": np.pad(g["x"], ((0, 0), (0, STRIDE0))),
        "w0": conv[0][:, 0, :],
        "w": np.concatenate([c.transpose(1, 2, 0) for c in conv[1:]], 1),
        "lnp": np.stack([g[n] for pair in names for n in pair], 1),
        "proj_w": g["L0_tok_proj_w"],
        "proj_b": g["L0_tok_proj_b"],
        "qkv_w": g["L0_attn_w_qkv"].T.reshape(D, 3, 2, D // 2).transpose(0, 2, 1, 3).reshape(D, 3 * D),
        "out_w": g["L0_attn_w_proj"].T,
        "out_b": g["L0_attn_b_proj"],
        "router_w": np.concatenate([g["L0_ffn_router_w"], g["L0_ffn_sg_w"]], 1),
        "gate_b": g["L0_ffn_sg_b"],
        "gate_w": np.concatenate([by_hidden(g["L0_ffn_w_gate"]), g["L0_ffn_ws_gate"]], 1),
        "up_w": np.concatenate([by_hidden(g["L0_ffn_w_up"]), g["L0_ffn_ws_up"]], 1),
        "down_w": np.concatenate([g["L0_ffn_w_down"].reshape(EXPERTS * HID, D), g["L0_ffn_ws_down"]], 0),
    }
    nc = bacc.Bacc("TRN2", target_bir_lowering=False, num_devices=1)
    io, sent = {}, {}
    for name, x in arrays.items():
        x = np.ascontiguousarray(x)
        sent[f"in_{name}"] = x
        io[name] = nc.dram_tensor(f"in_{name}", x.shape, mybir.dt.from_np(x.dtype), kind="ExternalInput").ap()
    io["out"] = nc.dram_tensor("out_tokens", (TOK, D), F32, kind="ExternalOutput").ap()
    audio_tower(nc, io)
    r = run_bass_kernel_spmd(nc, [sent], core_ids=[0])
    return r.results[0]["out_tokens"].reshape(BATCH, SEQ, D)
```
